# Optimizing a Trainium2 kernel written in Bass

```python
import numpy as np
import jax
import jax.numpy as jnp

def _softmax(x, axis=-1):
    return jax.nn.softmax(x, axis=axis)

def _gelu(x):
    return jax.nn.gelu(x, approximate=True)

def _silu(x):
    return jax.nn.silu(x)

def _sigmoid(x):
    return jax.nn.sigmoid(x)

def _layernorm(x, axis=-1, eps=1e-05):
    m = jnp.mean(x, axis=axis, keepdims=True)
    v = jnp.var(x, axis=axis, keepdims=True)
    return (x - m) / jnp.sqrt(v + eps)

def _scatter_add(tgt, idx, src, axis=0):
    return tgt.at[idx].add(src)

def _segment_sum(src, seg, n):
    return jax.ops.segment_sum(src, seg, n)
kernel_name = 'mk_macaron_d1_jaxref_r2_547caf'

def setup_inputs(seed: int=0):
    np.random.seed(seed)
    _w = jnp.asarray

    def _L0_attn_setup():
        import jax, jax.numpy as jnp
        import numpy as np
        from jax import lax
        D_MODEL = 512
        N_HEADS = 16
        HEAD_DIM = D_MODEL // N_HEADS
        B, S = (4, 1024)
        EPS = 1e-05

        def _l2_normalize(v, eps=1e-12):
            v32 = v.astype(jnp.float32)
            n = jnp.sqrt(jnp.sum(v32 * v32, axis=-1, keepdims=True))
            return (v32 / jnp.maximum(n, eps)).astype(v.dtype)

        def _rmsnorm(x, w):
            x32 = x.astype(jnp.float32)
            rms = lax.rsqrt(jnp.mean(x32 * x32, axis=-1, keepdims=True) + EPS)
            return (x32 * rms).astype(x.dtype) * w
        if __name__ == '__main__':
            out = reference(**setup_inputs())
            print(out.shape)
        key = jax.random.key(seed)
        ks = jax.random.split(key, 8)
        sc = 1.0 / np.sqrt(D_MODEL)
        return {'x': jax.random.normal(ks[0], (B, S, D_MODEL), dtype=jnp.float32), 'Wq': jax.random.normal(ks[1], (D_MODEL, D_MODEL), dtype=jnp.float32) * sc, 'Wk': jax.random.normal(ks[2], (D_MODEL, D_MODEL), dtype=jnp.float32) * sc, 'Wv': jax.random.normal(ks[3], (D_MODEL, D_MODEL), dtype=jnp.float32) * sc, 'Wa': jax.random.normal(ks[4], (D_MODEL, N_HEADS), dtype=jnp.float32) * sc, 'ba': jnp.zeros((N_HEADS,), dtype=jnp.float32), 'Wb': jax.random.normal(ks[5], (D_MODEL, N_HEADS), dtype=jnp.float32) * sc, 'bb': jnp.zeros((N_HEADS,), dtype=jnp.float32), 'Wg': jax.random.normal(ks[6], (D_MODEL, D_MODEL), dtype=jnp.float32) * sc, 'Wo': jax.random.normal(ks[7], (D_MODEL, D_MODEL), dtype=jnp.float32) * sc, 'g_norm': jnp.ones((D_MODEL,), dtype=jnp.float32)}
    _L0_attn_in = _L0_attn_setup()

    def _L0_ffn_setup():
        import jax, jax.numpy as jnp
        import numpy as np
        D_MODEL = 512
        NUM_SLOTS = 64
        TOP_K = 8
        B, T = (4, 2048)

        def _forward(x, slot_init, slot_scale, w1, b1, w2, b2, gru_wih, gru_whh, gru_bih, gru_bhh, wv, bv, wo, bo, tau):
            Bn, Tn, D = x.shape
            Sn = slot_init.shape[0]
            S = jnp.broadcast_to((slot_init * slot_scale)[None], (Bn, Sn, D)).astype(x.dtype)
            slot_mean = S.mean(axis=1, keepdims=True)
            ctx = jnp.concatenate([x, jnp.broadcast_to(slot_mean, x.shape)], axis=-1)
            h = jax.nn.gelu(ctx @ w1.T + b1, approximate=False)
            route_logits = (h @ w2.T + b2) / (jnp.abs(tau) + 0.1)
            topk_vals, topk_idx = jax.lax.top_k(route_logits, TOP_K)
            topk_w = jax.nn.softmax(topk_vals, axis=-1)
            alpha = jnp.sum(topk_w[..., None] * jax.nn.one_hot(topk_idx, Sn, dtype=x.dtype), axis=-2)
            slot_input = jnp.einsum('bts,btd->bsd', alpha, x)
            slot_wsum = alpha.sum(axis=1) + 1e-08
            gi = (slot_input / slot_wsum[..., None]).reshape(Bn * Sn, D)
            hs = S.reshape(Bn * Sn, D)
            gx = gi @ gru_wih.T + gru_bih
            gh = hs @ gru_whh.T + gru_bhh
            xr, xz, xn = jnp.split(gx, 3, axis=-1)
            hr, hz, hn = jnp.split(gh, 3, axis=-1)
            r = jax.nn.sigmoid(xr + hr)
            z = jax.nn.sigmoid(xz + hz)
            n = jnp.tanh(xn + r * hn)
            h_new = (1.0 - z) * n + z * hs
            S_new = h_new.reshape(Bn, Sn, D)
            slot_values = S_new @ wv.T + bv
            out = jnp.einsum('bts,bsd->btd', alpha, slot_values)
            return out @ wo.T + bo
        key = jax.random.key(seed)
        ks = jax.random.split(key, 16)
        D, S = (D_MODEL, NUM_SLOTS)
        H = D // 2
        sc = lambda fan_in: 1.0 / np.sqrt(fan_in)
        inp = {'x': jax.random.normal(ks[0], (B, T, D), dtype=jnp.float32), 'slot_init': jax.random.normal(ks[1], (S, D), dtype=jnp.float32) * 0.1, 'slot_scale': jnp.ones((S, 1), dtype=jnp.float32), 'w1': jax.random.normal(ks[2], (H, 2 * D), dtype=jnp.float32) * sc(2 * D), 'b1': jnp.zeros((H,), dtype=jnp.float32), 'w2': jax.random.normal(ks[3], (S, H), dtype=jnp.float32) * sc(H), 'b2': jnp.zeros((S,), dtype=jnp.float32), 'gru_wih': jax.random.normal(ks[4], (3 * D, D), dtype=jnp.float32) * sc(D), 'gru_whh': jax.random.normal(ks[5], (3 * D, D), dtype=jnp.float32) * sc(D), 'gru_bih': jnp.zeros((3 * D,), dtype=jnp.float32), 'gru_bhh': jnp.zeros((3 * D,), dtype=jnp.float32), 'wv': jax.random.normal(ks[6], (D, D), dtype=jnp.float32) * sc(D), 'bv': jnp.zeros((D,), dtype=jnp.float32), 'wo': jax.random.normal(ks[7], (D, D), dtype=jnp.float32) * sc(D), 'bo': jnp.zeros((D,), dtype=jnp.float32), 'tau': jnp.ones((1,), dtype=jnp.float32)}
        return inp
    _L0_ffn_in = _L0_ffn_setup()
    _d = {'L0_attn_x': _L0_attn_in['x'], 'L0_attn_Wq': _L0_attn_in['Wq'], 'L0_attn_Wk': _L0_attn_in['Wk'], 'L0_attn_Wv': _L0_attn_in['Wv'], 'L0_attn_Wa': _L0_attn_in['Wa'], 'L0_attn_ba': _L0_attn_in['ba'], 'L0_attn_Wb': _L0_attn_in['Wb'], 'L0_attn_bb': _L0_attn_in['bb'], 'L0_attn_Wg': _L0_attn_in['Wg'], 'L0_attn_Wo': _L0_attn_in['Wo'], 'L0_attn_g_norm': _L0_attn_in['g_norm'], 'L0_ffn_slot_init': _L0_ffn_in['slot_init'], 'L0_ffn_slot_scale': _L0_ffn_in['slot_scale'], 'L0_ffn_w1': _L0_ffn_in['w1'], 'L0_ffn_b1': _L0_ffn_in['b1'], 'L0_ffn_w2': _L0_ffn_in['w2'], 'L0_ffn_b2': _L0_ffn_in['b2'], 'L0_ffn_gru_wih': _L0_ffn_in['gru_wih'], 'L0_ffn_gru_whh': _L0_ffn_in['gru_whh'], 'L0_ffn_gru_bih': _L0_ffn_in['gru_bih'], 'L0_ffn_gru_bhh': _L0_ffn_in['gru_bhh'], 'L0_ffn_wv': _L0_ffn_in['wv'], 'L0_ffn_bv': _L0_ffn_in['bv'], 'L0_ffn_wo': _L0_ffn_in['wo'], 'L0_ffn_bo': _L0_ffn_in['bo'], 'L0_ffn_tau': _L0_ffn_in['tau']}
    _x0 = _d['L0_attn_x']
    _d['L0_attn_x'] = jax.random.normal(jax.random.fold_in(jax.random.key(seed), 1), (2, 4096, 512), dtype=_x0.dtype)
    del _x0
    return _d

def reference(L0_attn_x, L0_attn_Wq, L0_attn_Wk, L0_attn_Wv, L0_attn_Wa, L0_attn_ba, L0_attn_Wb, L0_attn_bb, L0_attn_Wg, L0_attn_Wo, L0_attn_g_norm, L0_ffn_slot_init, L0_ffn_slot_scale, L0_ffn_w1, L0_ffn_b1, L0_ffn_w2, L0_ffn_b2, L0_ffn_gru_wih, L0_ffn_gru_whh, L0_ffn_gru_bih, L0_ffn_gru_bhh, L0_ffn_wv, L0_ffn_bv, L0_ffn_wo, L0_ffn_bo, L0_ffn_tau):

    def _L0_attn_ref(x, Wq, Wk, Wv, Wa, ba, Wb, bb, Wg, Wo, g_norm):
        import jax, jax.numpy as jnp
        import numpy as np
        from jax import lax
        D_MODEL = 512
        N_HEADS = 16
        HEAD_DIM = D_MODEL // N_HEADS
        B, S = (4, 1024)
        EPS = 1e-05

        def _l2_normalize(v, eps=1e-12):
            v32 = v.astype(jnp.float32)
            n = jnp.sqrt(jnp.sum(v32 * v32, axis=-1, keepdims=True))
            return (v32 / jnp.maximum(n, eps)).astype(v.dtype)

        def _rmsnorm(x, w):
            x32 = x.astype(jnp.float32)
            rms = lax.rsqrt(jnp.mean(x32 * x32, axis=-1, keepdims=True) + EPS)
            return (x32 * rms).astype(x.dtype) * w
        if __name__ == '__main__':
            out = reference(**setup_inputs())
            print(out.shape)
        batch, seq_len, d_model = x.shape
        H, hd = (N_HEADS, HEAD_DIM)
        residual_input = x
        q = (x @ Wq).reshape(batch, seq_len, H, hd)
        k = (x @ Wk).reshape(batch, seq_len, H, hd)
        v = (x @ Wv).reshape(batch, seq_len, H, hd)
        q = _l2_normalize(q)
        k = _l2_normalize(k)
        alpha = jax.nn.sigmoid(x @ Wa + ba)
        beta = jax.nn.sigmoid(x @ Wb + bb)
        qt = jnp.moveaxis(q, 1, 0)
        kt = jnp.moveaxis(k, 1, 0)
        vt = jnp.moveaxis(v, 1, 0)
        at = jnp.moveaxis(alpha, 1, 0)
        bt = jnp.moveaxis(beta, 1, 0)
        state0 = jnp.zeros((batch, H, hd, hd), dtype=x.dtype)

        def step(state, inp):
            q_t, k_t, v_t, a_t, b_t = inp
            pred = jnp.einsum('bhde,bhd->bhe', state, k_t)
            error = v_t - pred
            update = jnp.einsum('bhe,bhd->bhde', b_t[..., None] * error, k_t)
            state = a_t[..., None, None] * state + update
            out = jnp.einsum('bhde,bhd->bhe', state, q_t)
            return (state, out)
        _, ys = lax.scan(step, state0, (qt, kt, vt, at, bt))
        y = jnp.moveaxis(ys, 0, 1).reshape(batch, seq_len, d_model)
        gate = jax.nn.silu(residual_input @ Wg)
        y = _rmsnorm(y, g_norm) * gate
        return y @ Wo

    def _L0_ffn_ref(x, slot_init, slot_scale, w1, b1, w2, b2, gru_wih, gru_whh, gru_bih, gru_bhh, wv, bv, wo, bo, tau):
        import jax, jax.numpy as jnp
        import numpy as np
        D_MODEL = 512
        NUM_SLOTS = 64
        TOP_K = 8
        B, T = (4, 2048)

        def _forward(x, slot_init, slot_scale, w1, b1, w2, b2, gru_wih, gru_whh, gru_bih, gru_bhh, wv, bv, wo, bo, tau):
            Bn, Tn, D = x.shape
            Sn = slot_init.shape[0]
            S = jnp.broadcast_to((slot_init * slot_scale)[None], (Bn, Sn, D)).astype(x.dtype)
            slot_mean = S.mean(axis=1, keepdims=True)
            ctx = jnp.concatenate([x, jnp.broadcast_to(slot_mean, x.shape)], axis=-1)
            h = jax.nn.gelu(ctx @ w1.T + b1, approximate=False)
            route_logits = (h @ w2.T + b2) / (jnp.abs(tau) + 0.1)
            topk_vals, topk_idx = jax.lax.top_k(route_logits, TOP_K)
            topk_w = jax.nn.softmax(topk_vals, axis=-1)
            alpha = jnp.sum(topk_w[..., None] * jax.nn.one_hot(topk_idx, Sn, dtype=x.dtype), axis=-2)
            slot_input = jnp.einsum('bts,btd->bsd', alpha, x)
            slot_wsum = alpha.sum(axis=1) + 1e-08
            gi = (slot_input / slot_wsum[..., None]).reshape(Bn * Sn, D)
            hs = S.reshape(Bn * Sn, D)
            gx = gi @ gru_wih.T + gru_bih
            gh = hs @ gru_whh.T + gru_bhh
            xr, xz, xn = jnp.split(gx, 3, axis=-1)
            hr, hz, hn = jnp.split(gh, 3, axis=-1)
            r = jax.nn.sigmoid(xr + hr)
            z = jax.nn.sigmoid(xz + hz)
            n = jnp.tanh(xn + r * hn)
            h_new = (1.0 - z) * n + z * hs
            S_new = h_new.reshape(Bn, Sn, D)
            slot_values = S_new @ wv.T + bv
            out = jnp.einsum('bts,bsd->btd', alpha, slot_values)
            return out @ wo.T + bo
        return _forward(x, slot_init, slot_scale, w1, b1, w2, b2, gru_wih, gru_whh, gru_bih, gru_bhh, wv, bv, wo, bo, tau)
    x = L0_attn_x
    x = x + 0.5 * _L0_ffn_ref(_layernorm(x, axis=-1), L0_ffn_slot_init, L0_ffn_slot_scale, L0_ffn_w1, L0_ffn_b1, L0_ffn_w2, L0_ffn_b2, L0_ffn_gru_wih, L0_ffn_gru_whh, L0_ffn_gru_bih, L0_ffn_gru_bhh, L0_ffn_wv, L0_ffn_bv, L0_ffn_wo, L0_ffn_bo, L0_ffn_tau)
    x = x + _L0_attn_ref(_layernorm(x, axis=-1), L0_attn_Wq, L0_attn_Wk, L0_attn_Wv, L0_attn_Wa, L0_attn_ba, L0_attn_Wb, L0_attn_bb, L0_attn_Wg, L0_attn_Wo, L0_attn_g_norm)
    x = x + 0.5 * _L0_ffn_ref(_layernorm(x, axis=-1), L0_ffn_slot_init, L0_ffn_slot_scale, L0_ffn_w1, L0_ffn_b1, L0_ffn_w2, L0_ffn_b2, L0_ffn_gru_wih, L0_ffn_gru_whh, L0_ffn_gru_bih, L0_ffn_gru_bhh, L0_ffn_wv, L0_ffn_bv, L0_ffn_wo, L0_ffn_bo, L0_ffn_tau)
    return x

_drawn_inputs = setup_inputs


def setup_inputs(seed=0):
    import zlib

    import numpy as np

    out = dict(_drawn_inputs(seed))
    spreads = {'L0_attn_ba': (0.0, 0.526),
     'L0_attn_bb': (0.0, 0.284),
     'L0_attn_g_norm': (1.0, 0.2),
     'L0_ffn_slot_scale': (1.0, 0.6),
     'L0_ffn_b1': (0.0, 0.8),
     'L0_ffn_b2': (0.0, 0.737),
     'L0_ffn_gru_bih': (0.0, 0.1),
     'L0_ffn_gru_bhh': (0.0, 0.315),
     'L0_ffn_bv': (0.0, 0.1),
     'L0_ffn_bo': (0.0, 0.1)}
    factors = {'L0_ffn_slot_init': 2.82,
     'L0_ffn_w1': 2.7,
     'L0_ffn_gru_wih': 2.823,
     'L0_ffn_gru_whh': 6.234}
    for name, (base, spread) in spreads.items():
        noise = np.random.default_rng([zlib.crc32(name.encode()), seed]).standard_normal(out[name].shape)
        drawn = base * np.exp(spread * noise) if base else spread * noise
        out[name] = jnp.asarray(drawn.astype(out[name].dtype))
    for name, factor in factors.items():
        out[name] = (out[name] * factor).astype(out[name].dtype)
    return out
```

```python
import numpy as np
import concourse.bass as bass
from concourse import mybir
from concourse.alu_op_type import AluOpType as ALU
from contextlib import ExitStack

f32 = mybir.dt.float32
i32 = mybir.dt.int32
ACT = mybir.ActivationFunctionType
AX = mybir.AxisListType

B, T, D = 2, 4096, 512
H, HD = 16, 32
NS, HID = 64, 256
P = 128
KC = D // P
NT = T // P
CH = 32
NC = P // CH
LEVELS = 4
BIG = -3.0e38


def build(nc, x, Wq, Wk, Wv, Wa, ba, Wb, bb, Wg, Wo, g_norm, slot_init, slot_scale, w1, b1, w2, b2,
          wih, whh, bih, bhh, wv, bv, wo, bo, tau, out):
    ctx = ExitStack()
    with ctx:
        def sb(name, cols, dt=f32):
            return ctx.enter_context(nc.sbuf_tensor(name, [P, cols], dt))

        def sem(name):
            return ctx.enter_context(nc.semaphore(name))

        def sem2(name):
            return [sem(f"{name}{b}") for b in range(B)]

        x2_dram = nc.dram_tensor("x2_scratch", (B, NT, P, D), f32, kind="Internal").ap()
        at_dram = [nc.dram_tensor(f"alphaT_scratch{m}", (NT, P, P), f32, kind="Internal").ap() for m in range(2)]
        x_t = x.rearrange("b (n p) d -> b n p d", p=P)
        out_t = out.rearrange("b (n p) d -> b n p d", p=P)

        w_kvqg = sb("w_kvqg", KC * 4 * D)
        w_ab = sb("w_ab", KC * 2 * H)
        w_out = sb("w_out", KC * D)
        w1T = sb("w1T", KC * HID)
        w2T = sb("w2T", 2 * NS)
        wihT = sb("wihT", KC * 3 * D)
        voT = sb("voT", KC * D)
        gh = sb("gh", 3 * D)
        bih_n = sb("bih_n", D)
        bvo = sb("bvo", D)
        hs = sb("hs", D)
        ident = sb("ident", P)
        ones = sb("ones", P)
        before = sb("before", P)
        upto = sb("upto", P)
        after = sb("after", P)
        chunk = sb("chunk", P)
        levmask = sb("levmask", (LEVELS + 1) * CH)
        tri = sb("tri", CH)
        eye32 = sb("eye32", CH)
        half = sb("half", H)
        ab_bias = sb("ab_bias", 2 * H)
        b2s = sb("b2s", NS)
        itau = sb("itau", 1)
        h_bias = sb("h_bias", 2)
        gcol = sb("gcol", KC)
        sv = sb("sv", D)
        alpha = sb("alpha", B * NS)
        aT_in = sb("aT_in", P)
        aT_out = sb("aT_out", P)
        slotacc = [sb(f"slotacc{b}", KC * NS + NS) for b in range(B)]

        xin = [sb(f"xin{b}", D) for b in range(B)]
        xc = [sb(f"xc{b}", D) for b in range(B)]
        xn = [sb(f"xn{b}", D) for b in range(B)]
        xnT = [sb(f"xnT{b}", D) for b in range(B)]
        kn = [sb(f"kn{b}", D) for b in range(B)]
        qs = [sb(f"qs{b}", D) for b in range(B)]
        scr = [sb(f"scr{b}", D) for b in range(B)]
        vk = [sb(f"vk{b}", 2 * D) for b in range(B)]
        gate = [sb(f"gate{b}", D) for b in range(B)]
        dr = [sb(f"dr{b}", D) for b in range(B)]
        uw = [sb(f"uw{b}", 2 * D + H) for b in range(B)]
        kqT = [sb(f"kqT{b}", 2 * D) for b in range(B)]
        qa = [sb(f"qa{b}", 2 * D) for b in range(B)]
        npk = [sb(f"npk{b}", 3 * D) for b in range(B)]
        no = [sb(f"no{b}", 2 * D) for b in range(B)]
        yy = [sb(f"yy{b}", D) for b in range(B)]
        xx = [sb(f"xx{b}", D) for b in range(B)]
        sm = [sb(f"sm{b}", 512) for b in range(B)]

        def heads(t, n=1):
            return t[:, 0:n * D].rearrange("p (h e) -> p h e", h=H)

        def bc(col):
            return col.unsqueeze(2).to_broadcast([P, H, HD])

        def allheads(mask):
            return mask.unsqueeze(1).to_broadcast([P, H, HD])

        SMALL = {}
        at = 0
        for name, n in [("stats", 6), ("mv", 2), ("vs", 1), ("rstd", 1), ("ssk", H), ("rk", H), ("ssq", H),
                        ("rq", H), ("ab", 2 * H), ("zi", 2 * H), ("ez", 2 * H), ("ln", H), ("la", H), ("opb", H),
                        ("be", H), ("e4", 4 * H), ("bel", H), ("ys", 1), ("yv", 1), ("yr", 1),
                        ("top", 8), ("negm", 1), ("den", 1), ("rden", 1)]:
            SMALL[name] = (at, n)
            at += n
        lgt = [sb(f"lgt{b}", 3 * NS) for b in range(B)]

        def s(b, name):
            o, n = SMALL[name]
            return sm[b][:, o:o + n]

        D33 = [uw[b][:, 0:H * (HD + 1)].rearrange("p (h e) -> p h e", h=H) for b in range(B)]
        hT = [kqT[b][:, 0:2 * P] for b in range(B)]

        AB = [ctx.enter_context(nc.psum_tensor(f"AB{b}", [P, 1024], f32)) for b in range(B)]
        C = [ctx.enter_context(nc.psum_tensor(f"C{b}", [P, 512], f32)) for b in range(B)]
        ST = [ctx.enter_context(nc.psum_tensor(f"ST{b}", [P, 512], f32)) for b in range(B)]
        A = [AB[b][:, 0:512] for b in range(B)]
        Bk = [AB[b][:, 512:1024] for b in range(B)]

        ld = sem("ld")
        ring_in = [sem(f"ring_in{r}") for r in range(4)]
        wt_ps, wt_ev = sem("wt_ps"), sem("wt_ev")
        gh_ps, gh_ev = sem("gh_ps"), sem("gh_ev")
        set_pe, set_dve, set_pool, ready = sem("set_pe"), sem("set_dve"), sem("set_pool"), sem("ready")
        dve_own, pool_own, act_own = sem("dve_own"), sem("pool_own"), sem("act_own")
        xin_in, at_in, x2_st, at_st = sem2("xin_in"), sem("at_in"), sem2("x2_st"), sem("at_st")
        each = ("ffn_ps x1 bn xn xT_ps xnT k_ps v_ps ab_ps q_ps g_ps ssk kn v_ev qsq ssq q_ev "
                "zi gate e4 dec_ps draw d33 gram_ps no z_ps zc inv_ps yx s_ps scp y_ps yq "
                "y3 yT_ps yT x2 rbn rrs rxn rxT_ps rxnT h_ps hT lg_ps top ex al sl_ps sacc").split()
        shared = ("uw qg wo_ps ksq rs rk rq ez ln la be tanh rhsd cum_ps kd kqt kp qaT ym yfin yv yrs ysq nn gq_ps "
                  "uw_ps").split()
        S = {n: sem2(n) for n in each}
        S.update({n: [sem(n)] * B for n in shared})

        def both(i, b):
            return 2 * i - 1 + b

        aT_ps, aT = sem("aT_ps"), sem("aT")
        carriers = sem("carriers")
        mid_pe, mid_act, mid_dve = sem("mid_pe"), sem("mid_act"), sem("mid_dve")

        block = ctx.enter_context(nc.Block())

        def stand_alone(e):
            e.sem_inc(carriers, 1)

        class Own:
            def __init__(self, e, sm_):
                self.e, self.sem, self.base, self.n = e, sm_, 0, 0

            def __call__(self, ins):
                ins.then_inc(self.sem, 1)
                self.n += 1
                self.e.wait_ge(self.sem, self.base + self.n)

        jobs = []
        for j in range(2):
            jobs.append((w1[j * P:(j + 1) * P, 0:D], P, KC, ("w1", j)))
        jobs.append((w2, NS, 2, ("w2", 0)))
        for j in range(4):
            jobs.append((wo[j * P:(j + 1) * P, :], P, KC, ("wo", j)))
        for j in range(12):
            jobs.append((wih[j * P:(j + 1) * P, :], P, KC, ("wih", j)))
        jobs.append((None, P, KC, ("hs", 0)))
        for j in range(12):
            jobs.append((whh[j * P:(j + 1) * P, :], P, KC, ("whh", j)))
        NJ = len(jobs)
        HSJ = [j for j in range(NJ) if jobs[j][3][0] == "hs"][0]
        rings = [kn[0], kn[1], qs[0], qs[1]]
        tps = [A[0], A[1], Bk[0], Bk[1]]
        woT = vk[0]
        hsT = gate[0]
        whh_ring = [gate[1], dr[0]]

        def woT_at(k):
            return (vk[0], vk[1])[k // 2][:, (k % 2) * D:(k % 2 + 1) * D]

        def dest(j):
            kind, r = jobs[j][3]
            if kind == "w1":
                return w1T[:, :].rearrange("p (k n) -> p k n", k=KC)[:, :, r * P:(r + 1) * P]
            if kind == "w2":
                return w2T[:, :].rearrange("p (k n) -> p k n", k=2)
            if kind == "wih":
                return wihT[:, :].rearrange("p (k n) -> p k n", k=KC)[:, :, r * P:(r + 1) * P]
            if kind == "hs":
                return hsT[:, :].rearrange("p (k n) -> p k n", k=KC)
            if kind == "whh":
                return whh_ring[r % 2][:, :].rearrange("p (k n) -> p k n", k=KC)
            return None

        LD = 16 * 20
        tmp_b = yy[0]
        b1c = xx[0]
        wvn = [npk[0][:, k * D:(k + 1) * D] for k in range(3)] + [npk[1][:, 0:D]]
        w1b = [npk[1][:, D:2 * D], npk[1][:, 2 * D:3 * D]]
        bhh_t, bih_t = (no[0], xnT[0]), (no[1], xnT[1])
        bv_c, bo_t = xx[1], yy[1]
        mean_t, prod_t = scr[0], scr[1]
        ssc = sm[0][:, 0:1]
        taut = sm[0][:, 1:2]

        def ring_user(j, n):
            seen = 0
            for jj in range(NJ):
                if jobs[jj][0] is not None:
                    if seen == n - 4:
                        return jj + 1
                    seen += 1

        def ring_no(j):
            return sum(1 for jj in range(j) if jobs[jj][0] is not None)

        def slot_sum_cols(b):
            return AB[b][:, 0:KC * NS + NS]

        def gh_part(pe, mm, r, j):
            pe.wait_ge(wt_ev, HSJ + 2 + r)
            if r >= 2:
                pe.wait_ge(gh_ev, r - 1)
            for k in range(KC):
                last = mm(C[r % 2][:, 0:P], hsT[:, k * P:(k + 1) * P], whh_ring[r % 2][:, k * P:(k + 1) * P],
                          start=(k == 0), stop=(k == KC - 1))
            last.then_inc(gh_ps, 1)

        giT, gr, gz, gn, ht, hTT = kn[0], qs[0], qs[1], gate[0], gate[1], kn[1]
        NMID = 4

        def mid(e, m):
            o_pe, o_act, o_dve = 3 * m, 4 * m, 7 * m
            if e is nc.tensor:
                mm, tr = nc.tensor.matmul, nc.tensor.transpose
                e.wait_ge(mid_dve, o_dve + 1)
                for j, dst in enumerate((A[0], A[1], C[0])):
                    for k in range(KC):
                        last = mm(dst[:, :], giT[:, k * P:(k + 1) * P], wihT[:, k * 3 * D + j * D:k * 3 * D + (j + 1) * D],
                                  start=(k == 0), stop=(k == KC - 1))
                last.then_inc(mid_pe, 1)
                e.wait_ge(mid_dve, o_dve + 6)
                e.wait_ge(aT, NT * (m + 1))
                for k in range(KC):
                    last = tr(Bk[0][:, k * P:(k + 1) * P], ht[:, k * P:(k + 1) * P], ident[:, :])
                last.then_inc(mid_pe, 1)
                e.wait_ge(mid_act, o_act + 4)
                for k in range(KC):
                    last = mm(Bk[1][:, :], hTT[:, k * P:(k + 1) * P], voT[:, k * D:(k + 1) * D],
                              start=(k == 0), stop=(k == KC - 1))
                last.then_inc(mid_pe, 1)
                e.wait_ge(mid_dve, o_dve + 7)
            elif e is nc.scalar:
                act = nc.scalar.activation
                e.wait_ge(mid_dve, o_dve + 2)
                act(gr[:, :], gr[:, :], ACT.Sigmoid).then_inc(mid_act, 1)
                e.wait_ge(mid_dve, o_dve + 3)
                act(gz[:, :], gz[:, :], ACT.Sigmoid).then_inc(mid_act, 1)
                e.wait_ge(mid_dve, o_dve + 4)
                act(gn[:, :], gn[:, :], ACT.Tanh).then_inc(mid_act, 1)
                e.wait_ge(mid_pe, o_pe + 2)
                act(hTT[:, :], Bk[0][:, :], ACT.Copy).then_inc(mid_act, 1)

        @block.sync
        def _(sp):
            def load(dst, src):
                sp.dma_start(dst, src, allow_slow_non_contiguous=True).then_inc(ld, 16)
            load(hs[0:NS, :], slot_init)
            load(hs[NS:P, :], slot_init)
            load(ssc[0:NS, :], slot_scale)
            load(ssc[NS:P, :], slot_scale)
            load(taut, tau.partition_broadcast(P))
            load(b1c[:, 0:2], b1.rearrange("(j p) -> p j", p=P))
            load(b2s[:, :], b2.partition_broadcast(P))
            load(bv_c[:, 0:KC], bv.rearrange("(j p) -> p j", p=P))
            load(bo_t[:, :], bo.partition_broadcast(P))
            load(ab_bias[:, 0:H], ba.partition_broadcast(P))
            load(ab_bias[:, H:2 * H], bb.partition_broadcast(P))
            load(gcol[:, :], g_norm.rearrange("(j p) -> p j", p=P))
            load(bih_t[0][:, :], bih[0:2 * D].partition_broadcast(P))
            load(bih_t[1][:, :], bih[2 * D:3 * D].partition_broadcast(P))
            load(bhh_t[0][:, :], bhh[0:2 * D].partition_broadcast(P))
            load(bhh_t[1][:, :], bhh[2 * D:3 * D].partition_broadcast(P))
            load(npk[0][:, :].rearrange("p (k n) -> p k n", k=3), wv[0:3 * P, :].rearrange("(k p) n -> p k n", p=P))
            load(npk[1][:, 0:D], wv[3 * P:4 * P, :])
            load(npk[1][:, D:3 * D].rearrange("p (k n) -> p k n", k=2),
                 w1[:, D:2 * D].rearrange("(k p) n -> p k n", p=P))
            load(w_out[:, :].rearrange("p (k n) -> p k n", k=KC), Wo.rearrange("(k p) n -> p k n", p=P))
            n_in = 0
            for j in range(NJ):
                if jobs[j][0] is None:
                    continue
                if n_in >= 4:
                    sp.wait_ge(wt_ps, ring_user(j, n_in))
                src, rows, cols, _ = jobs[j]
                sp.dma_start(rings[n_in % 4][0:rows, 0:cols * P], src).then_inc(ring_in[n_in % 4], 16)
                n_in += 1
            w4 = w_kvqg[:, :].rearrange("p (k m n) -> p k m n", k=KC, m=4)
            for m, w in enumerate((Wk, Wv, Wq, Wg)):
                load(w4[:, :, m, :], w.rearrange("(k p) n -> p k n", p=P))
            wab = w_ab[:, :].rearrange("p (k m n) -> p k m n", k=KC, m=2)
            for m, w in enumerate((Wa, Wb)):
                load(wab[:, :, m, :], w.rearrange("(k p) n -> p k n", p=P))

            def load_x(src, n, i, free):
                for b in range(B):
                    if free is not None:
                        sp.wait_ge(free[b], i)
                    sp.dma_start(xin[b][:, :], src[b, bass.ds(n, 1), :, :].rearrange("o p d -> (o p) d"))\
                        .then_inc(xin_in[b], 16)

            sp.wait_ge(ready, 1)
            for b in range(B):
                sp.dma_start(xin[b][:, :], x_t[b, 0, :, :]).then_inc(xin_in[b], 16)
            with sp.Fori(1, NT) as i:
                load_x(x_t, i, i, S["rxn"])
                sp.wait_ge(aT, i)
                sp.dma_start(at_dram[0][bass.ds(i - 1, 1), :, :].rearrange("o p d -> (o p) d"), aT_out[:, :])\
                    .then_inc(at_st, 16)
            sp.wait_ge(aT, NT)
            sp.dma_start(at_dram[0][NT - 1, :, :], aT_out[:, :]).then_inc(at_st, 16)
            for b in range(B):
                sp.wait_ge(S["rxn"][b], NT)
            sp.wait_ge(at_st, 16 * NT)

            def load_at(m, n):
                sp.dma_start(aT_in[:, :], at_dram[m][bass.ds(n, 1), :, :].rearrange("o p d -> (o p) d"))\
                    .then_inc(at_in, 16)
            for b in range(B):
                sp.dma_start(xin[b][:, :], x_t[b, 0, :, :]).then_inc(xin_in[b], 16)
            sp.dma_start(aT_in[:, :], at_dram[0][0, :, :]).then_inc(at_in, 16)
            with sp.Fori(1, NT) as i:
                load_x(x_t, i, i, S["x1"])
                load_at(0, i)
                for b in range(B):
                    sp.wait_ge(S["x2"][b], i)
                    sp.dma_start(x2_dram[b, bass.ds(i - 1, 1), :, :].rearrange("o p d -> (o p) d"), xc[b][:, :])\
                        .then_inc(x2_st[b], 16)
                sp.wait_ge(aT, i + NT)
                sp.dma_start(at_dram[1][bass.ds(i - 1, 1), :, :].rearrange("o p d -> (o p) d"), aT_out[:, :])\
                    .then_inc(at_st, 16)
            for b in range(B):
                sp.wait_ge(S["x2"][b], NT)
                sp.dma_start(x2_dram[b, NT - 1, :, :], xc[b][:, :]).then_inc(x2_st[b], 16)
            sp.wait_ge(aT, 2 * NT)
            sp.dma_start(at_dram[1][NT - 1, :, :], aT_out[:, :]).then_inc(at_st, 16)
            for b in range(B):
                sp.wait_ge(x2_st[b], 16 * NT)
            sp.wait_ge(at_st, 32 * NT)

            for b in range(B):
                sp.dma_start(xin[b][:, :], x2_dram[b, 0, :, :]).then_inc(xin_in[b], 16)
            sp.dma_start(aT_in[:, :], at_dram[1][0, :, :]).then_inc(at_in, 16)
            with sp.Fori(1, NT) as i:
                load_x(x2_dram, i, i + NT, S["x1"])
                load_at(1, i)
                for b in range(B):
                    sp.dma_start(out_t[b, bass.ds(i - 1, 1), :, :].rearrange("o p d -> (o p) d"), xc[b][:, :])\
                        .then_inc(x2_st[b], 16)
            for b in range(B):
                sp.wait_ge(S["x1"][b], 2 * NT)
                sp.dma_start(out_t[b, NT - 1, :, :], xc[b][:, :]).then_inc(x2_st[b], 16)
            for b in range(B):
                sp.wait_ge(x2_st[b], 32 * NT)

        @block.tensor
        def _(pe):
            mm, tr = nc.tensor.matmul, nc.tensor.transpose
            pe.wait_ge(set_pool, 1)
            for j in range(NJ):
                src, rows, cols, (kind, r) = jobs[j]
                if kind == "hs":
                    pe.wait_ge(set_dve, 1)
                    buf = hs
                else:
                    n = ring_no(j)
                    pe.wait_ge(ring_in[n % 4], 16 * (n // 4 + 1))
                    buf = rings[n % 4]
                if j >= 4:
                    pe.wait_ge(wt_ev, j - 3)
                for k in range(cols):
                    last = tr(tps[j % 4][:, k * rows:(k + 1) * rows], buf[0:rows, k * P:(k + 1) * P],
                              ident[0:rows, 0:rows])
                last.then_inc(wt_ps, 1)
                if kind == "whh" and r >= 1:
                    gh_part(pe, mm, r - 1, j)
            gh_part(pe, mm, 11, NJ)
            pe.wait_ge(set_dve, 2)
            pe.wait_ge(gh_ev, 12)
            mm(C[0][:, :], aT_in[0:NS, :], hs[0:NS, :], start=True, stop=True).then_inc(set_pe, 1)
            for k in range(KC):
                if k >= 2:
                    pe.wait_ge(set_dve, 1 + k)
                for e in range(KC):
                    last = mm(ST[k % 2][:, :], wvn[e][:, k * P:(k + 1) * P], woT_at(e), start=(e == 0), stop=(e == KC - 1))
                last.then_inc(set_pe, 1)
            pe.wait_ge(set_dve, 7)
            for e in range(KC):
                last = mm(C[0][:, :], xin[0][:, e * P:(e + 1) * P], woT_at(e), start=(e == 0), stop=(e == KC - 1))
            last.then_inc(set_pe, 1)

            def route(i, n):
                for b in range(B):
                    pe.wait_ge(S["rxn"][b], n)
                    if i is not None:
                        pe.wait_ge(S["yT"][b], i)
                    else:
                        pe.wait_ge(S["sacc"][b], n - 1)
                    for k in range(KC):
                        last = tr(A[b][:, k * P:(k + 1) * P], xn[b][:, k * P:(k + 1) * P], ident[:, :])
                    last.then_inc(S["rxT_ps"][b], 1)
                for b in range(B):
                    pe.wait_ge(S["rxnT"][b], n)
                    if i is not None:
                        pe.wait_ge(S["yq"][b], i)
                    for j in range(2):
                        for k in range(KC):
                            last = mm(C[b][:, j * P:(j + 1) * P], w1T[:, k * HID + j * P:k * HID + (j + 1) * P],
                                      xnT[b][:, k * P:(k + 1) * P], start=(k == 0), stop=(k == KC - 1))
                    last.then_inc(S["h_ps"][b], 1)
                for b in range(B):
                    pe.wait_ge(S["hT"][b], n)
                    if i is not None:
                        pe.wait_ge(S["x2"][b], i)
                    elif b == 0:
                        pe.wait_ge(aT, n - 1)
                    for j in range(2):
                        last = mm(Bk[b][:, 0:NS], hT[b][:, j * P:(j + 1) * P], w2T[:, j * NS:(j + 1) * NS],
                                  start=(j == 0), stop=(j == 1))
                    last.then_inc(S["lg_ps"][b], 1)
                for b in range(B):
                    pe.wait_ge(S["al"][b], n)
                    pe.wait_ge(S["rxnT"][b], n)
                    for k in range(KC):
                        mm(A[b][:, k * NS:(k + 1) * NS], xn[b][:, k * P:(k + 1) * P], alpha[:, b * NS:(b + 1) * NS],
                           start=True, stop=True)
                    mm(A[b][:, KC * NS:(KC + 1) * NS], ones[:, :], alpha[:, b * NS:(b + 1) * NS], start=True, stop=True)\
                        .then_inc(S["sl_ps"][b], 1)
                tr(Bk[0][:, P:2 * P], alpha[:, :], ident[:, :]).then_inc(aT_ps, 1)

            pe.wait_ge(ready, 1)
            with pe.Fori(1, NT + 1) as i:
                route(None, i)
            mid(pe, 0)

            with pe.Fori(1, NT + 1) as i:
                def h32(t, c, h, w, o, n):
                    return t[CH * c:CH * (c + 1), h * w + o:h * w + o + n]

                def cells(dst, dw, lhs, lw, lo, rhs, rw, ro, n):
                    for h in range(H):
                        for c in range(NC):
                            last = mm(h32(dst, c, h, dw, 0, n), h32(lhs, c, h, lw, lo, CH), h32(rhs, c, h, rw, ro, n),
                                      start=True, stop=True)
                    return last

                for b in range(B):
                    pe.wait_ge(at_in, 16 * i)
                    pe.wait_ge(S["sacc"][b], i + NT - 1)
                    mm(A[b][:, :], aT_in[b * NS:(b + 1) * NS, :], sv[b * NS:(b + 1) * NS, :], start=True, stop=True)\
                        .then_inc(S["ffn_ps"][b], 1)
                for b in range(B):
                    pe.wait_ge(S["xn"][b], i)
                    if b == 0:
                        pe.wait_ge(aT, i + NT - 1)
                    for k in range(KC):
                        last = tr(Bk[b][:, k * P:(k + 1) * P], xn[b][:, k * P:(k + 1) * P], ident[:, :])
                    last.then_inc(S["xT_ps"][b], 1)

                def project(b, m, dst):
                    for k in range(KC):
                        last = mm(dst, xnT[b][:, k * P:(k + 1) * P], w_kvqg[:, (k * 4 + m) * D:(k * 4 + m + 1) * D],
                                  start=(k == 0), stop=(k == KC - 1))
                    return last
                for b in range(B):
                    pe.wait_ge(S["xnT"][b], i)
                    project(b, 0, A[b][:, :]).then_inc(S["k_ps"][b], 1)
                    for k in range(KC):
                        last = mm(C[b][:, 0:2 * H], xnT[b][:, k * P:(k + 1) * P], w_ab[:, k * 2 * H:(k + 1) * 2 * H],
                                  start=(k == 0), stop=(k == KC - 1))
                    last.then_inc(S["ab_ps"][b], 1)
                    project(b, 1, Bk[b][:, :]).then_inc(S["v_ps"][b], 1)
                for b in range(B):
                    pe.wait_ge(S["v_ev"][b], i)
                    project(b, 2, Bk[b][:, :]).then_inc(S["q_ps"][b], 1)
                    pe.wait_ge(S["kn"][b], i)
                    project(b, 3, A[b][:, :]).then_inc(S["g_ps"][b], 1)
                for b in range(B):
                    pe.wait_ge(S["la"][b], both(i, b))
                    for m, mask in enumerate((before, upto, after, chunk)):
                        last = mm(C[b][:, 64 + m * H:64 + (m + 1) * H], mask[:, :], s(b, "la"), start=True, stop=True)
                    last.then_inc(S["cum_ps"][b], 1)
                for b in range(B):
                    pe.wait_ge(S["rhsd"][b], both(i, b))
                    pe.wait_ge(S["q_ev"][b], i)
                    mm(Bk[b][:, :], after[:, :], dr[b][:, :], start=True, stop=True).then_inc(S["dec_ps"][b], 1)
                for b in range(B):
                    pe.wait_ge(S["kqt"][b], both(i, b))
                    pe.wait_ge(S["gate"][b], i)
                    pe.wait_ge(S["draw"][b], i)
                    stand_alone(pe)
                    cells(AB[b], 2 * HD, kqT[b], 2 * HD, 0, kqT[b], 2 * HD, 0, 2 * HD).then_inc(S["gram_ps"][b], 1)
                for l in range(LEVELS):
                    for b in range(B):
                        pe.wait_ge(S["no"][b], LEVELS * (i - 1) + l + 1)
                        pe.wait_ge(S["yx"][b], LEVELS * (i - 1) + l + 1)
                        if l == 0:
                            pe.wait_ge(S["e4"][b], i)
                        stand_alone(pe)
                        cells(C[b], HD, no[b][:, (l % 2) * D:(l % 2 + 1) * D], HD, 0, xx[b], HD, 0, HD)\
                            .then_inc(S["z_ps"][b], 1)
                    for b in range(B):
                        pe.wait_ge(S["zc"][b], LEVELS * (i - 1) + l + 1)
                        stand_alone(pe)
                        cells(A[b], HD, dr[b], HD, 0, yy[b], HD, 0, HD).then_inc(S["inv_ps"][b], 1)
                for b in range(B):
                    pe.wait_ge(S["yfin"][b], both(i, b))
                    pe.wait_ge(S["kp"][b], both(i, b))
                    stand_alone(pe)
                    cells(AB[b], 2 * HD, yy[b], HD, 0, vk[b], 2 * HD, 0, 2 * HD).then_inc(S["uw_ps"][b], 1)
                for b in range(B):
                    pe.wait_ge(S["uw"][b], both(i, b))
                    pe.wait_ge(S["kd"][b], both(i, b))
                    stand_alone(pe)
                    cells(AB[b], 2 * HD, uw[b], 2 * HD, HD, npk[b], 3 * HD, HD, 2 * HD).then_inc(S["gq_ps"][b], 1)
                    for c in range(NC - 1):
                        for h in range(H):
                            mm(ST[b][CH * (c + 1):CH * (c + 2), h * HD:(h + 1) * HD], h32(npk[b], c, h, 3 * HD, 2 * HD, HD),
                               h32(uw[b], c, h, 2 * HD, 0, HD), start=(h == 0), stop=False, skip_group_check=True)
                    for h in range(H):
                        for c in range(NC):
                            mm(h32(C[b], c, h, HD, 0, HD), h32(npk[b], c, h, 3 * HD, HD, CH), h32(uw[b], c, h, 2 * HD, 0, HD),
                               start=(h == 0), stop=False, skip_group_check=True)
                for c in range(NC):
                    for b in range(B):
                        if c == 0:
                            pe.wait_ge(S["qg"][b], both(i, b))
                        pe.wait_ge(S["scp"][b], NC * (i - 1) + c + 1)
                        stand_alone(pe)
                        n = (c + 1) % NC
                        if c == NC - 1:
                            for h in range(H):
                                mm(ST[b][0:CH, h * HD:(h + 1) * HD], h32(npk[b], c, h, 3 * HD, 2 * HD, HD),
                                   h32(uw[b], c, h, 2 * HD, 0, HD), start=(h == 0), stop=False, skip_group_check=True)
                        for h in range(H):
                            last = mm(ST[b][CH * n:CH * (n + 1), h * HD:(h + 1) * HD], h32(kqT[b], c, h, 2 * HD, HD, HD),
                                      h32(xx[b], c, h, HD, 0, HD), start=False, stop=True, skip_group_check=True)
                        last.then_inc(S["s_ps"][b], 1)
                        for h in range(H):
                            last = mm(h32(C[b], c, h, HD, 0, HD), h32(kqT[b], c, h, 2 * HD, 0, CH),
                                      h32(xx[b], c, h, HD, 0, HD), start=False, stop=True, skip_group_check=True)
                        if c == NC - 1:
                            last.then_inc(S["y_ps"][b], 1)
                for b in range(B):
                    pe.wait_ge(S["y3"][b], i)
                    for k in range(KC):
                        last = tr(A[b][:, k * P:(k + 1) * P], qs[b][:, k * P:(k + 1) * P], ident[:, :])
                    last.then_inc(S["yT_ps"][b], 1)
                for b in range(B):
                    pe.wait_ge(S["yT"][b], i)
                    for k in range(KC):
                        last = mm(Bk[b][:, :], xnT[b][:, k * P:(k + 1) * P], w_out[:, k * D:(k + 1) * D],
                                  start=(k == 0), stop=(k == KC - 1))
                    last.then_inc(S["wo_ps"][b], 1)
                route(i, i + NT)
            mid(pe, 1)

            with pe.Fori(NT + 1, 2 * NT + 1) as i:
                for b in range(B):
                    pe.wait_ge(at_in, 16 * i)
                    pe.wait_ge(S["x1"][b], i - 1)
                    mm(A[b][:, :], aT_in[b * NS:(b + 1) * NS, :], sv[b * NS:(b + 1) * NS, :], start=True, stop=True)\
                        .then_inc(S["ffn_ps"][b], 1)

        @block.scalar
        def _(sc):
            act = nc.scalar.activation
            own = Own(sc, act_own)
            for j in range(0, NJ):
                src, rows, cols, (kind, r) = jobs[j]
                sc.wait_ge(wt_ps, j + 1)
                if kind == "whh" and r >= 2:
                    sc.wait_ge(gh_ps, r - 1)
                view = tps[j % 4][:, 0:cols * rows].rearrange("p (k n) -> p k n", k=cols)
                if kind == "wo":
                    for k in range(KC):
                        last = act(woT_at(k)[:, r * P:(r + 1) * P], view[:, k, :], ACT.Copy)
                    last.then_inc(wt_ev, 1)
                else:
                    act(dest(j), view, ACT.Copy).then_inc(wt_ev, 1)

            def move(dst, src, n, ps, done):
                sc.wait_ge(ps, n)
                act(dst, src, ACT.Copy).then_inc(done, 1)

            def route(i, n):
                for b in range(B):
                    move(xnT[b][:, :], A[b][:, :], n, S["rxT_ps"][b], S["rxnT"][b])
                for b in range(B):
                    sc.wait_ge(S["h_ps"][b], n)
                    for j in range(2):
                        last = act(hT[b][:, j * P:(j + 1) * P], C[b][:, j * P:(j + 1) * P], ACT.Gelu, bias=h_bias[:, j:j + 1])
                    last.then_inc(S["hT"][b], 1)
                for b in range(B):
                    sc.wait_ge(S["top"][b], n)
                    act(lgt[b][:, 2 * NS:3 * NS], lgt[b][:, 0:NS], ACT.Exp, bias=s(b, "negm")).then_inc(S["ex"][b], 1)
                sc.wait_ge(aT_ps, n)
                sc.wait_ge(at_st, 16 * (n - 1))
                act(aT_out[:, :], Bk[0][:, P:2 * P], ACT.Copy).then_inc(aT, 1)

            sc.wait_ge(ready, 1)
            with sc.Fori(1, NT + 1) as i:
                route(None, i)
            mid(sc, 0)

            with sc.Fori(1, NT + 1) as i:
                for b in range(B):
                    move(xnT[b][:, :], Bk[b][:, :], i, S["xT_ps"][b], S["xnT"][b])
                for b in range(B):
                    sc.wait_ge(S["k_ps"][b], i)
                    act(scr[b][:, :], A[b][:, :], ACT.Square).then_inc(S["ksq"][b], 1)
                    move(heads(vk[b], 2)[:, :, 0:HD], Bk[b][:, :].rearrange("p (h e) -> p h e", h=H), i,
                         S["v_ps"][b], S["v_ev"][b])
                for b in range(B):
                    sc.wait_ge(S["zi"][b], i)
                    act(s(b, "ez"), s(b, "zi"), ACT.Exp).then_inc(S["ez"][b], 1)
                for b in range(B):
                    sc.wait_ge(S["q_ps"][b], i)
                    act(qs[b][:, :], Bk[b][:, :], ACT.Copy)
                    sc.wait_ge(S["ssk"][b], i)
                    act(scr[b][:, :], Bk[b][:, :], ACT.Square).then_inc(S["q_ev"][b], 1)
                for b in range(B):
                    sc.wait_ge(S["g_ps"][b], i)
                    sc.wait_ge(S["ssq"][b], i)
                    act(scr[b][:, :], A[b][:, :], ACT.Tanh, scale=0.5).then_inc(S["tanh"][b], 1)
                for b in range(B):
                    sc.wait_ge(S["ez"][b], both(i, b))
                    act(s(b, "ln"), s(b, "ez")[:, 0:H], ACT.Ln, bias=1.0).then_inc(S["ln"][b], 1)
                for b in range(B):
                    sc.wait_ge(S["cum_ps"][b], both(i, b))
                    act(s(b, "e4"), C[b][:, 64:64 + 4 * H], ACT.Exp).then_inc(S["e4"][b], 1)
                for b in range(B):
                    sc.wait_ge(S["dec_ps"][b], i)
                    act(dr[b][:, :], Bk[b][:, :], ACT.Exp).then_inc(S["draw"][b], 1)
                for l in range(LEVELS):
                    for b in range(B):
                        sc.wait_ge(S["z_ps"][b], LEVELS * (i - 1) + l + 1)
                        if l == 0:
                            sc.wait_ge(S["d33"][b], i)
                        act(dr[b][:, :], C[b][:, :], ACT.Copy).then_inc(S["zc"][b], 1)
                for b in range(B):
                    move(uw[b][:, 0:2 * D], AB[b][:, :], both(i, b), S["uw_ps"][b], S["uw"][b])
                for c in range(NC):
                    for b in range(B):
                        sc.wait_ge(S["s_ps"][b], NC * (i - 1) + c)
                        if c == 0:
                            sc.wait_ge(S["z_ps"][b], LEVELS * i)
                        act(xx[b][CH * c:CH * (c + 1), :], ST[b][CH * c:CH * (c + 1), :], ACT.Copy).then_inc(S["scp"][b], 1)
                for b in range(B):
                    sc.wait_ge(S["yq"][b], i)
                    act(scr[b][:, :], kn[b][:, :], ACT.Square, accum_out=s(b, "ys")).then_inc(S["ysq"][b], 1)
                for b in range(B):
                    move(xnT[b][:, :], A[b][:, :], i, S["yT_ps"][b], S["yT"][b])
                route(i, i + NT)
            mid(sc, 1)

        @block.gpsimd
        def _(pl):
            g = nc.gpsimd
            own = Own(pl, pool_own)
            own(g.memset(ident[:, :], 0.0))
            g.affine_select(out=ident[:, :], in_=ident[:, :], compare_op=ALU.not_equal, fill=1.0, base=0,
                            pattern=[[-1, P]], channel_multiplier=1).then_inc(set_pool, 1)
            g.iota(kqT[0][:, 0:P].bitcast(i32), pattern=[[0, P]], base=0, channel_multiplier=1)
            g.iota(kqT[1][:, 0:P].bitcast(i32), pattern=[[1, P]], base=0, channel_multiplier=0).then_inc(set_pool, 1)

            def power(dst, a, n):
                return g.tensor_tensor(dst, a, half[:, 0:n], ALU.pow)

            def rstd(b, n, bn, rs):
                pl.wait_ge(bn, n)
                own(g.tensor_scalar(s(b, "vs"), s(b, "mv")[:, 1:2], 1e-5, None, ALU.add))
                power(s(b, "rstd"), s(b, "vs"), 1).then_inc(rs, 1)

            pl.wait_ge(ready, 1)
            with pl.Fori(1, NT + 1) as i:
                own.base, own.n = 1 + 2 * (i - 1), 0
                for b in range(B):
                    pl.wait_ge(S["rbn"][b], i)
                    stand_alone(pl)
                    own(g.tensor_scalar(s(b, "vs"), s(b, "mv")[:, 1:2], 1e-5, None, ALU.add))
                    power(s(b, "rstd"), s(b, "vs"), 1).then_inc(S["rrs"][b], 1)
                assert own.n == 2
            PER = 2 * 4
            with pl.Fori(1, NT + 1) as i:
                own.base, own.n = 1 + 2 * NT + PER * (i - 1), 0
                for b in range(B):
                    pl.wait_ge(S["bn"][b], i)
                    stand_alone(pl)
                    own(g.tensor_scalar(s(b, "vs"), s(b, "mv")[:, 1:2], 1e-5, None, ALU.add))
                    power(s(b, "rstd"), s(b, "vs"), 1).then_inc(S["rs"][b], 1)
                for b in range(B):
                    pl.wait_ge(S["ssk"][b], i)
                    power(s(b, "rk"), s(b, "ssk"), H).then_inc(S["rk"][b], 1)
                for b in range(B):
                    pl.wait_ge(S["ssq"][b], i)
                    power(s(b, "rq"), s(b, "ssq"), H).then_inc(S["rq"][b], 1)
                for b in range(B):
                    pl.wait_ge(S["la"][b], both(i, b))
                    g.tensor_tensor(heads(dr[b]), bc(s(b, "la")), allheads(tri[:, :]), ALU.mult).then_inc(S["rhsd"][b], 1)
                for b in range(B):
                    pl.wait_ge(S["be"][b], both(i, b))
                    pl.wait_ge(S["e4"][b], i)
                    own(g.tensor_tensor(s(b, "bel"), s(b, "be"), s(b, "e4")[:, 2 * H:3 * H], ALU.mult))
                    g.tensor_tensor(heads(npk[b], 3)[:, :, 2 * HD:3 * HD], heads(kn[b]), bc(s(b, "bel")), ALU.mult)\
                        .then_inc(S["kd"][b], 1)
                for b in range(B):
                    pl.wait_ge(S["draw"][b], i)
                    own(g.tensor_tensor(heads(dr[b]), heads(dr[b]), allheads(tri[:, :]), ALU.mult))
                    stand_alone(pl)
                    g.memset(D33[b][:, :, 0:1], 0.0)
                    g.tensor_tensor(D33[b][:, :, 1:HD + 1], heads(dr[b]), bc(s(b, "be")), ALU.mult).then_inc(S["d33"][b], 1)
                for b in range(B):
                    g.tensor_tensor(heads(qa[b], 2)[:, :, HD:2 * HD], bc(s(b, "e4")[:, 3 * H:4 * H]), allheads(eye32[:, :]),
                                    ALU.mult).then_inc(S["qaT"][b], 1)
                for b in range(B):
                    pl.wait_ge(S["nn"][b], both(i, b))
                    g.tensor_tensor(heads(yy[b]), heads(npk[b], 3)[:, :, 0:HD], allheads(levmask[:, 0:CH]), ALU.mult)\
                        .then_inc(S["ym"][b], 1)
                for l in range(LEVELS):
                    for b in range(B):
                        if l >= 2:
                            pl.wait_ge(S["z_ps"][b], LEVELS * (i - 1) + l - 1)
                        g.tensor_tensor(heads(no[b][:, (l % 2) * D:(l % 2 + 1) * D]), heads(npk[b], 3)[:, :, 0:HD],
                                        allheads(levmask[:, (l + 1) * CH:(l + 2) * CH]), ALU.mult).then_inc(S["no"][b], 1)
                for b in range(B):
                    pl.wait_ge(S["yv"][b], both(i, b))
                    power(s(b, "yr"), s(b, "yv"), 1).then_inc(S["yrs"][b], 1)
                for b in range(B):
                    pl.wait_ge(S["rbn"][b], i + NT)
                    stand_alone(pl)
                    own(g.tensor_scalar(s(b, "vs"), s(b, "mv")[:, 1:2], 1e-5, None, ALU.add))
                    power(s(b, "rstd"), s(b, "vs"), 1).then_inc(S["rrs"][b], 1)
                assert own.n == 2 * 4, own.n

        @block.vector
        def _(ve):
            v = nc.vector
            tt, ts, stt = v.tensor_tensor, v.tensor_scalar, v.scalar_tensor_tensor
            own = Own(ve, dve_own)
            ve.wait_ge(ld, LD)
            own(ts(hs[:, :], hs[:, :], ssc, None, ALU.mult))
            own(v.memset(aT_in[:, :], 1.0 / NS))
            ve.nop().then_inc(set_dve, 1)
            v.memset(ones[:, :], 1.0)
            v.memset(half[:, :], -0.5)
            for b in range(B):
                v.memset(ST[b][:, :], 0.0)
                own(v.memset(slotacc[b][:, :], 0.0))
            own(stt(sm[0][:, 2:3], taut, -1.0, taut, ALU.mult, ALU.max))
            own(ts(sm[0][:, 3:4], sm[0][:, 2:3], 0.1, None, ALU.add))
            own(v.reciprocal(itau[:, :], sm[0][:, 3:4]))
            own(ts(b2s[:, :], b2s[:, :], itau[:, :], None, ALU.mult))
            for k in range(KC):
                own(ts(w_out[:, k * D:(k + 1) * D], w_out[:, k * D:(k + 1) * D], gcol[:, k:k + 1], 0.5, ALU.mult, ALU.mult))
            own(tt(gh[:, 0:2 * D], bih_t[0][:, :], bhh_t[0][:, :], ALU.add))
            own(v.tensor_copy(gh[:, 2 * D:3 * D], bhh_t[1][:, :]))
            own(v.tensor_copy(bih_n[:, :], bih_t[1][:, :]))
            for k in range(KC):
                own(ts(xin[0][:, k * P:(k + 1) * P], ones[:, :], bv_c[:, k:k + 1], None, ALU.mult))
            pi, fi = kqT[0][:, 0:P].bitcast(i32), kqT[1][:, 0:P].bitcast(i32)
            u, w, z = (kqT[0][:, P * m:P * (m + 1)].bitcast(i32) for m in (1, 2, 3))
            same = kqT[1][:, P:2 * P]
            ve.wait_ge(set_pool, 2)
            own(tt(u, pi, fi, ALU.bitwise_xor))
            own(ts(w, u, 5, None, ALU.logical_shift_right))
            own(ts(chunk[:, :], w, 0, None, ALU.is_equal))
            own(tt(before[:, :], pi, fi, ALU.is_lt))
            own(tt(before[:, :], before[:, :], chunk[:, :], ALU.mult))
            own(tt(upto[:, :], pi, fi, ALU.is_le))
            own(tt(upto[:, :], upto[:, :], chunk[:, :], ALU.mult))
            own(tt(after[:, :], chunk[:, :], upto[:, :], ALU.subtract))
            own(ts(w, pi, 31, None, ALU.bitwise_and))
            own(tt(tri[:, :], w[:, 0:CH], fi[:, 0:CH], ALU.is_le))
            own(tt(u[:, 0:CH], w[:, 0:CH], fi[:, 0:CH], ALU.bitwise_xor))
            own(ts(eye32[:, :], u[:, 0:CH], 0, None, ALU.is_equal))
            for l in range(LEVELS + 1):
                own(ts(z[:, 0:CH], u[:, 0:CH], l, None, ALU.logical_shift_right))
                own(ts(levmask[:, l * CH:(l + 1) * CH], z[:, 0:CH], 1, None, ALU.is_equal))
            ve.nop().then_inc(set_dve, 1)
            for r in range(12):
                ve.wait_ge(gh_ps, r + 1)
                ins = tt(gh[:, r * P:(r + 1) * P], gh[:, r * P:(r + 1) * P], C[r % 2][:, 0:P], ALU.add)
                ins.then_inc(gh_ev, 1)
            ve.wait_ge(set_pe, 1)
            own(v.tensor_copy(mean_t[:, :], C[0][:, :]))
            for j in range(2):
                own(tt(prod_t[:, :], mean_t[:, :], w1b[j], ALU.mult))
                own(v.tensor_reduce(sm[0][:, 4 + j:5 + j], prod_t[:, :], AX.X, ALU.add))
            own(tt(h_bias[:, :], sm[0][:, 4:6], b1c[:, 0:2], ALU.add))
            for k in range(KC):
                ve.wait_ge(set_pe, 2 + k)
                ins = v.tensor_copy(voT[:, k * D:(k + 1) * D], ST[k % 2][:, :])
                ins.then_inc(set_dve, 1)
            ve.wait_ge(set_dve, 2 + KC)
            v.memset(ST[0][:, :], 0.0)
            own(v.memset(ST[1][:, :], 0.0))
            ve.nop().then_inc(set_dve, 1)
            ve.wait_ge(set_pe, 6)
            own(tt(bvo[:, :], C[0][:, :], bo_t[:, :], ALU.add))
            own(ts(bvo[:, :], bvo[:, :], 0.5, None, ALU.mult))
            ve.wait_ge(ld, LD + 16 * 6)
            ve.wait_ge(wt_ev, NJ)
            ve.nop().then_inc(ready, 1)

            def normalise(b, src, n, bn, rs, done):
                ve.wait_ge(rs, n)
                ts(xn[b][:, :], src, s(b, "mv")[:, 0:1], s(b, "rstd"), ALU.subtract, ALU.mult).then_inc(done, 1)

            def moments(b, src, bn):
                own(v.bn_stats(s(b, "stats"), src))
                stand_alone(ve)
                v.bn_aggr(s(b, "mv"), s(b, "stats")).then_inc(bn, 1)

            def route(i, n, src):
                for b in range(B):
                    if i is None:
                        ve.wait_ge(xin_in[b], 16 * n)
                    else:
                        stand_alone(ve)
                    moments(b, src[b][:, :], S["rbn"][b])
                for b in range(B):
                    ve.wait_ge(S["sl_ps"][b], n - 1)
                    ve.wait_ge(S["rrs"][b], n)
                    ts(xn[b][:, :], src[b][:, :], s(b, "mv")[:, 0:1], s(b, "rstd"), ALU.subtract, ALU.mult)\
                        .then_inc(S["rxn"][b], 1)
                for b in range(B):
                    lg, rep = lgt[b][:, 0:NS], lgt[b][:, NS:2 * NS]
                    ve.wait_ge(S["lg_ps"][b], n)
                    own(stt(lg, Bk[b][:, 0:NS], itau[:, :], b2s[:, :], ALU.mult, ALU.add))
                    stand_alone(ve)
                    own(v.max(s(b, "top"), lg))
                    ts(s(b, "negm"), s(b, "top")[:, 0:1], -1.0, None, ALU.mult).then_inc(S["top"][b], 1)
                    stand_alone(ve)
                    own(v.match_replace(out=rep, in_to_replace=s(b, "top"), in_values=lg, imm_value=BIG))
                    own(tt(rep, lg, rep, ALU.not_equal))
                for b in range(B):
                    e, al = lgt[b][:, 2 * NS:3 * NS], alpha[:, b * NS:(b + 1) * NS]
                    ve.wait_ge(S["ex"][b], n)
                    own(tt(lgt[b][:, 0:NS], e, lgt[b][:, NS:2 * NS], ALU.mult))
                    own(v.tensor_reduce(s(b, "den"), lgt[b][:, 0:NS], AX.X, ALU.add))
                    own(v.reciprocal(s(b, "rden"), s(b, "den")))
                    ve.wait_ge(aT_ps, n - 1)
                    ts(al, lgt[b][:, 0:NS], s(b, "rden"), None, ALU.mult).then_inc(S["al"][b], 1)
                for b in range(B):
                    ve.wait_ge(S["sl_ps"][b], n)
                    tt(slotacc[b][:, :], slotacc[b][:, :], slot_sum_cols(b), ALU.add).then_inc(S["sacc"][b], 1)

            ROUTE = 2 * (1 + 1 + 1 + 1 + 1 + 3)
            base0 = own.n
            with ve.Fori(1, NT + 1) as i:
                own.base, own.n = base0 + ROUTE * (i - 1), 0
                route(None, i, xin)
                assert own.n == ROUTE
            own.base, own.n = 0, base0 + ROUTE * NT

            def mid_dve_part(m):
                o_pe, o_act = 3 * m, 4 * m
                for b in range(B):
                    ve.wait_ge(S["sacc"][b], NT * (m + 1))
                    ws = slotacc[b][:, KC * NS:(KC + 1) * NS]
                    own(ts(ws, ws, 1e-8, None, ALU.add))
                    own(v.reciprocal(lgt[b][:, 0:NS], ws))
                    own(tt(giT[:, :].rearrange("p (k n) -> p k n", k=KC)[:, :, b * NS:(b + 1) * NS],
                           slotacc[b][:, 0:KC * NS].rearrange("p (k n) -> p k n", k=KC),
                           lgt[b][:, 0:NS].unsqueeze(1).to_broadcast([P, KC, NS]), ALU.mult))
                    own(v.memset(slotacc[b][:, :], 0.0))
                ve.nop().then_inc(mid_dve, 1)
                ve.wait_ge(mid_pe, o_pe + 1)
                tt(gr[:, :], A[0][:, :], gh[:, 0:D], ALU.add).then_inc(mid_dve, 1)
                tt(gz[:, :], A[1][:, :], gh[:, D:2 * D], ALU.add).then_inc(mid_dve, 1)
                own(tt(gn[:, :], C[0][:, :], bih_n[:, :], ALU.add))
                ve.wait_ge(mid_act, o_act + 1)
                own(tt(gr[:, :], gr[:, :], gh[:, 2 * D:3 * D], ALU.mult))
                tt(gn[:, :], gn[:, :], gr[:, :], ALU.add).then_inc(mid_dve, 1)
                ve.wait_ge(mid_act, o_act + 3)
                own(tt(gr[:, :], hs[:, :], gn[:, :], ALU.subtract))
                own(tt(gz[:, :], gz[:, :], gr[:, :], ALU.mult))
                own(tt(ht[:, :], gn[:, :], gz[:, :], ALU.add))
                ve.nop().then_inc(mid_dve, 2)
                ve.wait_ge(mid_pe, o_pe + 3)
                stt(sv[:, :], Bk[1][:, :], 0.5, bvo[:, :], ALU.mult, ALU.add).then_inc(mid_dve, 1)
            mid_dve_part(0)

            PER = ROUTE + 2 * 12
            base1 = own.n
            with ve.Fori(1, NT + 1) as i:
                own.base, own.n = base1 + 1000 * 0 + PER * (i - 1), 0
                for b in range(B):
                    ve.wait_ge(S["ffn_ps"][b], i)
                    ve.wait_ge(xin_in[b], 16 * (i + NT))
                    ve.wait_ge(x2_st[b], 16 * (i - 1))
                    tt(xc[b][:, :], xin[b][:, :], A[b][:, :], ALU.add).then_inc(S["x1"][b], 1)
                    ve.wait_ge(S["x1"][b], i)
                    moments(b, xc[b][:, :], S["bn"][b])
                for b in range(B):
                    ve.wait_ge(S["rs"][b], both(i, b))
                    ts(xn[b][:, :], xc[b][:, :], s(b, "mv")[:, 0:1], s(b, "rstd"), ALU.subtract, ALU.mult)\
                        .then_inc(S["xn"][b], 1)
                for b in range(B):
                    ve.wait_ge(S["ksq"][b], both(i, b))
                    own(v.tensor_reduce(s(b, "ssk"), heads(scr[b]), AX.X, ALU.add))
                    ts(s(b, "ssk"), s(b, "ssk"), 1e-24, None, ALU.max).then_inc(S["ssk"][b], 1)
                    ve.wait_ge(S["ab_ps"][b], i)
                    own(tt(s(b, "ab"), C[b][:, 0:2 * H], ab_bias[:, :], ALU.add))
                    za, zb = s(b, "ab")[:, 0:H], s(b, "ab")[:, H:2 * H]
                    stt(s(b, "zi")[:, 0:H], za, -1.0, za, ALU.mult, ALU.min)
                    ts(s(b, "zi")[:, H:2 * H], zb, -1.0, 80.0, ALU.mult, ALU.min).then_inc(S["zi"][b], 1)
                    ve.wait_ge(S["rk"][b], both(i, b))
                    tt(heads(kn[b]), A[b][:, :].rearrange("p (h e) -> p h e", h=H), bc(s(b, "rk")), ALU.mult)\
                        .then_inc(S["kn"][b], 1)
                for b in range(B):
                    ve.wait_ge(S["kn"][b], i)
                    v.transpose(heads(kqT[b], 2)[:, :, 0:HD], heads(kn[b]))
                    ve.wait_ge(S["q_ev"][b], i)
                    own(v.tensor_reduce(s(b, "ssq"), heads(scr[b]), AX.X, ALU.add))
                    ts(s(b, "ssq"), s(b, "ssq"), 1e-24, None, ALU.max).then_inc(S["ssq"][b], 1)
                    v.transpose(heads(kqT[b], 2)[:, :, HD:2 * HD], heads(qs[b])).then_inc(S["kqt"][b], 1)
                for b in range(B):
                    ve.wait_ge(S["ln"][b], both(i, b))
                    stt(s(b, "la"), s(b, "ab")[:, 0:H], 0.0, s(b, "ln"), ALU.min, ALU.subtract).then_inc(S["la"][b], 1)
                    own(ts(s(b, "opb"), s(b, "ez")[:, H:2 * H], 1.0, None, ALU.add))
                    v.reciprocal(s(b, "be"), s(b, "opb")).then_inc(S["be"][b], 1)
                for b in range(B):
                    ve.wait_ge(S["tanh"][b], both(i, b))
                    stt(gate[b][:, :], scr[b][:, :], 1.0, A[b][:, :], ALU.add, ALU.mult).then_inc(S["gate"][b], 1)
                for b in range(B):
                    ve.wait_ge(S["e4"][b], i)
                    tt(heads(vk[b], 2)[:, :, HD:2 * HD], heads(kn[b]), bc(s(b, "e4")[:, 0:H]), ALU.mult)\
                        .then_inc(S["kp"][b], 1)
                    ve.wait_ge(S["gate"][b], i)
                    own(tt(heads(scr[b]), heads(qs[b]), bc(s(b, "e4")[:, H:2 * H]), ALU.mult))
                    own(v.transpose(heads(qa[b], 2)[:, :, 0:HD], heads(scr[b])))
                for b in range(B):
                    ve.wait_ge(S["gram_ps"][b], i)
                    ve.wait_ge(S["d33"][b], i)
                    own(tt(heads(npk[b], 3)[:, :, 0:HD], AB[b][:, :].rearrange("p (h e) -> p h e", h=H)[:, :, 0:HD],
                           D33[b][:, :, 0:HD], ALU.mult))
                    tt(heads(npk[b], 3)[:, :, HD:2 * HD], AB[b][:, :].rearrange("p (h e) -> p h e", h=H)[:, :, HD:2 * HD],
                       D33[b][:, :, 1:HD + 1], ALU.mult).then_inc(S["nn"][b], 1)
                for b in range(B):
                    ve.wait_ge(S["ym"][b], both(i, b))
                    own(tt(heads(yy[b]), allheads(eye32[:, :]), heads(yy[b]), ALU.subtract))
                    v.transpose(xx[b][:, :], yy[b][:, :]).then_inc(S["yx"][b], 1)
                for l in range(LEVELS):
                    for b in range(B):
                        ve.wait_ge(S["inv_ps"][b], LEVELS * (i - 1) + l + 1)
                        ins = tt(yy[b][:, :], yy[b][:, :], A[b][:, :], ALU.subtract)
                        if l < LEVELS - 1:
                            own(ins)
                            v.transpose(xx[b][:, :], yy[b][:, :]).then_inc(S["yx"][b], 1)
                        else:
                            ins.then_inc(S["yfin"][b], 1)
                for b in range(B):
                    ve.wait_ge(S["gq_ps"][b], both(i, b))
                    ve.wait_ge(S["qaT"][b], both(i, b))
                    tt(kqT[b][:, :], qa[b][:, :], AB[b][:, :], ALU.subtract).then_inc(S["qg"][b], 1)
                for b in range(B):
                    ve.wait_ge(S["y_ps"][b], i)
                    ve.wait_ge(S["rq"][b], both(i, b))
                    tt(heads(kn[b]), C[b][:, :].rearrange("p (h e) -> p h e", h=H), bc(s(b, "rq")), ALU.mult)\
                        .then_inc(S["yq"][b], 1)
                for b in range(B):
                    ve.wait_ge(S["ysq"][b], both(i, b))
                    ts(s(b, "yv"), s(b, "ys"), 1.0 / D, 1e-5, ALU.mult, ALU.add).then_inc(S["yv"][b], 1)
                for b in range(B):
                    ve.wait_ge(S["yrs"][b], both(i, b))
                    stt(qs[b][:, :], kn[b][:, :], s(b, "yr"), gate[b][:, :], ALU.mult, ALU.mult).then_inc(S["y3"][b], 1)
                for b in range(B):
                    ve.wait_ge(S["wo_ps"][b], both(i, b))
                    tt(xc[b][:, :], xc[b][:, :], Bk[b][:, :], ALU.add).then_inc(S["x2"][b], 1)
                for b in range(B):
                    ve.wait_ge(S["x2"][b], i)
                route(i, i + NT, xc)
                assert own.n == PER
            own.base, own.n = 0, base1 + PER * NT
            mid_dve_part(1)

            with ve.Fori(NT + 1, 2 * NT + 1) as i:
                for b in range(B):
                    ve.wait_ge(S["ffn_ps"][b], i)
                    ve.wait_ge(xin_in[b], 16 * (i + NT))
                    ve.wait_ge(x2_st[b], 16 * (i - 1))
                    tt(xc[b][:, :], xin[b][:, :], A[b][:, :], ALU.add).then_inc(S["x1"][b], 1)


_INS = ['L0_attn_x', 'L0_attn_Wq', 'L0_attn_Wk', 'L0_attn_Wv', 'L0_attn_Wa', 'L0_attn_ba', 'L0_attn_Wb', 'L0_attn_bb',
        'L0_attn_Wg', 'L0_attn_Wo', 'L0_attn_g_norm', 'L0_ffn_slot_init', 'L0_ffn_slot_scale', 'L0_ffn_w1', 'L0_ffn_b1',
        'L0_ffn_w2', 'L0_ffn_b2', 'L0_ffn_gru_wih', 'L0_ffn_gru_whh', 'L0_ffn_gru_bih', 'L0_ffn_gru_bhh', 'L0_ffn_wv',
        'L0_ffn_bv', 'L0_ffn_wo', 'L0_ffn_bo', 'L0_ffn_tau']
_OUTS = [((B, T, D), 'float32')]


def kernel(**inputs):
    import numpy as _np
    import concourse.bacc as _bacc
    from concourse import mybir as _mybir
    from concourse.bass_utils import run_bass_kernel_spmd as _run

    nc = _bacc.Bacc("TRN2", target_bir_lowering=False, num_devices=1)
    arrays, args = {}, []
    for name in _INS:
        a = _np.ascontiguousarray(inputs[name])
        arrays[f"in_{name}_dram"] = a
        args.append(nc.dram_tensor(f"in_{name}_dram", a.shape, _mybir.dt.from_np(a.dtype), kind="ExternalInput").ap())
    for i, (shape, dtype) in enumerate(_OUTS):
        dt = _mybir.dt.from_np(_np.dtype(dtype))
        args.append(nc.dram_tensor(f"out_{i}_dram", shape, dt, kind="ExternalOutput").ap())
    build(nc, *args)
    r = _run(nc, [arrays], core_ids=[0])
    got = tuple(r.results[0][f"out_{i}_dram"] for i in range(len(_OUTS)))
    return got[0]
```

```python
import numpy as np
import concourse.bass as bass
from concourse import mybir
from concourse.alu_op_type import AluOpType as ALU
from contextlib import ExitStack

f32 = mybir.dt.float32
i32 = mybir.dt.int32
ACT = mybir.ActivationFunctionType
AX = mybir.AxisListType

B, T, D = 2, 4096, 512
H, HD = 16, 32
NS, HID = 64, 256
P = 128
KC = D // P
NT = T // P
CH = 32
NC = P // CH
BIG = -3.0e38


def build(nc, x, Wq, Wk, Wv, Wa, ba, Wb, bb, Wg, Wo, g_norm, slot_init, slot_scale, w1, b1, w2, b2,
          wih, whh, bih, bhh, wv, bv, wo, bo, tau, out):
    ctx = ExitStack()
    with ctx:
        def sb(name, cols, dt=f32):
            return ctx.enter_context(nc.sbuf_tensor(name, [P, cols], dt))

        def sem(name):
            return ctx.enter_context(nc.semaphore(name))

        def sem2(name):
            return [sem(f"{name}{b}") for b in range(B)]

        x2_dram = nc.dram_tensor("x2_scratch", (B, NT, P, D), f32, kind="Internal").ap()
        at_dram = [nc.dram_tensor(f"alphaT_scratch{m}", (NT, P, P), f32, kind="Internal").ap() for m in range(2)]
        n_dram = nc.dram_tensor("n_scratch", (B, H, P, CH), f32, kind="Internal").ap()
        y_dram = nc.dram_tensor("y_scratch", (B, H, P, CH), f32, kind="Internal").ap()
        wih_dram = nc.dram_tensor("wihT_scratch", (6, P, 2 * D), f32, kind="Internal").ap()
        x_t = x.rearrange("b (n p) d -> b n p d", p=P)
        out_t = out.rearrange("b (n p) d -> b n p d", p=P)

        w_kvqg = sb("w_kvqg", KC * 4 * D)
        w_ab = sb("w_ab", KC * 2 * H)
        w_out = sb("w_out", KC * D)
        w1T = sb("w1T", KC * HID)
        w2T = sb("w2T", 2 * NS)
        voT = sb("voT", KC * D)
        gh = sb("gh", 3 * D)
        bih_n = sb("bih_n", D)
        bvo = sb("bvo", D)
        hs = sb("hs", D)
        ident = sb("ident", P)
        ones = sb("ones", P)
        before = sb("before", P)
        upto = sb("upto", P)
        after = sb("after", P)
        chunk = sb("chunk", P)
        tri = sb("tri", CH)
        eye32 = sb("eye32", CH)
        half = sb("half", H)
        ab_bias = sb("ab_bias", 2 * H)
        b2s = sb("b2s", NS)
        itau = sb("itau", 1)
        h_bias = sb("h_bias", 2)
        gcol = sb("gcol", KC)
        sv = sb("sv", D)
        alpha = sb("alpha", B * NS)
        aT_in = sb("aT_in", P)
        aT_out = sb("aT_out", P)
        slotacc = [sb(f"slotacc{b}", KC * NS + NS) for b in range(B)]

        xin = [sb(f"xin{b}", D) for b in range(B)]
        xc = [sb(f"xc{b}", D) for b in range(B)]
        xh = [sb(f"xh{b}", D) for b in range(B)]
        xn = [sb(f"xn{b}", D) for b in range(B)]
        xnT = [sb(f"xnT{b}", D) for b in range(B)]
        kn = [sb(f"kn{b}", D) for b in range(B)]
        qs = [sb(f"qs{b}", D) for b in range(B)]
        scr = [sb(f"scr{b}", D) for b in range(B)]
        vk = [sb(f"vk{b}", 2 * D) for b in range(B)]
        gate = [sb(f"gate{b}", D) for b in range(B)]
        gateh = [sb(f"gateh{b}", D) for b in range(B)]
        dr = [sb(f"dr{b}", D) for b in range(B)]
        dm = [sb(f"dm{b}", H * (HD + 1)) for b in range(B)]
        uw = [sb(f"uw{b}", 2 * D) for b in range(B)]
        kqT = [sb(f"kqT{b}", 2 * D) for b in range(B)]
        qg = [sb(f"qg{b}", 2 * D) for b in range(B)]
        qa = [sb(f"qa{b}", 2 * D) for b in range(B)]
        nn = [sb(f"nn{b}", D) for b in range(B)]
        pk = [sb(f"pk{b}", 2 * D) for b in range(B)]
        yy = [sb(f"yy{b}", D) for b in range(B)]
        ss = [sb(f"ss{b}", D) for b in range(B)]
        nblk = sb("nblk", CH * CH)
        yblk = sb("yblk", CH * CH)
        outer = sb("outer", 256)
        sm = [sb(f"sm{b}", 352) for b in range(B)]

        def heads(t, n=1):
            return t[:, 0:n * D].rearrange("p (h e) -> p h e", h=H)

        def bc(col):
            return col.unsqueeze(2).to_broadcast([P, H, HD])

        def allheads(mask):
            return mask.unsqueeze(1).to_broadcast([P, H, HD])

        SMALL = {}
        at = 0
        for name, n in [("stats", 6), ("mv", 2), ("vs", 1), ("rstd", 1), ("ssk", H), ("rk", H), ("ssq", H),
                        ("rq", H), ("rqh", H), ("ab", 2 * H), ("zi", 2 * H), ("ez", 2 * H), ("ln", H), ("la", H), ("opb", H),
                        ("be", H), ("e4", 4 * H), ("bel", H), ("ys", 1), ("yv", 1), ("yr", 1),
                        ("top", 8), ("negm", 1), ("den", 1), ("rden", 1)]:
            SMALL[name] = (at, n)
            at += n
        lgt = [sb(f"lgt{b}", 3 * NS) for b in range(B)]

        def s(b, name):
            o, n = SMALL[name]
            return sm[b][:, o:o + n]

        D33 = [dm[b][:, :].rearrange("p (h e) -> p h e", h=H) for b in range(B)]
        hT = [kn[b][:, 0:2 * P] for b in range(B)]
        rx = qs

        AB = [ctx.enter_context(nc.psum_tensor(f"AB{b}", [P, 1024], f32)) for b in range(B)]
        C = [ctx.enter_context(nc.psum_tensor(f"C{b}", [P, 512], f32)) for b in range(B)]
        ST = [ctx.enter_context(nc.psum_tensor(f"ST{b}", [P, 512], f32)) for b in range(B)]
        A = [AB[b][:, 0:512] for b in range(B)]
        Bk = [AB[b][:, 512:1024] for b in range(B)]

        ld = sem("ld")
        ring_in = [sem(f"ring_in{r}") for r in range(4)]
        wt_ps, wt_ev = sem("wt_ps"), sem("wt_ev")
        gh_ps, gh_ev = sem("gh_ps"), sem("gh_ev")
        set_pe, set_dve, set_pool, ready = sem("set_pe"), sem("set_dve"), sem("set_pool"), sem("ready")
        dve_own, pool_own, act_own = sem("dve_own"), sem("pool_own"), sem("act_own")
        xin_in, at_in, x2_st, at_st = sem2("xin_in"), sem("at_in"), sem2("x2_st"), sem("at_st")
        each = ("ffn_ps x1 bn xn xT_ps xnT k_ps v_ps ab_ps q_ps g_ps ssk kn v_ev qsq ssq q_ev "
                "zi gate e4 dec_ps draw d33 gram_ps s_ps scp y_ps yq "
                "y3 yT_ps yT x2 rbn rrs rxn rxT_ps rxnT h_ps hT lg_ps top ex al sl_ps sacc").split()
        shared = ("uw qg wo_ps ksq rs rk rq ez ln la be tanh rhsd cum_ps kd kqt kp qaT yv yrs ysq nn gq_ps "
                  "uw_ps y1_ps xhold ghold rqh").split()
        S = {n: sem2(n) for n in each}
        S.update({n: [sem(n)] * B for n in shared})

        def both(i, b):
            return 2 * i - 1 + b

        aT_ps, aT = sem("aT_ps"), sem("aT")
        n_out, n_in, y_out, y_in = sem("n_out"), sem("n_in"), sem("y_out"), sem("y_in")
        eye_set, inv, wih_st, wih_in = sem("eye_set"), sem("inv"), sem("wih_st"), sem("wih_in")
        carriers = sem("carriers")
        mid_pe, mid_act, mid_dve = sem("mid_pe"), sem("mid_act"), sem("mid_dve")

        block = ctx.enter_context(nc.Block())

        def stand_alone(e):
            e.sem_inc(carriers, 1)

        class Own:
            def __init__(self, e, sm_):
                self.e, self.sem, self.base, self.n = e, sm_, 0, 0

            def __call__(self, ins):
                ins.then_inc(self.sem, 1)
                self.n += 1
                self.e.wait_ge(self.sem, self.base + self.n)

        jobs = []
        for j in range(2):
            jobs.append((w1[j * P:(j + 1) * P, 0:D], P, KC, ("w1", j)))
        jobs.append((w2, NS, 2, ("w2", 0)))
        for j in range(4):
            jobs.append((wo[j * P:(j + 1) * P, :], P, KC, ("wo", j)))
        for j in range(12):
            jobs.append((wih[j * P:(j + 1) * P, :], P, KC, ("wih", j)))
        jobs.append((None, P, KC, ("hs", 0)))
        for j in range(12):
            jobs.append((whh[j * P:(j + 1) * P, :], P, KC, ("whh", j)))
        NJ = len(jobs)
        HSJ = [j for j in range(NJ) if jobs[j][3][0] == "hs"][0]
        rings = [kn[0], kn[1], qs[0], qs[1]]
        tps = [A[0], A[1], Bk[0], Bk[1]]
        woT = vk[0]
        hsT = gate[0]
        whh_ring = [gate[1], dr[0]]

        wih_region = [uw[0], uw[1], kqT[0], kqT[1], qg[0], qg[1]]

        def wihT_at(k, j):
            n = 3 * k + j
            return wih_region[n // 2][:, (n % 2) * D:(n % 2 + 1) * D]

        def woT_at(k):
            return (vk[0], vk[1])[k // 2][:, (k % 2) * D:(k % 2 + 1) * D]

        def dest(j):
            kind, r = jobs[j][3]
            if kind == "w1":
                return w1T[:, :].rearrange("p (k n) -> p k n", k=KC)[:, :, r * P:(r + 1) * P]
            if kind == "w2":
                return w2T[:, :].rearrange("p (k n) -> p k n", k=2)
            if kind == "hs":
                return hsT[:, :].rearrange("p (k n) -> p k n", k=KC)
            if kind == "whh":
                return whh_ring[r % 2][:, :].rearrange("p (k n) -> p k n", k=KC)
            return None

        LD = 16 * 20
        b1c = ss[0]
        wvn = [pk[k // 2][:, (k % 2) * D:(k % 2 + 1) * D] for k in range(KC)]
        w1b = [nblk[:, 0:D], nblk[:, D:2 * D]]
        bhh_t, bih_t = (yblk, xnT[0]), (qa[1], xnT[1])
        bv_c, bo_t = ss[1], yy[1]
        mean_t, prod_t = scr[0], scr[1]
        ssc = sm[0][:, 0:1]
        taut = sm[0][:, 1:2]

        def ring_user(j, n):
            seen = 0
            for jj in range(NJ):
                if jobs[jj][0] is not None:
                    if seen == n - 4:
                        return jj + 1
                    seen += 1

        def ring_no(j):
            return sum(1 for jj in range(j) if jobs[jj][0] is not None)

        def slot_sum_cols(b):
            return AB[b][:, 0:KC * NS + NS]

        def gh_part(pe, mm, r, j):
            pe.wait_ge(wt_ev, HSJ + 2 + r)
            if r >= 2:
                pe.wait_ge(gh_ev, r - 1)
            for k in range(KC):
                last = mm(C[r % 2][:, 0:P], hsT[:, k * P:(k + 1) * P], whh_ring[r % 2][:, k * P:(k + 1) * P],
                          start=(k == 0), stop=(k == KC - 1))
            last.then_inc(gh_ps, 1)

        giT, gr, gz, gn, ht, hTT = kn[0], qs[0], qs[1], gate[0], gate[1], kn[1]
        NMID = 4

        def mid(e, m):
            o_pe, o_act, o_dve = 3 * m, 4 * m, 7 * m
            if e is nc.tensor:
                mm, tr = nc.tensor.matmul, nc.tensor.transpose
                e.wait_ge(mid_dve, o_dve + 1)
                if m == 1:
                    e.wait_ge(wih_in, 16 * 6)
                for j, dst in enumerate((A[0], A[1], C[0])):
                    for k in range(KC):
                        last = mm(dst[:, :], giT[:, k * P:(k + 1) * P], wihT_at(k, j),
                                  start=(k == 0), stop=(k == KC - 1))
                last.then_inc(mid_pe, 1)
                e.wait_ge(mid_dve, o_dve + 6)
                e.wait_ge(aT, NT * (m + 1))
                for k in range(KC):
                    last = tr(Bk[0][:, k * P:(k + 1) * P], ht[:, k * P:(k + 1) * P], ident[:, :])
                last.then_inc(mid_pe, 1)
                e.wait_ge(mid_act, o_act + 4)
                for k in range(KC):
                    last = mm(Bk[1][:, :], hTT[:, k * P:(k + 1) * P], voT[:, k * D:(k + 1) * D],
                              start=(k == 0), stop=(k == KC - 1))
                last.then_inc(mid_pe, 1)
                e.wait_ge(mid_dve, o_dve + 7)
            elif e is nc.scalar:
                act = nc.scalar.activation
                e.wait_ge(mid_dve, o_dve + 2)
                act(gr[:, :], gr[:, :], ACT.Sigmoid).then_inc(mid_act, 1)
                e.wait_ge(mid_dve, o_dve + 3)
                act(gz[:, :], gz[:, :], ACT.Sigmoid).then_inc(mid_act, 1)
                e.wait_ge(mid_dve, o_dve + 4)
                act(gn[:, :], gn[:, :], ACT.Tanh).then_inc(mid_act, 1)
                e.wait_ge(mid_pe, o_pe + 2)
                act(hTT[:, :], Bk[0][:, :], ACT.Copy).then_inc(mid_act, 1)

        @block.sync
        def _(sp):
            def load(dst, src):
                sp.dma_start(dst, src, allow_slow_non_contiguous=True).then_inc(ld, 16)
            load(hs[0:NS, :], slot_init)
            load(hs[NS:P, :], slot_init)
            load(ssc[0:NS, :], slot_scale)
            load(ssc[NS:P, :], slot_scale)
            load(taut, tau.partition_broadcast(P))
            load(b1c[:, 0:2], b1.rearrange("(j p) -> p j", p=P))
            load(b2s[:, :], b2.partition_broadcast(P))
            load(bv_c[:, 0:KC], bv.rearrange("(j p) -> p j", p=P))
            load(bo_t[:, :], bo.partition_broadcast(P))
            load(ab_bias[:, 0:H], ba.partition_broadcast(P))
            load(ab_bias[:, H:2 * H], bb.partition_broadcast(P))
            load(gcol[:, :], g_norm.rearrange("(j p) -> p j", p=P))
            load(bih_t[0][:, :], bih[0:2 * D].partition_broadcast(P))
            load(bih_t[1][:, :], bih[2 * D:3 * D].partition_broadcast(P))
            load(bhh_t[0][:, :], bhh[0:2 * D].partition_broadcast(P))
            load(bhh_t[1][:, :], bhh[2 * D:3 * D].partition_broadcast(P))
            for j in range(2):
                load(pk[j][:, :].rearrange("p (k n) -> p k n", k=2),
                     wv[2 * j * P:2 * (j + 1) * P, :].rearrange("(k p) n -> p k n", p=P))
            load(nblk[:, :].rearrange("p (k n) -> p k n", k=2),
                 w1[:, D:2 * D].rearrange("(k p) n -> p k n", p=P))
            load(w_out[:, :].rearrange("p (k n) -> p k n", k=KC), Wo.rearrange("(k p) n -> p k n", p=P))
            loaded = 0
            for j in range(NJ):
                if jobs[j][0] is None:
                    continue
                if loaded >= 4:
                    sp.wait_ge(wt_ps, ring_user(j, loaded))
                src, rows, cols, _ = jobs[j]
                sp.dma_start(rings[loaded % 4][0:rows, 0:cols * P], src).then_inc(ring_in[loaded % 4], 16)
                loaded += 1
            w4 = w_kvqg[:, :].rearrange("p (k m n) -> p k m n", k=KC, m=4)
            for m, w in enumerate((Wk, Wv, Wq, Wg)):
                load(w4[:, :, m, :], w.rearrange("(k p) n -> p k n", p=P))
            wab = w_ab[:, :].rearrange("p (k m n) -> p k m n", k=KC, m=2)
            for m, w in enumerate((Wa, Wb)):
                load(wab[:, :, m, :], w.rearrange("(k p) n -> p k n", p=P))

            def load_x(src, n, i, free):
                for b in range(B):
                    if free is not None:
                        sp.wait_ge(free[b], i)
                    sp.dma_start(xin[b][:, :], src[b, bass.ds(n, 1), :, :].rearrange("o p d -> (o p) d"))\
                        .then_inc(xin_in[b], 16)

            def store_at(m, n, count):
                sp.wait_ge(aT, count)
                sp.dma_start(at_dram[m][bass.ds(n, 1), :, :].rearrange("o p d -> (o p) d"), aT_out[:, :])\
                    .then_inc(at_st, 16)

            sp.wait_ge(wt_ev, HSJ)
            for r in range(6):
                sp.dma_start(wih_dram[r, :, :], wih_region[r][:, :]).then_inc(wih_st, 16)

            sp.wait_ge(ready, 1)
            for b in range(B):
                sp.dma_start(xin[b][:, :], x_t[b, 0, :, :]).then_inc(xin_in[b], 16)
            with sp.Fori(1, NT) as i:
                load_x(x_t, i, i, S["rxn"])
                store_at(0, i - 1, i)
            store_at(0, NT - 1, NT)
            for b in range(B):
                sp.wait_ge(S["rxn"][b], NT)
            sp.wait_ge(at_st, 16 * NT)

            def load_at(m, n):
                sp.dma_start(aT_in[:, :], at_dram[m][bass.ds(n, 1), :, :].rearrange("o p d -> (o p) d"))\
                    .then_inc(at_in, 16)

            def prefetch(m):
                load_x(x_t, m, m, S["x1"])
                load_at(0, m)

            def step_sp(n, j, m, more):
                if n is not None:
                    for b in range(B):
                        sp.wait_ge(S["nn"][b], both(n, b))
                        sp.dma_start(n_dram[b, :, :, :].rearrange("h p t -> p h t"), heads(nn[b])).then_inc(n_out, 16)
                    sp.wait_ge(n_out, 32 * n)
                    sp.dma_start(nblk[:, :], n_dram.rearrange("b h (c s) t -> (b h c) (s t)", s=CH)).then_inc(n_in, 16)
                    sp.wait_ge(inv, n)
                    sp.dma_start(y_dram.rearrange("b h (c s) t -> (b h c) (s t)", s=CH), yblk[:, :]).then_inc(y_out, 16)
                    sp.wait_ge(y_out, 16 * n)
                    for b in range(B):
                        sp.dma_start(heads(yy[b]), y_dram[b, :, :, :].rearrange("h p t -> p h t")).then_inc(y_in, 16)
                if more:
                    prefetch(m)
                if j is not None:
                    store_at(1, j - 1, j + NT)
            for b in range(B):
                sp.dma_start(xin[b][:, :], x_t[b, 0, :, :]).then_inc(xin_in[b], 16)
            load_at(0, 0)
            prefetch(1)
            step_sp(1, None, 2, True)
            with sp.Fori(1, NT - 2) as i:
                step_sp(i + 1, i, i + 2, True)
            step_sp(NT - 1, NT - 2, NT, False)
            step_sp(NT, NT - 1, None, False)
            step_sp(None, NT, None, False)
            for b in range(B):
                sp.wait_ge(S["y_ps"][b], NT)
            sp.wait_ge(wih_st, 16 * 6)
            for r in range(6):
                sp.dma_start(wih_region[r][:, :], wih_dram[r, :, :]).then_inc(wih_in, 16)
            for b in range(B):
                sp.wait_ge(x2_st[b], 16 * NT)
            sp.wait_ge(at_st, 32 * NT)

            for b in range(B):
                sp.dma_start(xin[b][:, :], x2_dram[b, 0, :, :]).then_inc(xin_in[b], 16)
            sp.dma_start(aT_in[:, :], at_dram[1][0, :, :]).then_inc(at_in, 16)
            with sp.Fori(1, NT) as i:
                load_x(x2_dram, i, i + NT, S["x1"])
                load_at(1, i)
                for b in range(B):
                    sp.dma_start(out_t[b, bass.ds(i - 1, 1), :, :].rearrange("o p d -> (o p) d"), xc[b][:, :])\
                        .then_inc(x2_st[b], 16)
            for b in range(B):
                sp.wait_ge(S["x1"][b], 2 * NT)
                sp.dma_start(out_t[b, NT - 1, :, :], xc[b][:, :]).then_inc(x2_st[b], 16)
            for b in range(B):
                sp.wait_ge(x2_st[b], 32 * NT)

        @block.tensor
        def _(pe):
            mm, tr = nc.tensor.matmul, nc.tensor.transpose
            pe.wait_ge(set_pool, 1)
            for j in range(NJ):
                src, rows, cols, (kind, r) = jobs[j]
                if kind == "hs":
                    pe.wait_ge(set_dve, 1)
                    buf = hs
                else:
                    n = ring_no(j)
                    pe.wait_ge(ring_in[n % 4], 16 * (n // 4 + 1))
                    buf = rings[n % 4]
                if j >= 4:
                    pe.wait_ge(wt_ev, j - 3)
                for k in range(cols):
                    last = tr(tps[j % 4][:, k * rows:(k + 1) * rows], buf[0:rows, k * P:(k + 1) * P],
                              ident[0:rows, 0:rows])
                last.then_inc(wt_ps, 1)
                if kind == "whh" and r >= 1:
                    gh_part(pe, mm, r - 1, j)
            gh_part(pe, mm, 11, NJ)
            pe.wait_ge(set_dve, 2)
            pe.wait_ge(gh_ev, 12)
            mm(C[0][:, :], aT_in[0:NS, :], hs[0:NS, :], start=True, stop=True).then_inc(set_pe, 1)
            for k in range(KC):
                if k >= 2:
                    pe.wait_ge(set_dve, 1 + k)
                for e in range(KC):
                    last = mm(ST[k % 2][:, :], wvn[e][:, k * P:(k + 1) * P], woT_at(e), start=(e == 0), stop=(e == KC - 1))
                last.then_inc(set_pe, 1)
            pe.wait_ge(set_dve, 7)
            for e in range(KC):
                last = mm(C[0][:, :], xin[0][:, e * P:(e + 1) * P], woT_at(e), start=(e == 0), stop=(e == KC - 1))
            last.then_inc(set_pe, 1)

            def transpose_to(dst, src):
                for k in range(KC):
                    last = tr(dst[:, k * P:(k + 1) * P], src[:, k * P:(k + 1) * P], ident[:, :])
                return last

            def route_xT(j, n):
                for b in range(B):
                    pe.wait_ge(S["rxn"][b], n)
                    if j is not None:
                        pe.wait_ge(S["yT"][b], j)
                    else:
                        pe.wait_ge(S["sacc"][b], n - 1)
                    transpose_to(A[b], rx[b]).then_inc(S["rxT_ps"][b], 1)

            def route_hidden(j, n):
                for b in range(B):
                    pe.wait_ge(S["rxnT"][b], n)
                    if j is not None:
                        pe.wait_ge(S["x2"][b], j)
                    elif b == 0:
                        pe.wait_ge(aT, n - 1)
                    for j2 in range(2):
                        for k in range(KC):
                            last = mm(Bk[b][:, j2 * P:(j2 + 1) * P], w1T[:, k * HID + j2 * P:k * HID + (j2 + 1) * P],
                                      xnT[b][:, k * P:(k + 1) * P], start=(k == 0), stop=(k == KC - 1))
                    last.then_inc(S["h_ps"][b], 1)

            def route_logits(n):
                for b in range(B):
                    pe.wait_ge(S["hT"][b], n)
                    for j2 in range(2):
                        last = mm(Bk[b][:, HID:HID + NS], hT[b][:, j2 * P:(j2 + 1) * P], w2T[:, j2 * NS:(j2 + 1) * NS],
                                  start=(j2 == 0), stop=(j2 == 1))
                    last.then_inc(S["lg_ps"][b], 1)

            def route_slots(n):
                for b in range(B):
                    pe.wait_ge(S["al"][b], n)
                    for k in range(KC):
                        mm(A[b][:, k * NS:(k + 1) * NS], rx[b][:, k * P:(k + 1) * P], alpha[:, b * NS:(b + 1) * NS],
                           start=True, stop=True)
                    mm(A[b][:, KC * NS:(KC + 1) * NS], ones[:, :], alpha[:, b * NS:(b + 1) * NS], start=True, stop=True)\
                        .then_inc(S["sl_ps"][b], 1)
                tr(Bk[0][:, 3 * P:4 * P], alpha[:, :], ident[:, :]).then_inc(aT_ps, 1)

            pe.wait_ge(ready, 1)
            with pe.Fori(1, NT + 1) as i:
                route_xT(None, i)
                route_hidden(None, i)
                route_logits(i)
                route_slots(i)
            mid(pe, 0)

            def h32(t, c, h, w, o, n):
                return t[CH * c:CH * (c + 1), h * w + o:h * w + o + n]

            def cells(dst, dw, lhs, lw, lo, rhs, rw, ro, n):
                for h in range(H):
                    for c in range(NC):
                        last = mm(h32(dst, c, h, dw, 0, n), h32(lhs, c, h, lw, lo, CH), h32(rhs, c, h, rw, ro, n),
                                  start=True, stop=True)
                return last

            def project(b, m, dst):
                for k in range(KC):
                    last = mm(dst, xnT[b][:, k * P:(k + 1) * P], w_kvqg[:, (k * 4 + m) * D:(k * 4 + m + 1) * D],
                              start=(k == 0), stop=(k == KC - 1))
                return last

            def first_ffn(m, free, count):
                for b in range(B):
                    if free is not None:
                        pe.wait_ge(S[free][b], count)
                    pe.wait_ge(at_in, 16 * m)
                    mm(C[b][:, :], aT_in[b * NS:(b + 1) * NS, :], sv[b * NS:(b + 1) * NS, :], start=True, stop=True)\
                        .then_inc(S["ffn_ps"][b], 1)

            def first_xT(m):
                for b in range(B):
                    pe.wait_ge(S["xn"][b], m)
                    transpose_to(C[b], xn[b]).then_inc(S["xT_ps"][b], 1)

            def step_pe(n, j, m):
                if n is not None:
                    for b in range(B):
                        pe.wait_ge(S["xnT"][b], n)
                        project(b, 0, C[b][:, :]).then_inc(S["k_ps"][b], 1)
                        if j is not None:
                            pe.wait_ge(S["sacc"][b], j + NT - 1)
                        for k in range(KC):
                            last = mm(A[b][:, 0:2 * H], xnT[b][:, k * P:(k + 1) * P], w_ab[:, k * 2 * H:(k + 1) * 2 * H],
                                      start=(k == 0), stop=(k == KC - 1))
                        last.then_inc(S["ab_ps"][b], 1)
                if j is not None:
                    pe.wait_ge(aT, j + NT - 1)
                    pe.wait_ge(y_in, 32 * j)
                    for b in range(B):
                        pe.wait_ge(S["kp"][b], both(j, b))
                        if n is not None:
                            pe.wait_ge(S["zi"][b], n)
                        else:
                            pe.wait_ge(S["sacc"][b], j + NT - 1)
                        stand_alone(pe)
                        cells(AB[b], 2 * HD, yy[b], HD, 0, vk[b], 2 * HD, 0, 2 * HD).then_inc(S["uw_ps"][b], 1)
                if n is not None:
                    for b in range(B):
                        pe.wait_ge(S["kn"][b], n)
                        project(b, 2, C[b][:, :]).then_inc(S["q_ps"][b], 1)
                if j is not None:
                    for b in range(B):
                        pe.wait_ge(S["uw"][b], both(j, b))
                        pe.wait_ge(S["kd"][b], both(j, b))
                        stand_alone(pe)
                        cells(AB[b], 2 * HD, uw[b], 2 * HD, HD, pk[b], 2 * HD, 0, 2 * HD).then_inc(S["gq_ps"][b], 1)
                        pe.wait_ge(S["scp"][b], NC * (j - 1) + 1)
                        stand_alone(pe)
                        for c in range(NC):
                            o = CH * ((c + 1) % NC)
                            for h in range(H):
                                mm(ST[b][o:o + CH, h * HD:(h + 1) * HD], h32(pk[b], c, h, 2 * HD, HD, HD),
                                   h32(uw[b], c, h, 2 * HD, 0, HD), start=(h == 0), stop=False, skip_group_check=True)
                if n is not None:
                    for b in range(B):
                        pe.wait_ge(S["q_ev"][b], n)
                        project(b, 1, C[b][:, :]).then_inc(S["v_ps"][b], 1)
                    for b in range(B):
                        pe.wait_ge(S["la"][b], both(n, b))
                        if j is not None:
                            pe.wait_ge(S["qg"][b], both(j, b))
                        for m2, mask in enumerate((before, upto, after, chunk)):
                            last = mm(A[b][:, m2 * H:(m2 + 1) * H], mask[:, :], s(b, "la"), start=True, stop=True)
                        last.then_inc(S["cum_ps"][b], 1)
                        pe.wait_ge(S["v_ev"][b], n)
                        project(b, 3, C[b][:, :]).then_inc(S["g_ps"][b], 1)
                    for b in range(B):
                        pe.wait_ge(S["rhsd"][b], both(n, b))
                        mm(Bk[b][:, :], after[:, :], dr[b][:, :], start=True, stop=True).then_inc(S["dec_ps"][b], 1)
                if j is not None:
                    for b in range(B):
                        if n is not None:
                            pe.wait_ge(S["gate"][b], n)
                        stand_alone(pe)
                        for h in range(H):
                            for c in range(NC):
                                last = mm(h32(C[b], c, h, HD, 0, HD), h32(pk[b], c, h, 2 * HD, 0, CH),
                                          h32(uw[b], c, h, 2 * HD, 0, HD), start=(h == 0), stop=False, skip_group_check=True)
                        last.then_inc(S["y1_ps"][b], 1)
                if n is not None:
                    for b in range(B):
                        pe.wait_ge(S["kqt"][b], both(n, b))
                        pe.wait_ge(S["e4"][b], n)
                        pe.wait_ge(S["draw"][b], n)
                        stand_alone(pe)
                        cells(AB[b], 2 * HD, kqT[b], 2 * HD, 0, kqT[b], 2 * HD, 0, 2 * HD).then_inc(S["gram_ps"][b], 1)
                if j is not None:
                    for c in range(NC):
                        for b in range(B):
                            if c == 0:
                                pe.wait_ge(S["qg"][b], both(j, b))
                            pe.wait_ge(S["scp"][b], NC * (j - 1) + c + 1)
                            stand_alone(pe)
                            o = CH * ((c + 1) % NC)
                            for h in range(H):
                                last = mm(ST[b][o:o + CH, h * HD:(h + 1) * HD], h32(qg[b], c, h, 2 * HD, HD, HD),
                                          h32(ss[b], c, h, HD, 0, HD), start=False, stop=True, skip_group_check=True)
                            last.then_inc(S["s_ps"][b], 1)
                            for h in range(H):
                                last = mm(h32(C[b], c, h, HD, 0, HD), h32(qg[b], c, h, 2 * HD, 0, CH),
                                          h32(ss[b], c, h, HD, 0, HD), start=False, stop=True, skip_group_check=True)
                            if c == NC - 1:
                                last.then_inc(S["y_ps"][b], 1)
                    for b in range(B):
                        if n is not None:
                            pe.wait_ge(S["nn"][b], both(n, b))
                        pe.wait_ge(S["y3"][b], j)
                        transpose_to(A[b], qs[b]).then_inc(S["yT_ps"][b], 1)
                    for b in range(B):
                        pe.wait_ge(S["yT"][b], j)
                        for k in range(KC):
                            last = mm(Bk[b][:, :], xnT[b][:, k * P:(k + 1) * P], w_out[:, k * D:(k + 1) * D],
                                      start=(k == 0), stop=(k == KC - 1))
                        last.then_inc(S["wo_ps"][b], 1)
                if m is not None:
                    first_ffn(m, "gate" if j is None else "yq", n if j is None else j)
                if j is not None:
                    route_xT(j, j + NT)
                    route_hidden(j, j + NT)
                if m is not None:
                    first_xT(m)
                if j is not None:
                    route_logits(j + NT)
                    route_slots(j + NT)

            first_ffn(1, None, 0)
            first_xT(1)
            step_pe(1, None, 2)
            with pe.Fori(1, NT - 1) as i:
                step_pe(i + 1, i, i + 2)
            step_pe(NT, NT - 1, None)
            step_pe(None, NT, None)
            mid(pe, 1)

            with pe.Fori(NT + 1, 2 * NT + 1) as i:
                for b in range(B):
                    pe.wait_ge(at_in, 16 * i)
                    pe.wait_ge(S["x1"][b], i - 1)
                    mm(C[b][:, :], aT_in[b * NS:(b + 1) * NS, :], sv[b * NS:(b + 1) * NS, :], start=True, stop=True)\
                        .then_inc(S["ffn_ps"][b], 1)

        @block.scalar
        def _(sc):
            act = nc.scalar.activation
            own = Own(sc, act_own)
            for j in range(0, NJ):
                src, rows, cols, (kind, r) = jobs[j]
                sc.wait_ge(wt_ps, j + 1)
                if kind == "whh" and r >= 2:
                    sc.wait_ge(gh_ps, r - 1)
                view = tps[j % 4][:, 0:cols * rows].rearrange("p (k n) -> p k n", k=cols)
                if kind in ("wo", "wih"):
                    for k in range(KC):
                        to = woT_at(k)[:, r * P:(r + 1) * P] if kind == "wo" else wihT_at(k, r // 4)[:, r % 4 * P:(r % 4 + 1) * P]
                        last = act(to, view[:, k, :], ACT.Copy)
                    last.then_inc(wt_ev, 1)
                else:
                    act(dest(j), view, ACT.Copy).then_inc(wt_ev, 1)

            def move(dst, src, n, ps, done):
                sc.wait_ge(ps, n)
                act(dst, src, ACT.Copy).then_inc(done, 1)

            def route_moves(n):
                for b in range(B):
                    move(xnT[b][:, :], A[b][:, :], n, S["rxT_ps"][b], S["rxnT"][b])
                for b in range(B):
                    sc.wait_ge(S["h_ps"][b], n)
                    for j in range(2):
                        last = act(hT[b][:, j * P:(j + 1) * P], Bk[b][:, j * P:(j + 1) * P], ACT.Gelu, bias=h_bias[:, j:j + 1])
                    last.then_inc(S["hT"][b], 1)

            def route_exp(n):
                for b in range(B):
                    sc.wait_ge(S["top"][b], n)
                    act(lgt[b][:, 2 * NS:3 * NS], lgt[b][:, 0:NS], ACT.Exp, bias=s(b, "negm")).then_inc(S["ex"][b], 1)
                sc.wait_ge(aT_ps, n)
                sc.wait_ge(at_st, 16 * (n - 1))
                act(aT_out[:, :], Bk[0][:, 3 * P:4 * P], ACT.Copy).then_inc(aT, 1)

            sc.wait_ge(ready, 1)
            with sc.Fori(1, NT + 1) as i:
                route_moves(i)
                route_exp(i)
            mid(sc, 0)

            def move_first(m):
                for b in range(B):
                    move(xnT[b][:, :], C[b][:, :], m, S["xT_ps"][b], S["xnT"][b])

            def move_state(j, b, c):
                sc.wait_ge(S["s_ps"][b], NC * (j - 1) + c)
                act(ss[b][CH * c:CH * (c + 1), :], ST[b][CH * c:CH * (c + 1), :], ACT.Copy).then_inc(S["scp"][b], 1)

            def step_act(n, j, m):
                if j is not None:
                    for b in range(B):
                        move_state(j, b, 0)
                if n is not None:
                    for b in range(B):
                        sc.wait_ge(S["k_ps"][b], n)
                        act(scr[b][:, :], C[b][:, :], ACT.Square).then_inc(S["ksq"][b], 1)
                    for b in range(B):
                        sc.wait_ge(S["zi"][b], n)
                        act(s(b, "ez"), s(b, "zi"), ACT.Exp).then_inc(S["ez"][b], 1)
                if j is not None:
                    for b in range(B):
                        move(uw[b][:, 0:2 * D], AB[b][:, :], both(j, b), S["uw_ps"][b], S["uw"][b])
                if n is not None:
                    for b in range(B):
                        sc.wait_ge(S["q_ps"][b], n)
                        act(qs[b][:, :], C[b][:, :], ACT.Copy)
                        sc.wait_ge(S["ssk"][b], n)
                        act(scr[b][:, :], C[b][:, :], ACT.Square).then_inc(S["q_ev"][b], 1)
                    for b in range(B):
                        sc.wait_ge(S["ez"][b], both(n, b))
                        act(s(b, "ln"), s(b, "ez")[:, 0:H], ACT.Ln, bias=1.0).then_inc(S["ln"][b], 1)
                    for b in range(B):
                        move(heads(vk[b], 2)[:, :, 0:HD], C[b][:, :].rearrange("p (h e) -> p h e", h=H), n,
                             S["v_ps"][b], S["v_ev"][b])
                    for b in range(B):
                        sc.wait_ge(S["cum_ps"][b], both(n, b))
                        act(s(b, "e4"), A[b][:, 0:4 * H], ACT.Exp).then_inc(S["e4"][b], 1)
                    for b in range(B):
                        sc.wait_ge(S["g_ps"][b], n)
                        sc.wait_ge(S["ssq"][b], n)
                        act(scr[b][:, :], C[b][:, :], ACT.Tanh, scale=0.5).then_inc(S["tanh"][b], 1)
                    for b in range(B):
                        sc.wait_ge(S["dec_ps"][b], n)
                        act(dr[b][:, :], Bk[b][:, :], ACT.Exp).then_inc(S["draw"][b], 1)
                if j is not None:
                    for c in range(1, NC):
                        for b in range(B):
                            move_state(j, b, c)
                    for b in range(B):
                        sc.wait_ge(S["yq"][b], j)
                        act(scr[b][:, :], kn[b][:, :], ACT.Square, accum_out=s(b, "ys")).then_inc(S["ysq"][b], 1)
                    for b in range(B):
                        move(xnT[b][:, :], A[b][:, :], j, S["yT_ps"][b], S["yT"][b])
                    for b in range(B):
                        sc.wait_ge(S["x2"][b], j)
                        sc.dma_start(x2_dram[b, bass.ds(j - 1, 1), :, :].rearrange("o p d -> (o p) d"), xh[b][:, :])\
                            .then_inc(x2_st[b], 16)
                    route_moves(j + NT)
                if m is not None:
                    move_first(m)
                if j is not None:
                    route_exp(j + NT)

            sc.wait_ge(wih_st, 16 * 6)
            move_first(1)
            step_act(1, None, 2)
            with sc.Fori(1, NT - 1) as i:
                step_act(i + 1, i, i + 2)
            step_act(NT, NT - 1, None)
            step_act(None, NT, None)
            mid(sc, 1)

        @block.gpsimd
        def _(pl):
            g = nc.gpsimd
            own = Own(pl, pool_own)
            own(g.memset(ident[:, :], 0.0))
            g.affine_select(out=ident[:, :], in_=ident[:, :], compare_op=ALU.not_equal, fill=1.0, base=0,
                            pattern=[[-1, P]], channel_multiplier=1).then_inc(set_pool, 1)
            g.iota(qa[0][:, 0:P].bitcast(i32), pattern=[[0, P]], base=0, channel_multiplier=1)
            g.iota(gateh[0][:, 0:P].bitcast(i32), pattern=[[1, P]], base=0, channel_multiplier=0).then_inc(set_pool, 1)

            def power(dst, a, n):
                return g.tensor_tensor(dst, a, half[:, 0:n], ALU.pow)

            def rstd(b, n, bn, rs):
                pl.wait_ge(S[bn][b], n)
                stand_alone(pl)
                own(g.tensor_scalar(s(b, "vs"), s(b, "mv")[:, 1:2], 1e-5, None, ALU.add))
                power(s(b, "rstd"), s(b, "vs"), 1).then_inc(S[rs][b], 1)

            pl.wait_ge(ready, 1)
            with pl.Fori(1, NT + 1) as i:
                own.base, own.n = 1 + 2 * (i - 1), 0
                for b in range(B):
                    rstd(b, i, "rbn", "rrs")
                assert own.n == 2
            own.base, own.n = 0, 1 + 2 * NT

            def hold(dst, src):
                return g.tensor_copy(dst, src)

            def step_pool(n, j, m):
                if n is not None:
                    pl.wait_ge(y_out, 16 * (n - 1))
                    stand_alone(pl)
                    own(g.memset(yblk[:, :], 0.0))
                    stand_alone(pl)
                    g.memset(yblk[:, 0:CH * CH:CH + 1], 1.0).then_inc(eye_set, 1)
                    for b in range(B):
                        pl.wait_ge(S["ssk"][b], n)
                        power(s(b, "rk"), s(b, "ssk"), H).then_inc(S["rk"][b], 1)
                    for b in range(B):
                        pl.wait_ge(S["ssq"][b], n)
                        power(s(b, "rq"), s(b, "ssq"), H).then_inc(S["rq"][b], 1)
                    for b in range(B):
                        pl.wait_ge(S["la"][b], both(n, b))
                        g.tensor_tensor(heads(dr[b]), bc(s(b, "la")), allheads(tri[:, :]), ALU.mult).then_inc(S["rhsd"][b], 1)
                    for b in range(B):
                        if j is not None:
                            pl.wait_ge(S["qg"][b], both(j, b))
                        pl.wait_ge(S["e4"][b], n)
                        g.tensor_tensor(heads(qa[b], 2)[:, :, HD:2 * HD], bc(s(b, "e4")[:, 3 * H:4 * H]),
                                        allheads(eye32[:, :]), ALU.mult).then_inc(S["qaT"][b], 1)
                    for b in range(B):
                        pl.wait_ge(S["draw"][b], n)
                        own(g.tensor_tensor(heads(dr[b]), heads(dr[b]), allheads(tri[:, :]), ALU.mult))
                        pl.wait_ge(S["be"][b], both(n, b))
                        stand_alone(pl)
                        g.memset(D33[b][:, :, 0:1], 0.0)
                        g.tensor_tensor(D33[b][:, :, 1:HD + 1], heads(dr[b]), bc(s(b, "be")), ALU.mult).then_inc(S["d33"][b], 1)
                    for b in range(B):
                        own(g.tensor_tensor(s(b, "bel"), s(b, "be"), s(b, "e4")[:, 2 * H:3 * H], ALU.mult))
                        if j is not None:
                            pl.wait_ge(S["y1_ps"][b], both(j, b))
                        g.tensor_tensor(heads(pk[b], 2)[:, :, HD:2 * HD], heads(kn[b]), bc(s(b, "bel")), ALU.mult)\
                            .then_inc(S["kd"][b], 1)
                    for b in range(B):
                        if j is not None:
                            pl.wait_ge(S["yq"][b], j)
                            stand_alone(pl)
                        hold(s(b, "rqh"), s(b, "rq")).then_inc(S["rqh"][b], 1)
                if j is not None:
                    for b in range(B):
                        pl.wait_ge(S["yv"][b], both(j, b))
                        power(s(b, "yr"), s(b, "yv"), 1).then_inc(S["yrs"][b], 1)
                if n is not None:
                    for b in range(B):
                        if j is not None:
                            pl.wait_ge(S["y3"][b], j)
                        pl.wait_ge(S["gate"][b], n)
                        stand_alone(pl)
                        hold(gateh[b][:, :], gate[b][:, :]).then_inc(S["ghold"][b], 1)
                if j is not None:
                    for b in range(B):
                        rstd(b, j + NT, "rbn", "rrs")
                if n is not None:
                    for b in range(B):
                        if j is not None:
                            pl.wait_ge(x2_st[b], 16 * j)
                            pl.wait_ge(S["rxn"][b], j + NT)
                        stand_alone(pl)
                        hold(xh[b][:, :], xc[b][:, :]).then_inc(S["xhold"][b], 1)
                if m is not None:
                    for b in range(B):
                        rstd(b, m, "bn", "rs")

            for b in range(B):
                rstd(b, 1, "bn", "rs")
            step_pool(1, None, 2)
            PER = 1 + 2 * 4
            base = own.n
            with pl.Fori(1, NT - 1) as i:
                own.base, own.n = base + PER * (i - 1), 0
                step_pool(i + 1, i, i + 2)
                assert own.n == PER
            own.base, own.n = 0, base + PER * (NT - 2)
            step_pool(NT, NT - 1, None)
            step_pool(None, NT, None)

        @block.vector
        def _(ve):
            v = nc.vector
            tt, ts, stt = v.tensor_tensor, v.tensor_scalar, v.scalar_tensor_tensor
            own = Own(ve, dve_own)
            ve.wait_ge(ld, LD)
            own(ts(hs[:, :], hs[:, :], ssc, None, ALU.mult))
            own(v.memset(aT_in[:, :], 1.0 / NS))
            ve.nop().then_inc(set_dve, 1)
            v.memset(ones[:, :], 1.0)
            v.memset(half[:, :], -0.5)
            for b in range(B):
                v.memset(ST[b][:, :], 0.0)
                own(v.memset(slotacc[b][:, :], 0.0))
            own(stt(sm[0][:, 2:3], taut, -1.0, taut, ALU.mult, ALU.max))
            own(ts(sm[0][:, 3:4], sm[0][:, 2:3], 0.1, None, ALU.add))
            own(v.reciprocal(itau[:, :], sm[0][:, 3:4]))
            own(ts(b2s[:, :], b2s[:, :], itau[:, :], None, ALU.mult))
            for k in range(KC):
                own(ts(w_out[:, k * D:(k + 1) * D], w_out[:, k * D:(k + 1) * D], gcol[:, k:k + 1], 0.5, ALU.mult, ALU.mult))
            own(tt(gh[:, 0:2 * D], bih_t[0][:, :], bhh_t[0][:, :], ALU.add))
            own(v.tensor_copy(gh[:, 2 * D:3 * D], bhh_t[1][:, :]))
            own(v.tensor_copy(bih_n[:, :], bih_t[1][:, :]))
            for k in range(KC):
                own(ts(xin[0][:, k * P:(k + 1) * P], ones[:, :], bv_c[:, k:k + 1], None, ALU.mult))
            pi, fi = qa[0][:, 0:P].bitcast(i32), gateh[0][:, 0:P].bitcast(i32)
            u, w = (qa[0][:, P * m:P * (m + 1)].bitcast(i32) for m in (1, 2))
            ve.wait_ge(set_pool, 2)
            own(tt(u, pi, fi, ALU.bitwise_xor))
            own(ts(w, u, 5, None, ALU.logical_shift_right))
            own(ts(chunk[:, :], w, 0, None, ALU.is_equal))
            own(tt(before[:, :], pi, fi, ALU.is_lt))
            own(tt(before[:, :], before[:, :], chunk[:, :], ALU.mult))
            own(tt(upto[:, :], pi, fi, ALU.is_le))
            own(tt(upto[:, :], upto[:, :], chunk[:, :], ALU.mult))
            own(tt(after[:, :], chunk[:, :], upto[:, :], ALU.subtract))
            own(ts(w, pi, 31, None, ALU.bitwise_and))
            own(tt(tri[:, :], w[:, 0:CH], fi[:, 0:CH], ALU.is_le))
            own(tt(u[:, 0:CH], w[:, 0:CH], fi[:, 0:CH], ALU.bitwise_xor))
            own(ts(eye32[:, :], u[:, 0:CH], 0, None, ALU.is_equal))
            ve.nop().then_inc(set_dve, 1)
            for r in range(12):
                ve.wait_ge(gh_ps, r + 1)
                ins = tt(gh[:, r * P:(r + 1) * P], gh[:, r * P:(r + 1) * P], C[r % 2][:, 0:P], ALU.add)
                ins.then_inc(gh_ev, 1)
            ve.wait_ge(set_pe, 1)
            own(v.tensor_copy(mean_t[:, :], C[0][:, :]))
            for j in range(2):
                own(tt(prod_t[:, :], mean_t[:, :], w1b[j], ALU.mult))
                own(v.tensor_reduce(sm[0][:, 4 + j:5 + j], prod_t[:, :], AX.X, ALU.add))
            own(tt(h_bias[:, :], sm[0][:, 4:6], b1c[:, 0:2], ALU.add))
            for k in range(KC):
                ve.wait_ge(set_pe, 2 + k)
                ins = v.tensor_copy(voT[:, k * D:(k + 1) * D], ST[k % 2][:, :])
                ins.then_inc(set_dve, 1)
            ve.wait_ge(set_dve, 2 + KC)
            v.memset(ST[0][:, :], 0.0)
            own(v.memset(ST[1][:, :], 0.0))
            ve.nop().then_inc(set_dve, 1)
            ve.wait_ge(set_pe, 6)
            own(tt(bvo[:, :], C[0][:, :], bo_t[:, :], ALU.add))
            own(ts(bvo[:, :], bvo[:, :], 0.5, None, ALU.mult))
            ve.wait_ge(ld, LD + 16 * 6)
            ve.wait_ge(wt_ev, NJ)
            ve.nop().then_inc(ready, 1)

            def moments(b, src, bn):
                own(v.bn_stats(s(b, "stats"), src))
                stand_alone(ve)
                v.bn_aggr(s(b, "mv"), s(b, "stats")).then_inc(bn, 1)

            def route_normalise(src, n):
                for b in range(B):
                    if src is xin:
                        ve.wait_ge(xin_in[b], 16 * n)
                    else:
                        ve.wait_ge(S["x2"][b], n - NT)
                    stand_alone(ve)
                    moments(b, src[b][:, :], S["rbn"][b])
                for b in range(B):
                    ve.wait_ge(S["sl_ps"][b], n - 1)
                    ve.wait_ge(S["rrs"][b], n)
                    ts(rx[b][:, :], src[b][:, :], s(b, "mv")[:, 0:1], s(b, "rstd"), ALU.subtract, ALU.mult)\
                        .then_inc(S["rxn"][b], 1)

            def route_top(n):
                for b in range(B):
                    lg, rep = lgt[b][:, 0:NS], lgt[b][:, NS:2 * NS]
                    ve.wait_ge(S["lg_ps"][b], n)
                    own(stt(lg, Bk[b][:, HID:HID + NS], itau[:, :], b2s[:, :], ALU.mult, ALU.add))
                    stand_alone(ve)
                    own(v.max(s(b, "top"), lg))
                    ts(s(b, "negm"), s(b, "top")[:, 0:1], -1.0, None, ALU.mult).then_inc(S["top"][b], 1)
                    stand_alone(ve)
                    own(v.match_replace(out=rep, in_to_replace=s(b, "top"), in_values=lg, imm_value=BIG))
                    own(tt(rep, lg, rep, ALU.not_equal))

            def route_weights(n):
                for b in range(B):
                    e, al = lgt[b][:, 2 * NS:3 * NS], alpha[:, b * NS:(b + 1) * NS]
                    ve.wait_ge(S["ex"][b], n)
                    own(tt(lgt[b][:, 0:NS], e, lgt[b][:, NS:2 * NS], ALU.mult))
                    own(v.tensor_reduce(s(b, "den"), lgt[b][:, 0:NS], AX.X, ALU.add))
                    own(v.reciprocal(s(b, "rden"), s(b, "den")))
                    ve.wait_ge(aT_ps, n - 1)
                    ts(al, lgt[b][:, 0:NS], s(b, "rden"), None, ALU.mult).then_inc(S["al"][b], 1)

            def route_sums(n):
                for b in range(B):
                    ve.wait_ge(S["sl_ps"][b], n)
                    tt(slotacc[b][:, :], slotacc[b][:, :], slot_sum_cols(b), ALU.add).then_inc(S["sacc"][b], 1)

            ROUTE = 2 * (1 + 1 + 1 + 1 + 1 + 3)
            base0 = own.n
            with ve.Fori(1, NT + 1) as i:
                own.base, own.n = base0 + ROUTE * (i - 1), 0
                route_normalise(xin, i)
                route_top(i)
                route_weights(i)
                route_sums(i)
                assert own.n == ROUTE
            own.base, own.n = 0, base0 + ROUTE * NT

            def mid_dve_part(m):
                o_pe, o_act = 3 * m, 4 * m
                for b in range(B):
                    ve.wait_ge(S["sacc"][b], NT * (m + 1))
                    ws = slotacc[b][:, KC * NS:(KC + 1) * NS]
                    own(ts(ws, ws, 1e-8, None, ALU.add))
                    own(v.reciprocal(lgt[b][:, 0:NS], ws))
                    own(tt(giT[:, :].rearrange("p (k n) -> p k n", k=KC)[:, :, b * NS:(b + 1) * NS],
                           slotacc[b][:, 0:KC * NS].rearrange("p (k n) -> p k n", k=KC),
                           lgt[b][:, 0:NS].unsqueeze(1).to_broadcast([P, KC, NS]), ALU.mult))
                    own(v.memset(slotacc[b][:, :], 0.0))
                ve.nop().then_inc(mid_dve, 1)
                ve.wait_ge(mid_pe, o_pe + 1)
                tt(gr[:, :], A[0][:, :], gh[:, 0:D], ALU.add).then_inc(mid_dve, 1)
                tt(gz[:, :], A[1][:, :], gh[:, D:2 * D], ALU.add).then_inc(mid_dve, 1)
                own(tt(gn[:, :], C[0][:, :], bih_n[:, :], ALU.add))
                ve.wait_ge(mid_act, o_act + 1)
                own(tt(gr[:, :], gr[:, :], gh[:, 2 * D:3 * D], ALU.mult))
                tt(gn[:, :], gn[:, :], gr[:, :], ALU.add).then_inc(mid_dve, 1)
                ve.wait_ge(mid_act, o_act + 3)
                own(tt(gr[:, :], hs[:, :], gn[:, :], ALU.subtract))
                own(tt(gz[:, :], gz[:, :], gr[:, :], ALU.mult))
                own(tt(ht[:, :], gn[:, :], gz[:, :], ALU.add))
                ve.nop().then_inc(mid_dve, 2)
                ve.wait_ge(mid_pe, o_pe + 3)
                stt(sv[:, :], Bk[1][:, :], 0.5, bvo[:, :], ALU.mult, ALU.add).then_inc(mid_dve, 1)
            mid_dve_part(0)

            def first_x1(m, held):
                for b in range(B):
                    ve.wait_ge(S["ffn_ps"][b], m)
                    ve.wait_ge(xin_in[b], 16 * (m + NT))
                    if held:
                        ve.wait_ge(S["xhold"][b], both(m - 1, b))
                    tt(xc[b][:, :], xin[b][:, :], C[b][:, :], ALU.add).then_inc(S["x1"][b], 1)
                    ve.wait_ge(S["x1"][b], m)
                    moments(b, xc[b][:, :], S["bn"][b])
                for b in range(B):
                    ve.wait_ge(S["rs"][b], both(m, b))
                    ts(xn[b][:, :], xc[b][:, :], s(b, "mv")[:, 0:1], s(b, "rstd"), ALU.subtract, ALU.mult)\
                        .then_inc(S["xn"][b], 1)

            def invert(n, first, last):
                if n is None:
                    return
                if first == 0:
                    ve.wait_ge(eye_set, n)
                    ve.wait_ge(n_in, 16 * n)
                N = nblk[:, :].rearrange("p (s t) -> p s t", s=CH)
                Y = yblk[:, :].rearrange("p (r t) -> p r t", r=CH)
                for s_ in range(first, last):
                    rows, cols = s_ + 1, CH - 1 - s_
                    o = outer[:, 0:rows * cols].rearrange("p (r t) -> p r t", r=rows)
                    own(tt(o, Y[:, 0:rows, s_:s_ + 1].to_broadcast([P, rows, cols]),
                           N[:, s_:s_ + 1, s_ + 1:CH].to_broadcast([P, rows, cols]), ALU.mult))
                    ins = tt(Y[:, 0:rows, s_ + 1:CH], Y[:, 0:rows, s_ + 1:CH], o, ALU.subtract)
                    if s_ < CH - 2:
                        own(ins)
                    else:
                        ins.then_inc(inv, 1)

            def step_dve(n, j, m):
                if n is not None:
                    for b in range(B):
                        ve.wait_ge(S["ksq"][b], both(n, b))
                        own(v.tensor_reduce(s(b, "ssk"), heads(scr[b]), AX.X, ALU.add))
                        ts(s(b, "ssk"), s(b, "ssk"), 1e-24, None, ALU.max).then_inc(S["ssk"][b], 1)
                        ve.wait_ge(S["ab_ps"][b], n)
                        own(tt(s(b, "ab"), A[b][:, 0:2 * H], ab_bias[:, :], ALU.add))
                        za, zb = s(b, "ab")[:, 0:H], s(b, "ab")[:, H:2 * H]
                        stt(s(b, "zi")[:, 0:H], za, -1.0, za, ALU.mult, ALU.min)
                        ts(s(b, "zi")[:, H:2 * H], zb, -1.0, 80.0, ALU.mult, ALU.min).then_inc(S["zi"][b], 1)
                        ve.wait_ge(S["rk"][b], both(n, b))
                        tt(heads(kn[b]), C[b][:, :].rearrange("p (h e) -> p h e", h=H), bc(s(b, "rk")), ALU.mult)\
                            .then_inc(S["kn"][b], 1)
                    for b in range(B):
                        ve.wait_ge(S["kn"][b], n)
                        v.transpose(heads(kqT[b], 2)[:, :, 0:HD], heads(kn[b]))
                    for b in range(B):
                        ve.wait_ge(S["q_ev"][b], n)
                        own(v.tensor_reduce(s(b, "ssq"), heads(scr[b]), AX.X, ALU.add))
                        ts(s(b, "ssq"), s(b, "ssq"), 1e-24, None, ALU.max).then_inc(S["ssq"][b], 1)
                        v.transpose(heads(kqT[b], 2)[:, :, HD:2 * HD], heads(qs[b])).then_inc(S["kqt"][b], 1)
                    for b in range(B):
                        ve.wait_ge(S["ln"][b], both(n, b))
                        stt(s(b, "la"), s(b, "ab")[:, 0:H], 0.0, s(b, "ln"), ALU.min, ALU.subtract).then_inc(S["la"][b], 1)
                        own(ts(s(b, "opb"), s(b, "ez")[:, H:2 * H], 1.0, None, ALU.add))
                        v.reciprocal(s(b, "be"), s(b, "opb")).then_inc(S["be"][b], 1)
                if j is not None:
                    for b in range(B):
                        ve.wait_ge(S["gq_ps"][b], both(j, b))
                        ve.wait_ge(S["qaT"][b], both(j, b))
                        tt(qg[b][:, :], qa[b][:, :], AB[b][:, :], ALU.subtract).then_inc(S["qg"][b], 1)
                if n is not None:
                    for b in range(B):
                        ve.wait_ge(S["e4"][b], n)
                        tt(heads(vk[b], 2)[:, :, HD:2 * HD], heads(kn[b]), bc(s(b, "e4")[:, 0:H]), ALU.mult)\
                            .then_inc(S["kp"][b], 1)
                    for b in range(B):
                        ve.wait_ge(S["tanh"][b], both(n, b))
                        if j is not None:
                            ve.wait_ge(S["ghold"][b], both(n - 1, b))
                        stt(gate[b][:, :], scr[b][:, :], 1.0, C[b][:, :], ALU.add, ALU.mult).then_inc(S["gate"][b], 1)
                    for b in range(B):
                        ve.wait_ge(S["gate"][b], n)
                        if j is not None:
                            ve.wait_ge(S["qg"][b], both(j, b))
                        own(tt(heads(scr[b]), heads(qs[b]), bc(s(b, "e4")[:, H:2 * H]), ALU.mult))
                        own(v.transpose(heads(qa[b], 2)[:, :, 0:HD], heads(scr[b])))
                    for b in range(B):
                        ve.wait_ge(S["gram_ps"][b], n)
                        ve.wait_ge(S["d33"][b], n)
                        own(tt(heads(nn[b]), AB[b][:, :].rearrange("p (h e) -> p h e", h=H)[:, :, 0:HD],
                               D33[b][:, :, 0:HD], ALU.mult))
                        tt(heads(pk[b], 2)[:, :, 0:HD], AB[b][:, :].rearrange("p (h e) -> p h e", h=H)[:, :, HD:2 * HD],
                           D33[b][:, :, 1:HD + 1], ALU.mult).then_inc(S["nn"][b], 1)
                invert(n, 0, 10)
                if j is not None:
                    for b in range(B):
                        ve.wait_ge(S["y_ps"][b], j)
                        ve.wait_ge(S["rqh"][b], both(j, b))
                        if n is not None:
                            ve.wait_ge(S["kd"][b], both(n, b))
                        tt(heads(kn[b]), C[b][:, :].rearrange("p (h e) -> p h e", h=H), bc(s(b, "rqh")), ALU.mult)\
                            .then_inc(S["yq"][b], 1)
                    for b in range(B):
                        ve.wait_ge(S["ysq"][b], both(j, b))
                        ts(s(b, "yv"), s(b, "ys"), 1.0 / D, 1e-5, ALU.mult, ALU.add).then_inc(S["yv"][b], 1)
                    for b in range(B):
                        ve.wait_ge(S["yrs"][b], both(j, b))
                        ve.wait_ge(S["ghold"][b], both(j, b))
                        stt(qs[b][:, :], kn[b][:, :], s(b, "yr"), gateh[b][:, :], ALU.mult, ALU.mult).then_inc(S["y3"][b], 1)
                invert(n, 10, 20)
                if j is not None:
                    for b in range(B):
                        ve.wait_ge(S["wo_ps"][b], both(j, b))
                        ve.wait_ge(S["xhold"][b], both(j, b))
                        tt(xh[b][:, :], xh[b][:, :], Bk[b][:, :], ALU.add).then_inc(S["x2"][b], 1)
                    route_normalise(xh, j + NT)
                invert(n, 20, CH - 1)
                if m is not None:
                    first_x1(m, True)
                if j is not None:
                    route_top(j + NT)
                    route_weights(j + NT)
                    route_sums(j + NT)

            ve.wait_ge(wih_st, 16 * 6)
            first_x1(1, False)
            step_dve(1, None, 2)
            PER = ROUTE + 2 * 8 + 2 * (CH - 1) - 1
            base1 = own.n
            with ve.Fori(1, NT - 1) as i:
                own.base, own.n = base1 + PER * (i - 1), 0
                step_dve(i + 1, i, i + 2)
                assert own.n == PER, own.n
            own.base, own.n = 0, base1 + PER * (NT - 2)
            step_dve(NT, NT - 1, None)
            step_dve(None, NT, None)
            mid_dve_part(1)

            with ve.Fori(NT + 1, 2 * NT + 1) as i:
                for b in range(B):
                    ve.wait_ge(S["ffn_ps"][b], i)
                    ve.wait_ge(xin_in[b], 16 * (i + NT))
                    ve.wait_ge(x2_st[b], 16 * (i - 1))
                    tt(xc[b][:, :], xin[b][:, :], C[b][:, :], ALU.add).then_inc(S["x1"][b], 1)


_INS = ['L0_attn_x', 'L0_attn_Wq', 'L0_attn_Wk', 'L0_attn_Wv', 'L0_attn_Wa', 'L0_attn_ba', 'L0_attn_Wb', 'L0_attn_bb',
        'L0_attn_Wg', 'L0_attn_Wo', 'L0_attn_g_norm', 'L0_ffn_slot_init', 'L0_ffn_slot_scale', 'L0_ffn_w1', 'L0_ffn_b1',
        'L0_ffn_w2', 'L0_ffn_b2', 'L0_ffn_gru_wih', 'L0_ffn_gru_whh', 'L0_ffn_gru_bih', 'L0_ffn_gru_bhh', 'L0_ffn_wv',
        'L0_ffn_bv', 'L0_ffn_wo', 'L0_ffn_bo', 'L0_ffn_tau']
_OUTS = [((B, T, D), 'float32')]


def kernel(**inputs):
    import numpy as _np
    import concourse.bacc as _bacc
    from concourse import mybir as _mybir
    from concourse.bass_utils import run_bass_kernel_spmd as _run

    nc = _bacc.Bacc("TRN2", target_bir_lowering=False, num_devices=1)
    arrays, args = {}, []
    for name in _INS:
        a = _np.ascontiguousarray(inputs[name])
        arrays[f"in_{name}_dram"] = a
        args.append(nc.dram_tensor(f"in_{name}_dram", a.shape, _mybir.dt.from_np(a.dtype), kind="ExternalInput").ap())
    for i, (shape, dtype) in enumerate(_OUTS):
        dt = _mybir.dt.from_np(_np.dtype(dtype))
        args.append(nc.dram_tensor(f"out_{i}_dram", shape, dt, kind="ExternalOutput").ap())
    build(nc, *args)
    r = _run(nc, [arrays], core_ids=[0])
    got = tuple(r.results[0][f"out_{i}_dram"] for i in range(len(_OUTS)))
    return got[0]
```

```python
import numpy as np
import concourse.bass as bass
from concourse import mybir
from concourse.alu_op_type import AluOpType as ALU
from contextlib import ExitStack

f32 = mybir.dt.float32
i32 = mybir.dt.int32
ACT = mybir.ActivationFunctionType
AX = mybir.AxisListType

B, T, D = 2, 4096, 512
H, HD = 16, 32
NS, HID = 64, 256
P = 128
KC = D // P
NT = T // P
CH = 32
NC = P // CH
BIG = -3.0e38


def build(nc, x, Wq, Wk, Wv, Wa, ba, Wb, bb, Wg, Wo, g_norm, slot_init, slot_scale, w1, b1, w2, b2,
          wih, whh, bih, bhh, wv, bv, wo, bo, tau, out):
    ctx = ExitStack()
    with ctx:
        def sb(name, cols, dt=f32):
            return ctx.enter_context(nc.sbuf_tensor(name, [P, cols], dt))

        def sem(name):
            return ctx.enter_context(nc.semaphore(name))

        def sem2(name):
            return [sem(f"{name}{b}") for b in range(B)]

        x2_dram = nc.dram_tensor("x2_scratch", (B, NT, P, D), f32, kind="Internal").ap()
        at_dram = [nc.dram_tensor(f"alphaT_scratch{m}", (NT, P, P), f32, kind="Internal").ap() for m in range(2)]
        n_dram = nc.dram_tensor("n_scratch", (B, H, P, CH), f32, kind="Internal").ap()
        y_dram = nc.dram_tensor("y_scratch", (B, H, P, CH), f32, kind="Internal").ap()
        wih_dram = nc.dram_tensor("wihT_scratch", (P, 12 * D), f32, kind="Internal").ap()
        vo_dram = nc.dram_tensor("voT_scratch", (P, KC * D), f32, kind="Internal").ap()
        x_t = x.rearrange("b (n p) d -> b n p d", p=P)
        out_t = out.rearrange("b (n p) d -> b n p d", p=P)

        w_kvqg = sb("w_kvqg", KC * 4 * D)
        w_ab = sb("w_ab", KC * 2 * H)
        w_out = sb("w_out", KC * D)
        w1T = sb("w1T", KC * HID)
        w2T = sb("w2T", 2 * NS)
        gh = sb("gh", 3 * D)
        bih_n = sb("bih_n", D)
        bvo = sb("bvo", D)
        hs = sb("hs", D)
        ident = sb("ident", P)
        ones = sb("ones", P)
        before = sb("before", P)
        upto = sb("upto", P)
        after = sb("after", P)
        chunk = sb("chunk", P)
        tri = sb("tri", CH)
        eye32 = sb("eye32", CH)
        half = sb("half", H)
        ab_bias = sb("ab_bias", 2 * H)
        b2s = sb("b2s", NS)
        itau = sb("itau", 1)
        h_bias = sb("h_bias", 2)
        gcol = sb("gcol", KC)
        sv = sb("sv", D)
        alpha = sb("alpha", B * NS)
        aT_in = sb("aT_in", P)
        aT_out = sb("aT_out", P)
        slotacc = sb("slotacc", D + 1)

        xin = [sb(f"xin{b}", D) for b in range(B)]
        xc = [sb(f"xc{b}", D) for b in range(B)]
        xh = [sb(f"xh{b}", D) for b in range(B)]
        xn = [sb(f"xn{b}", D) for b in range(B)]
        xnT = [sb(f"xnT{b}", D) for b in range(B)]
        kn = [sb(f"kn{b}", D) for b in range(B)]
        qs = [sb(f"qs{b}", D) for b in range(B)]
        scr = [sb(f"scr{b}", D) for b in range(B)]
        vk = [sb(f"vk{b}", 2 * D) for b in range(B)]
        gate = [sb(f"gate{b}", D) for b in range(B)]
        gateh = [sb(f"gateh{b}", D) for b in range(B)]
        dr = [sb(f"dr{b}", D) for b in range(B)]
        dm = [sb(f"dm{b}", H * (HD + 1)) for b in range(B)]
        u = [sb(f"u{b}", D) for b in range(B)]
        bd = [sb(f"bd{b}", H * P) for b in range(B)]
        kqT = [sb(f"kqT{b}", 2 * D) for b in range(B)]
        qg = [sb(f"qg{b}", 2 * D) for b in range(B)]
        qa = [sb(f"qa{b}", 2 * D) for b in range(B)]
        nn = [sb(f"nn{b}", D) for b in range(B)]
        pk = [sb(f"pk{b}", 2 * D) for b in range(B)]
        ss = [sb(f"ss{b}", D) for b in range(B)]
        nblk = sb("nblk", CH * CH)
        yblk = sb("yblk", CH * CH)
        outer = sb("outer", 256)
        sm = [sb(f"sm{b}", 352) for b in range(B)]

        def heads(t, n=1):
            return t[:, 0:n * D].rearrange("p (h e) -> p h e", h=H)

        def bc(col):
            return col.unsqueeze(2).to_broadcast([P, H, HD])

        def allheads(mask):
            return mask.unsqueeze(1).to_broadcast([P, H, HD])

        SMALL = {}
        at = 0
        for name, n in [("stats", 6), ("mv", 2), ("vs", 1), ("rstd", 1), ("ssk", H), ("rk", H), ("ssq", H),
                        ("rq", H), ("rqh", H), ("ab", 2 * H), ("zi", 2 * H), ("ez", 2 * H), ("ln", H), ("la", H), ("opb", H),
                        ("be", H), ("e4", 4 * H), ("bel", H), ("ys", 1), ("yv", 1), ("yr", 1),
                        ("top", 8), ("negm", 1), ("den", 1), ("rden", 1)]:
            SMALL[name] = (at, n)
            at += n
        lgt = [sb(f"lgt{b}", 3 * NS) for b in range(B)]

        def s(b, name):
            o, n = SMALL[name]
            return sm[b][:, o:o + n]

        voT = bd[0]
        D33 = [dm[b][:, :].rearrange("p (h e) -> p h e", h=H) for b in range(B)]
        hT = [kn[b][:, 0:2 * P] for b in range(B)]
        rx = [xn, qs]

        AB = [ctx.enter_context(nc.psum_tensor(f"AB{b}", [P, 1024], f32)) for b in range(B)]
        C = [ctx.enter_context(nc.psum_tensor(f"C{b}", [P, 512], f32)) for b in range(B)]
        ST = [ctx.enter_context(nc.psum_tensor(f"ST{b}", [P, 512], f32)) for b in range(B)]
        A = [AB[b][:, 0:512] for b in range(B)]
        Bk = [AB[b][:, 512:1024] for b in range(B)]

        ld = sem("ld")
        ring_in = [sem(f"ring_in{r}") for r in range(4)]
        wt_ps, wt_ev = sem("wt_ps"), sem("wt_ev")
        gh_ps, gh_ev = sem("gh_ps"), sem("gh_ev")
        set_pe, set_dve, set_pool, ready = sem("set_pe"), sem("set_dve"), sem("set_pool"), sem("ready")
        dve_own, pool_own, act_own = sem("dve_own"), sem("pool_own"), sem("act_own")
        xin_in, at_in, x2_st, at_st = sem2("xin_in"), sem("at_in"), sem2("x2_st"), sem("at_st")
        each = ("ffn_ps x1 bn xn xT_ps xnT k_ps v_ps ab_ps q_ps g_ps ssk kn v_ev qsq ssq q_ev "
                "zi gate e4 dec_ps draw d33 gram_ps s_ps scp y_ps yq "
                "y3 yT_ps yT x2 rbn rrs rxn rxT_ps rxnT h_ps hT lg_ps top ex al").split()
        shared = ("uw qg wo_ps ksq rs rk rq ez ln la be tanh rhsd cum_ps kd kqt kp qaT yv yrs ysq nn gq_ps "
                  "uw_ps kbd pt qe y1_ps xhold ghold rqh").split()
        S = {n: sem2(n) for n in each}
        S.update({n: [sem(n)] * B for n in shared})

        def both(i, b):
            return 2 * i - 1 + b

        sl_ps, sacc, aT_ps, aT = sem("sl_ps"), sem("sacc"), sem("aT_ps"), sem("aT")
        n_out, n_in, y_out, y_in = sem("n_out"), sem("n_in"), sem("y_out"), sem("y_in")
        eye_set, inv, wih_st, wih_in = sem("eye_set"), sem("inv"), sem("wih_st"), sem("wih_in")
        carriers = sem("carriers")
        mid_pe, mid_act, mid_dve = sem("mid_pe"), sem("mid_act"), sem("mid_dve")

        block = ctx.enter_context(nc.Block())

        def stand_alone(e):
            e.sem_inc(carriers, 1)

        class Own:
            def __init__(self, e, sm_):
                self.e, self.sem, self.base, self.n = e, sm_, 0, 0

            def __call__(self, ins):
                ins.then_inc(self.sem, 1)
                self.n += 1
                self.e.wait_ge(self.sem, self.base + self.n)

        jobs = []
        for j in range(2):
            jobs.append((w1[j * P:(j + 1) * P, 0:D], P, KC, ("w1", j)))
        jobs.append((w2, NS, 2, ("w2", 0)))
        for j in range(4):
            jobs.append((wo[j * P:(j + 1) * P, :], P, KC, ("wo", j)))
        for j in range(12):
            jobs.append((wih[j * P:(j + 1) * P, :], P, KC, ("wih", j)))
        jobs.append((None, P, KC, ("hs", 0)))
        for j in range(12):
            jobs.append((whh[j * P:(j + 1) * P, :], P, KC, ("whh", j)))
        NJ = len(jobs)
        HSJ = [j for j in range(NJ) if jobs[j][3][0] == "hs"][0]
        rings = [kn[0], kn[1], qs[0], qs[1]]
        tps = [A[0], A[1], Bk[0], Bk[1]]
        hsT = gate[0]
        whh_ring = [gate[1], dr[0]]

        wih_region = [(kqT[0], 2), (kqT[1], 2), (qg[0], 2), (qg[1], 2), (bd[1], 4)]

        def wihT_at(k, j):
            n = 3 * k + j
            for buf, cols in wih_region:
                if n < cols:
                    return buf[:, n * D:(n + 1) * D]
                n -= cols

        def woT_at(k):
            return (vk[0], vk[1])[k // 2][:, (k % 2) * D:(k % 2 + 1) * D]

        def dest(j):
            kind, r = jobs[j][3]
            if kind == "w1":
                return w1T[:, :].rearrange("p (k n) -> p k n", k=KC)[:, :, r * P:(r + 1) * P]
            if kind == "w2":
                return w2T[:, :].rearrange("p (k n) -> p k n", k=2)
            if kind == "hs":
                return hsT[:, :].rearrange("p (k n) -> p k n", k=KC)
            if kind == "whh":
                return whh_ring[r % 2][:, :].rearrange("p (k n) -> p k n", k=KC)
            return None

        LD = 16 * 20
        b1c = ss[0]
        wvn = [pk[k // 2][:, (k % 2) * D:(k % 2 + 1) * D] for k in range(KC)]
        w1b = [nblk[:, 0:D], nblk[:, D:2 * D]]
        bhh_t, bih_t = (yblk, xnT[0]), (qa[1], xnT[1])
        bv_c, bo_t = ss[1], u[1]
        mean_t, prod_t = scr[0], scr[1]
        ssc = sm[0][:, 0:1]
        taut = sm[0][:, 1:2]

        def ring_user(j, n):
            seen = 0
            for jj in range(NJ):
                if jobs[jj][0] is not None:
                    if seen == n - 4:
                        return jj + 1
                    seen += 1

        def ring_no(j):
            return sum(1 for jj in range(j) if jobs[jj][0] is not None)

        def ab_place(b):
            at = HID + NS + b * 2 * H
            return Bk[1][:, at:at + 2 * H]

        def diagonal(b, c):
            return bd[b][CH * c:CH * (c + 1), :].rearrange("p (h m) -> p h m", h=H)[:, :, CH * c:CH * (c + 1)]

        def gh_part(pe, mm, r, j):
            pe.wait_ge(wt_ev, HSJ + 2 + r)
            if r >= 2:
                pe.wait_ge(gh_ev, r - 1)
            for k in range(KC):
                last = mm(C[r % 2][:, 0:P], hsT[:, k * P:(k + 1) * P], whh_ring[r % 2][:, k * P:(k + 1) * P],
                          start=(k == 0), stop=(k == KC - 1))
            last.then_inc(gh_ps, 1)

        giT, gr, gz, gn, ht, hTT = kn[0], qs[0], qs[1], gate[0], gate[1], kn[1]
        NMID = 4

        def mid(e, m):
            o_pe, o_act, o_dve = 4 * m, 5 * m, 7 * m
            if e is nc.tensor:
                mm, tr = nc.tensor.matmul, nc.tensor.transpose
                e.wait_ge(mid_dve, o_dve + 1)
                e.wait_ge(aT, NT * (m + 1))
                for k in range(KC):
                    last = tr(Bk[0][:, k * P:(k + 1) * P], ht[:, k * P:(k + 1) * P], ident[:, :])
                last.then_inc(mid_pe, 1)
                e.wait_ge(mid_act, o_act + 1)
                if m == 1:
                    e.wait_ge(wih_in, 16 * (len(wih_region) + 1))
                for j, dst in enumerate((A[0], A[1], C[0])):
                    for k in range(KC):
                        last = mm(dst[:, :], giT[:, k * P:(k + 1) * P], wihT_at(k, j),
                                  start=(k == 0), stop=(k == KC - 1))
                last.then_inc(mid_pe, 1)
                e.wait_ge(mid_dve, o_dve + 6)
                for k in range(KC):
                    last = tr(Bk[0][:, k * P:(k + 1) * P], ht[:, k * P:(k + 1) * P], ident[:, :])
                last.then_inc(mid_pe, 1)
                e.wait_ge(mid_act, o_act + 5)
                for k in range(KC):
                    last = mm(Bk[1][:, :], hTT[:, k * P:(k + 1) * P], voT[:, k * D:(k + 1) * D],
                              start=(k == 0), stop=(k == KC - 1))
                last.then_inc(mid_pe, 1)
                e.wait_ge(mid_dve, o_dve + 7)
            elif e is nc.scalar:
                act = nc.scalar.activation
                e.wait_ge(mid_pe, o_pe + 1)
                act(giT[:, :], Bk[0][:, :], ACT.Copy).then_inc(mid_act, 1)
                e.wait_ge(mid_dve, o_dve + 2)
                act(gr[:, :], gr[:, :], ACT.Sigmoid).then_inc(mid_act, 1)
                e.wait_ge(mid_dve, o_dve + 3)
                act(gz[:, :], gz[:, :], ACT.Sigmoid).then_inc(mid_act, 1)
                e.wait_ge(mid_dve, o_dve + 4)
                act(gn[:, :], gn[:, :], ACT.Tanh).then_inc(mid_act, 1)
                e.wait_ge(mid_pe, o_pe + 3)
                act(hTT[:, :], Bk[0][:, :], ACT.Copy).then_inc(mid_act, 1)

        @block.sync
        def _(sp):
            def load(dst, src):
                sp.dma_start(dst, src, allow_slow_non_contiguous=True).then_inc(ld, 16)
            load(hs[0:NS, :], slot_init)
            load(hs[NS:P, :], slot_init)
            load(ssc[0:NS, :], slot_scale)
            load(ssc[NS:P, :], slot_scale)
            load(taut, tau.partition_broadcast(P))
            load(b1c[:, 0:2], b1.rearrange("(j p) -> p j", p=P))
            load(b2s[:, :], b2.partition_broadcast(P))
            load(bv_c[:, 0:KC], bv.rearrange("(j p) -> p j", p=P))
            load(bo_t[:, :], bo.partition_broadcast(P))
            load(ab_bias[:, 0:H], ba.partition_broadcast(P))
            load(ab_bias[:, H:2 * H], bb.partition_broadcast(P))
            load(gcol[:, :], g_norm.rearrange("(j p) -> p j", p=P))
            load(bih_t[0][:, :], bih[0:2 * D].partition_broadcast(P))
            load(bih_t[1][:, :], bih[2 * D:3 * D].partition_broadcast(P))
            load(bhh_t[0][:, :], bhh[0:2 * D].partition_broadcast(P))
            load(bhh_t[1][:, :], bhh[2 * D:3 * D].partition_broadcast(P))
            for j in range(2):
                load(pk[j][:, :].rearrange("p (k n) -> p k n", k=2),
                     wv[2 * j * P:2 * (j + 1) * P, :].rearrange("(k p) n -> p k n", p=P))
            load(nblk[:, :].rearrange("p (k n) -> p k n", k=2),
                 w1[:, D:2 * D].rearrange("(k p) n -> p k n", p=P))
            load(w_out[:, :].rearrange("p (k n) -> p k n", k=KC), Wo.rearrange("(k p) n -> p k n", p=P))
            loaded = 0
            for j in range(NJ):
                if jobs[j][0] is None:
                    continue
                if loaded >= 4:
                    sp.wait_ge(wt_ps, ring_user(j, loaded))
                src, rows, cols, _ = jobs[j]
                sp.dma_start(rings[loaded % 4][0:rows, 0:cols * P], src).then_inc(ring_in[loaded % 4], 16)
                loaded += 1
            w4 = w_kvqg[:, :].rearrange("p (k m n) -> p k m n", k=KC, m=4)
            for m, w in enumerate((Wk, Wv, Wq, Wg)):
                load(w4[:, :, m, :], w.rearrange("(k p) n -> p k n", p=P))
            wab = w_ab[:, :].rearrange("p (k m n) -> p k m n", k=KC, m=2)
            for m, w in enumerate((Wa, Wb)):
                load(wab[:, :, m, :], w.rearrange("(k p) n -> p k n", p=P))

            def load_x(src, n, i, free):
                for b in range(B):
                    if free is not None:
                        sp.wait_ge(free[b], i)
                    sp.dma_start(xin[b][:, :], src[b, bass.ds(n, 1), :, :].rearrange("o p d -> (o p) d"))\
                        .then_inc(xin_in[b], 16)

            def store_at(m, n, count):
                sp.wait_ge(aT, count)
                sp.dma_start(at_dram[m][bass.ds(n, 1), :, :].rearrange("o p d -> (o p) d"), aT_out[:, :])\
                    .then_inc(at_st, 16)

            sp.wait_ge(wt_ev, HSJ)
            n = 0
            for buf, cols in wih_region:
                sp.dma_start(wih_dram[:, n * D:(n + cols) * D], buf[:, :]).then_inc(wih_st, 16)
                n += cols
            sp.wait_ge(set_dve, 2 + KC)
            sp.dma_start(vo_dram, voT[:, :]).then_inc(wih_st, 16)

            sp.wait_ge(ready, 1)
            for b in range(B):
                sp.dma_start(xin[b][:, :], x_t[b, 0, :, :]).then_inc(xin_in[b], 16)
            load_x(x_t, 1, 1, S["rxn"])
            load_x(x_t, 2, 2, S["rxn"])
            with sp.Fori(1, NT - 2) as i:
                load_x(x_t, i + 2, i + 2, S["rxn"])
                store_at(0, i - 1, i)
            for n in range(NT - 2, NT + 1):
                store_at(0, n - 1, n)
            for b in range(B):
                sp.wait_ge(S["rxn"][b], NT)
            sp.wait_ge(at_st, 16 * NT)

            def load_at(m, n):
                sp.dma_start(aT_in[:, :], at_dram[m][bass.ds(n, 1), :, :].rearrange("o p d -> (o p) d"))\
                    .then_inc(at_in, 16)

            def prefetch(m):
                load_x(x_t, m, m, S["x1"])
                load_at(0, m)

            def step_sp(n, j, m, more):
                if n is not None:
                    for b in range(B):
                        sp.wait_ge(S["nn"][b], both(n, b))
                        sp.dma_start(n_dram[b, :, :, :].rearrange("h p t -> p h t"), heads(nn[b])).then_inc(n_out, 16)
                    sp.wait_ge(n_out, 32 * n)
                    sp.dma_start(nblk[:, :], n_dram.rearrange("b h (c s) t -> (b h c) (s t)", s=CH)).then_inc(n_in, 16)
                    sp.wait_ge(inv, n)
                    sp.dma_start(y_dram.rearrange("b h (c s) t -> (b h c) (s t)", s=CH), yblk[:, :]).then_inc(y_out, 16)
                    sp.wait_ge(y_out, 16 * n)
                    for b in range(B):
                        for c in range(NC):
                            sp.dma_start(diagonal(b, c), y_dram[b, :, CH * c:CH * (c + 1), :].rearrange("h p t -> p h t"))\
                                .then_inc(y_in, 16)
                if more:
                    prefetch(m)
                if j is not None:
                    store_at(1, j - 1, j + NT)
            for b in range(B):
                sp.dma_start(xin[b][:, :], x_t[b, 0, :, :]).then_inc(xin_in[b], 16)
            load_at(0, 0)
            prefetch(1)
            step_sp(1, None, 2, True)
            with sp.Fori(1, NT - 2) as i:
                step_sp(i + 1, i, i + 2, True)
            step_sp(NT - 1, NT - 2, NT, False)
            step_sp(NT, NT - 1, None, False)
            step_sp(None, NT, None, False)
            for b in range(B):
                sp.wait_ge(S["y_ps"][b], NT)
            sp.wait_ge(wih_st, 16 * (len(wih_region) + 1))
            n = 0
            for buf, cols in wih_region:
                sp.dma_start(buf[:, :], wih_dram[:, n * D:(n + cols) * D]).then_inc(wih_in, 16)
                n += cols
            sp.dma_start(voT[:, :], vo_dram).then_inc(wih_in, 16)
            for b in range(B):
                sp.wait_ge(x2_st[b], 16 * NT)
            sp.wait_ge(at_st, 32 * NT)

            for b in range(B):
                sp.dma_start(xin[b][:, :], x2_dram[b, 0, :, :]).then_inc(xin_in[b], 16)
            sp.dma_start(aT_in[:, :], at_dram[1][0, :, :]).then_inc(at_in, 16)
            with sp.Fori(1, NT) as i:
                load_x(x2_dram, i, i + NT, S["x1"])
                load_at(1, i)
                for b in range(B):
                    sp.dma_start(out_t[b, bass.ds(i - 1, 1), :, :].rearrange("o p d -> (o p) d"), xc[b][:, :])\
                        .then_inc(x2_st[b], 16)
            for b in range(B):
                sp.wait_ge(S["x1"][b], 2 * NT)
                sp.dma_start(out_t[b, NT - 1, :, :], xc[b][:, :]).then_inc(x2_st[b], 16)
            for b in range(B):
                sp.wait_ge(x2_st[b], 32 * NT)

        @block.tensor
        def _(pe):
            mm, tr = nc.tensor.matmul, nc.tensor.transpose
            pe.wait_ge(set_pool, 1)
            for j in range(NJ):
                src, rows, cols, (kind, r) = jobs[j]
                if kind == "hs":
                    pe.wait_ge(set_dve, 1)
                    buf = hs
                else:
                    n = ring_no(j)
                    pe.wait_ge(ring_in[n % 4], 16 * (n // 4 + 1))
                    buf = rings[n % 4]
                if j >= 4:
                    pe.wait_ge(wt_ev, j - 3)
                for k in range(cols):
                    last = tr(tps[j % 4][:, k * rows:(k + 1) * rows], buf[0:rows, k * P:(k + 1) * P],
                              ident[0:rows, 0:rows])
                last.then_inc(wt_ps, 1)
                if kind == "whh" and r >= 1:
                    gh_part(pe, mm, r - 1, j)
            gh_part(pe, mm, 11, NJ)
            pe.wait_ge(set_dve, 2)
            pe.wait_ge(gh_ev, 12)
            mm(C[0][:, :], aT_in[0:NS, :], hs[0:NS, :], start=True, stop=True).then_inc(set_pe, 1)
            for k in range(KC):
                if k >= 2:
                    pe.wait_ge(set_dve, 1 + k)
                for e in range(KC):
                    last = mm(ST[k % 2][:, :], wvn[e][:, k * P:(k + 1) * P], woT_at(e), start=(e == 0), stop=(e == KC - 1))
                last.then_inc(set_pe, 1)
            pe.wait_ge(set_dve, 7)
            for e in range(KC):
                last = mm(C[0][:, :], xin[0][:, e * P:(e + 1) * P], woT_at(e), start=(e == 0), stop=(e == KC - 1))
            last.then_inc(set_pe, 1)

            def transpose_to(dst, src):
                for k in range(KC):
                    last = tr(dst[:, k * P:(k + 1) * P], src[:, k * P:(k + 1) * P], ident[:, :])
                return last

            def route_xT(j, n, dst, src, bs=range(B)):
                for b in bs:
                    pe.wait_ge(S["rxn"][b], n)
                    if j is not None:
                        pe.wait_ge(S["yT"][b], j)
                    transpose_to(dst[b], src[b]).then_inc(S["rxT_ps"][b], 1)

            def route_hidden(j, n, dst, bs=range(B)):
                for b in bs:
                    pe.wait_ge(S["rxnT"][b], n)
                    if j is not None:
                        pe.wait_ge(S["x2"][b], j)
                    for j2 in range(2):
                        for k in range(KC):
                            last = mm(dst[b][:, j2 * P:(j2 + 1) * P], w1T[:, k * HID + j2 * P:k * HID + (j2 + 1) * P],
                                      xnT[b][:, k * P:(k + 1) * P], start=(k == 0), stop=(k == KC - 1))
                    last.then_inc(S["h_ps"][b], 1)

            def route_logits(j, n):
                for b in range(B):
                    if j is None and b == 0:
                        pe.wait_ge(aT, n - 1)
                    pe.wait_ge(S["hT"][b], n)
                    for j2 in range(2):
                        last = mm(Bk[b][:, HID:HID + NS], hT[b][:, j2 * P:(j2 + 1) * P], w2T[:, j2 * NS:(j2 + 1) * NS],
                                  start=(j2 == 0), stop=(j2 == 1))
                    last.then_inc(S["lg_ps"][b], 1)

            def route_slots(j, n, src):
                if j is None:
                    pe.wait_ge(sacc, n - 1)
                for b in range(B):
                    pe.wait_ge(S["al"][b], n)
                    al = alpha[:, b * NS:(b + 1) * NS]
                    mm(A[0][b * NS:(b + 1) * NS, :], al, src[b][:, :], start=True, stop=True)
                    last = mm(A[1][b * NS:(b + 1) * NS, 0:1], al, ones[:, 0:1], start=True, stop=True)
                last.then_inc(sl_ps, 1)
                tr(Bk[0][:, 3 * P:4 * P], alpha[:, :], ident[:, :]).then_inc(aT_ps, 1)

            def pass1_pe(n, odd, more):
                route_logits(None, n)
                if more:
                    route_xT(None, n + 1, C, rx[1 - odd])
                    route_hidden(None, n + 1, ST)
                route_slots(None, n, rx[odd])

            pe.wait_ge(ready, 1)
            route_xT(None, 1, C, rx[1])
            route_hidden(None, 1, ST)
            with pe.Fori(1, NT // 2) as i:
                pass1_pe(2 * i - 1, 1, True)
                pass1_pe(2 * i, 0, True)
            pass1_pe(NT - 1, 1, True)
            pass1_pe(NT, 0, False)
            mid(pe, 0)

            def h32(t, c, h, w, o, n):
                return t[CH * c:CH * (c + 1), h * w + o:h * w + o + n]

            def blocks(b, rhs):
                for h in range(H):
                    last = mm(AB[b][:, h * 2 * HD:(h + 1) * 2 * HD], bd[b][:, h * P:(h + 1) * P],
                              rhs[:, h * 2 * HD:(h + 1) * 2 * HD], start=True, stop=True)
                return last

            def project(b, m, dst):
                for k in range(KC):
                    last = mm(dst, xnT[b][:, k * P:(k + 1) * P], w_kvqg[:, (k * 4 + m) * D:(k * 4 + m + 1) * D],
                              start=(k == 0), stop=(k == KC - 1))
                return last

            def first_ffn(m, free, count):
                for b in range(B):
                    if free is not None:
                        pe.wait_ge(S[free][b], count)
                    pe.wait_ge(at_in, 16 * m)
                    mm(C[b][:, :], aT_in[b * NS:(b + 1) * NS, :], sv[b * NS:(b + 1) * NS, :], start=True, stop=True)\
                        .then_inc(S["ffn_ps"][b], 1)

            def first_xT(m):
                for b in range(B):
                    pe.wait_ge(S["xn"][b], m)
                    transpose_to(C[b], xn[b]).then_inc(S["xT_ps"][b], 1)

            def first_k(m):
                for b in range(B):
                    pe.wait_ge(S["xnT"][b], m)
                    project(b, 0, C[b][:, :]).then_inc(S["k_ps"][b], 1)

            def project_q(b, n):
                pe.wait_ge(S["kn"][b], n)
                project(b, 2, C[b][:, :]).then_inc(S["q_ps"][b], 1)

            def project_v(b, n):
                pe.wait_ge(S["q_ev"][b], n)
                project(b, 1, C[b][:, :]).then_inc(S["v_ps"][b], 1)

            def update(b, j):
                pe.wait_ge(S["scp"][b], NC * (j - 1) + 1)
                stand_alone(pe)
                for c in range(NC):
                    o = CH * ((c + 1) % NC)
                    for h in range(H):
                        mm(ST[b][o:o + CH, h * HD:(h + 1) * HD], h32(pk[b], c, h, 2 * HD, HD, HD),
                           h32(u[b], c, h, HD, 0, HD), start=(h == 0), stop=False, skip_group_check=True)

            def step_pe(n, j, m):
                if n is not None:
                    for b in range(B):
                        for k in range(KC):
                            last = mm(ab_place(b), xnT[b][:, k * P:(k + 1) * P], w_ab[:, k * 2 * H:(k + 1) * 2 * H],
                                      start=(k == 0), stop=(k == KC - 1))
                        last.then_inc(S["ab_ps"][b], 1)
                    project_q(0, n)
                    project_q(1, n)
                    if j is not None:
                        pe.wait_ge(sacc, j + NT - 1)
                        pe.wait_ge(aT, j + NT - 1)
                    for b in range(B):
                        pe.wait_ge(S["la"][b], both(n, b))
                        for m2, mask in enumerate((before, upto, after, chunk)):
                            last = mm(A[b][:, m2 * H:(m2 + 1) * H], mask[:, :], s(b, "la"), start=True, stop=True)
                        last.then_inc(S["cum_ps"][b], 1)
                    for b in range(B):
                        pe.wait_ge(S["rhsd"][b], both(n, b))
                        mm(Bk[b][:, :], after[:, :], dr[b][:, :], start=True, stop=True).then_inc(S["dec_ps"][b], 1)
                if j is not None:
                    pe.wait_ge(aT, j + NT - 1)
                    pe.wait_ge(y_in, 16 * B * NC * j)
                    for b in range(B):
                        pe.wait_ge(S["kp"][b], both(j, b))
                        if n is not None:
                            pe.wait_ge(S["e4"][b], n)
                            pe.wait_ge(S["draw"][b], n)
                        else:
                            pe.wait_ge(sacc, j + NT - 1)
                        blocks(b, vk[b]).then_inc(S["uw_ps"][b], 1)
                if n is not None:
                    project_v(0, n)
                if j is not None:
                    for b in range(B):
                        pe.wait_ge(S["uw"][b], both(j, b))
                        pe.wait_ge(S["kd"][b], both(j, b))
                        blocks(b, pk[b]).then_inc(S["gq_ps"][b], 1)
                for b in range(B):
                    if n is not None:
                        pe.wait_ge(S["kbd"][b], both(n, b))
                        if j is not None:
                            pe.wait_ge(S["qg"][b], both(j, b))
                        else:
                            pe.wait_ge(S["e4"][b], n)
                            pe.wait_ge(S["draw"][b], n)
                        blocks(b, kqT[b]).then_inc(S["gram_ps"][b], 1)
                if n is not None:
                    project_v(1, n)
                if j is not None:
                    update(0, j)
                    update(1, j)
                for b in range(B):
                    if j is not None:
                        if n is not None:
                            pe.wait_ge(S["v_ev"][b], n)
                        stand_alone(pe)
                        for h in range(H):
                            for c in range(NC):
                                last = mm(h32(C[b], c, h, HD, 0, HD), h32(pk[b], c, h, 2 * HD, 0, CH),
                                          h32(u[b], c, h, HD, 0, HD), start=(h == 0), stop=False, skip_group_check=True)
                        last.then_inc(S["y1_ps"][b], 1)

                def project_g(first, last):
                    if n is None:
                        return
                    for q in range(first, last):
                        b, k = q // KC, q % KC
                        if k == 0:
                            pe.wait_ge(S["pt"][b], both(n, b))
                        ins = mm(Bk[b][:, :], xnT[b][:, k * P:(k + 1) * P], w_kvqg[:, (k * 4 + 3) * D:(k * 4 + 4) * D],
                                 start=(k == 0), stop=(k == KC - 1))
                        if k == KC - 1:
                            ins.then_inc(S["g_ps"][b], 1)
                G_UPTO = (4, 6, 8, 8, 8)
                project_g(0, 4)
                for c in range(NC):
                    if j is not None:
                        for b in range(B):
                            if c == 0:
                                pe.wait_ge(S["qg"][b], both(j, b))
                            pe.wait_ge(S["scp"][b], NC * (j - 1) + c + 1)
                            stand_alone(pe)
                            o = CH * ((c + 1) % NC)
                            for h in range(H):
                                last = mm(ST[b][o:o + CH, h * HD:(h + 1) * HD], h32(qg[b], c, h, 2 * HD, HD, HD),
                                          h32(ss[b], c, h, HD, 0, HD), start=False, stop=True, skip_group_check=True)
                            last.then_inc(S["s_ps"][b], 1)
                            for h in range(H):
                                last = mm(h32(C[b], c, h, HD, 0, HD), h32(qg[b], c, h, 2 * HD, 0, CH),
                                          h32(ss[b], c, h, HD, 0, HD), start=False, stop=True, skip_group_check=True)
                            if c == NC - 1:
                                last.then_inc(S["y_ps"][b], 1)
                    project_g(G_UPTO[c], G_UPTO[c + 1])
                if m is not None:
                    first_ffn(m, "v_ev" if j is None else "yq", n if j is None else j)
                if j is None:
                    for b in range(B):
                        pe.wait_ge(S["gate"][b], n)
                if j is not None:
                    for b in range(B):
                        if n is not None:
                            pe.wait_ge(S["pt"][b], both(n, b))
                        pe.wait_ge(S["y3"][b], j)
                        transpose_to(A[b], qs[b]).then_inc(S["yT_ps"][b], 1)
                    for b in range(B):
                        pe.wait_ge(S["yT"][b], j)
                        if n is not None:
                            pe.wait_ge(S["gate"][b], n)
                        for k in range(KC):
                            last = mm(Bk[b][:, :], xnT[b][:, k * P:(k + 1) * P], w_out[:, k * D:(k + 1) * D],
                                      start=(k == 0), stop=(k == KC - 1))
                        last.then_inc(S["wo_ps"][b], 1)
                if j is not None:
                    for b in range(B):
                        route_xT(j, j + NT, A, qs, (b,))
                        route_hidden(j, j + NT, Bk, (b,))
                    route_logits(j, j + NT)
                if m is not None:
                    first_xT(m)
                    first_k(m)
                if j is not None:
                    route_slots(j, j + NT, qs)

            first_ffn(1, None, 0)
            first_xT(1)
            first_k(1)
            step_pe(1, None, 2)
            with pe.Fori(1, NT - 1) as i:
                step_pe(i + 1, i, i + 2)
            step_pe(NT, NT - 1, None)
            step_pe(None, NT, None)
            mid(pe, 1)

            with pe.Fori(NT + 1, 2 * NT + 1) as i:
                for b in range(B):
                    pe.wait_ge(at_in, 16 * i)
                    pe.wait_ge(S["x1"][b], i - 1)
                    mm(C[b][:, :], aT_in[b * NS:(b + 1) * NS, :], sv[b * NS:(b + 1) * NS, :], start=True, stop=True)\
                        .then_inc(S["ffn_ps"][b], 1)

        @block.scalar
        def _(sc):
            act = nc.scalar.activation
            own = Own(sc, act_own)
            for j in range(0, NJ):
                src, rows, cols, (kind, r) = jobs[j]
                sc.wait_ge(wt_ps, j + 1)
                if kind == "whh" and r >= 2:
                    sc.wait_ge(gh_ps, r - 1)
                view = tps[j % 4][:, 0:cols * rows].rearrange("p (k n) -> p k n", k=cols)
                if kind in ("wo", "wih"):
                    for k in range(KC):
                        to = woT_at(k)[:, r * P:(r + 1) * P] if kind == "wo" else wihT_at(k, r // 4)[:, r % 4 * P:(r % 4 + 1) * P]
                        last = act(to, view[:, k, :], ACT.Copy)
                    last.then_inc(wt_ev, 1)
                else:
                    act(dest(j), view, ACT.Copy).then_inc(wt_ev, 1)

            def move(dst, src, n, ps, done):
                sc.wait_ge(ps, n)
                act(dst, src, ACT.Copy).then_inc(done, 1)

            def route_move_x(n, src, bs=range(B)):
                for b in bs:
                    move(xnT[b][:, :], src[b][:, :], n, S["rxT_ps"][b], S["rxnT"][b])

            def route_gelu(n, src):
                for b in range(B):
                    sc.wait_ge(S["h_ps"][b], n)
                    for j in range(2):
                        last = act(hT[b][:, j * P:(j + 1) * P], src[b][:, j * P:(j + 1) * P], ACT.Gelu, bias=h_bias[:, j:j + 1])
                    last.then_inc(S["hT"][b], 1)

            def route_exp(n):
                for b in range(B):
                    sc.wait_ge(S["top"][b], n)
                    act(lgt[b][:, 2 * NS:3 * NS], lgt[b][:, 0:NS], ACT.Exp, bias=s(b, "negm")).then_inc(S["ex"][b], 1)

            def route_aT(n):
                sc.wait_ge(aT_ps, n)
                sc.wait_ge(at_st, 16 * (n - 1))
                act(aT_out[:, :], Bk[0][:, 3 * P:4 * P], ACT.Copy).then_inc(aT, 1)

            sc.wait_ge(ready, 1)
            route_move_x(1, C)
            route_gelu(1, ST)
            with sc.Fori(1, NT) as i:
                route_move_x(i + 1, C)
                route_exp(i)
                route_gelu(i + 1, ST)
                route_aT(i)
            route_exp(NT)
            route_aT(NT)
            mid(sc, 0)

            def move_first(m):
                for b in range(B):
                    move(xnT[b][:, :], C[b][:, :], m, S["xT_ps"][b], S["xnT"][b])

            def square_k(m):
                for b in range(B):
                    sc.wait_ge(S["k_ps"][b], m)
                    act(scr[b][:, :], C[b][:, :], ACT.Square).then_inc(S["ksq"][b], 1)

            def move_state(j, b, c):
                sc.wait_ge(S["s_ps"][b], NC * (j - 1) + c)
                act(ss[b][CH * c:CH * (c + 1), :], ST[b][CH * c:CH * (c + 1), :], ACT.Copy).then_inc(S["scp"][b], 1)

            def step_act(n, j, m):
                if j is not None:
                    for b in range(B):
                        move_state(j, b, 0)
                if n is not None:
                    for b in range(B):
                        sc.wait_ge(S["zi"][b], n)
                        act(s(b, "ez"), s(b, "zi"), ACT.Exp).then_inc(S["ez"][b], 1)
                    for b in range(B):
                        sc.wait_ge(S["ez"][b], both(n, b))
                        act(s(b, "ln"), s(b, "ez")[:, 0:H], ACT.Ln, bias=1.0).then_inc(S["ln"][b], 1)

                    def move_q(b):
                        sc.wait_ge(S["q_ps"][b], n)
                        act(qs[b][:, :], C[b][:, :], ACT.Copy)
                        sc.wait_ge(S["ssk"][b], n)
                        act(scr[b][:, :], C[b][:, :], ACT.Square).then_inc(S["q_ev"][b], 1)
                    move_q(0)
                    move_q(1)
                    for b in range(B):
                        sc.wait_ge(S["cum_ps"][b], both(n, b))
                        act(s(b, "e4"), A[b][:, 0:4 * H], ACT.Exp).then_inc(S["e4"][b], 1)
                    for b in range(B):
                        sc.wait_ge(S["dec_ps"][b], n)
                        act(dr[b][:, :], Bk[b][:, :], ACT.Exp).then_inc(S["draw"][b], 1)

                def move_v(b):
                    if n is None:
                        return
                    if j is not None:
                        sc.wait_ge(S["uw_ps"][b], both(j, b))
                    move(heads(vk[b], 2)[:, :, 0:HD], C[b][:, :].rearrange("p (h e) -> p h e", h=H), n,
                         S["v_ps"][b], S["v_ev"][b])
                if j is not None:
                    for b in range(B):
                        sc.wait_ge(S["uw_ps"][b], both(j, b))
                        for c in range(NC):
                            act(diagonal(b, c), heads(AB[b], 2)[CH * c:CH * (c + 1), :, HD:2 * HD], ACT.Copy)
                        act(heads(u[b]), heads(AB[b], 2)[:, :, 0:HD], ACT.Copy).then_inc(S["uw"][b], 1)
                move_v(0)
                if n is not None:
                    for b in range(B):
                        sc.wait_ge(S["kqt"][b], both(n, b))
                        if j is not None:
                            sc.wait_ge(S["gq_ps"][b], both(j, b))
                        for c in range(NC):
                            last = act(diagonal(b, c), heads(kqT[b], 2)[CH * c:CH * (c + 1), :, 0:HD], ACT.Copy)
                        last.then_inc(S["kbd"][b], 1)
                move_v(1)

                def tanh_g(b):
                    if n is not None:
                        sc.wait_ge(S["g_ps"][b], n)
                        sc.wait_ge(S["qe"][b], both(n, b))
                        act(scr[b][:, :], Bk[b][:, :], ACT.Tanh, scale=0.5).then_inc(S["tanh"][b], 1)
                for c in range(1, NC):
                    if j is not None:
                        for b in range(B):
                            move_state(j, b, c)
                    if c >= NC - B:
                        tanh_g(c - (NC - B))
                if j is not None:
                    for b in range(B):
                        sc.wait_ge(S["yq"][b], j)
                        act(u[b][:, :], kn[b][:, :], ACT.Square, accum_out=s(b, "ys")).then_inc(S["ysq"][b], 1)
                    for b in range(B):
                        move(xnT[b][:, :], A[b][:, :], j, S["yT_ps"][b], S["yT"][b])
                    for b in range(B):
                        sc.wait_ge(S["x2"][b], j)
                        sc.dma_start(x2_dram[b, bass.ds(j - 1, 1), :, :].rearrange("o p d -> (o p) d"), xh[b][:, :])\
                            .then_inc(x2_st[b], 16)
                        route_move_x(j + NT, A, (b,))
                    route_gelu(j + NT, Bk)
                if m is not None:
                    move_first(m)
                if j is not None:
                    route_exp(j + NT)
                if m is not None:
                    square_k(m)
                if j is not None:
                    route_aT(j + NT)

            sc.wait_ge(wih_st, 16 * (len(wih_region) + 1))
            move_first(1)
            square_k(1)
            step_act(1, None, 2)
            with sc.Fori(1, NT - 1) as i:
                step_act(i + 1, i, i + 2)
            step_act(NT, NT - 1, None)
            step_act(None, NT, None)
            mid(sc, 1)

        @block.gpsimd
        def _(pl):
            g = nc.gpsimd
            own = Own(pl, pool_own)
            own(g.memset(ident[:, :], 0.0))
            g.affine_select(out=ident[:, :], in_=ident[:, :], compare_op=ALU.not_equal, fill=1.0, base=0,
                            pattern=[[-1, P]], channel_multiplier=1).then_inc(set_pool, 1)
            g.iota(qa[0][:, 0:P].bitcast(i32), pattern=[[0, P]], base=0, channel_multiplier=1)
            g.iota(gateh[0][:, 0:P].bitcast(i32), pattern=[[1, P]], base=0, channel_multiplier=0).then_inc(set_pool, 1)

            def power(dst, a, n):
                return g.tensor_tensor(dst, a, half[:, 0:n], ALU.pow)

            def rstd(b, n, bn, rs):
                pl.wait_ge(S[bn][b], n)
                stand_alone(pl)
                own(g.tensor_scalar(s(b, "vs"), s(b, "mv")[:, 1:2], 1e-5, None, ALU.add))
                power(s(b, "rstd"), s(b, "vs"), 1).then_inc(S[rs][b], 1)

            pl.wait_ge(ready, 1)
            with pl.Fori(1, NT + 1) as i:
                own.base, own.n = 1 + 2 * (i - 1), 0
                for b in range(B):
                    rstd(b, i, "rbn", "rrs")
                assert own.n == 2
            own.base, own.n = 0, 1 + 2 * NT

            def hold(dst, src):
                return g.tensor_copy(dst, src)

            def step_pool(n, j, m):
                if n is not None:
                    for b in range(B):
                        pl.wait_ge(S["la"][b], both(n, b))
                        g.tensor_tensor(heads(dr[b]), bc(s(b, "la")), allheads(tri[:, :]), ALU.mult).then_inc(S["rhsd"][b], 1)
                    for b in range(B):
                        pl.wait_ge(S["ssq"][b], n)
                        power(s(b, "rq"), s(b, "ssq"), H).then_inc(S["rq"][b], 1)
                    pl.wait_ge(y_out, 16 * (n - 1))
                    stand_alone(pl)
                    own(g.memset(yblk[:, :], 0.0))
                    stand_alone(pl)
                    g.memset(yblk[:, 0:CH * CH:CH + 1], 1.0).then_inc(eye_set, 1)
                    for b in range(B):
                        pl.wait_ge(S["draw"][b], n)
                        own(g.tensor_tensor(heads(dr[b]), heads(dr[b]), allheads(tri[:, :]), ALU.mult))
                        pl.wait_ge(S["be"][b], both(n, b))
                        stand_alone(pl)
                        g.memset(D33[b][:, :, 0:1], 0.0)
                        g.tensor_tensor(D33[b][:, :, 1:HD + 1], heads(dr[b]), bc(s(b, "be")), ALU.mult).then_inc(S["d33"][b], 1)
                    for b in range(B):
                        if j is not None:
                            pl.wait_ge(S["qg"][b], both(j, b))
                        pl.wait_ge(S["e4"][b], n)
                        g.tensor_tensor(heads(qa[b], 2)[:, :, HD:2 * HD], bc(s(b, "e4")[:, 3 * H:4 * H]),
                                        allheads(eye32[:, :]), ALU.mult).then_inc(S["qaT"][b], 1)
                    for b in range(B):
                        own(g.tensor_tensor(s(b, "bel"), s(b, "be"), s(b, "e4")[:, 2 * H:3 * H], ALU.mult))
                        if j is not None:
                            pl.wait_ge(S["y1_ps"][b], both(j, b))
                        g.tensor_tensor(heads(pk[b], 2)[:, :, HD:2 * HD], heads(kn[b]), bc(s(b, "bel")), ALU.mult)\
                            .then_inc(S["kd"][b], 1)
                    for b in range(B):
                        if j is not None:
                            pl.wait_ge(S["yq"][b], j)
                            stand_alone(pl)
                        hold(s(b, "rqh"), s(b, "rq")).then_inc(S["rqh"][b], 1)
                if j is not None:
                    for b in range(B):
                        pl.wait_ge(S["yv"][b], both(j, b))
                        power(s(b, "yr"), s(b, "yv"), 1).then_inc(S["yrs"][b], 1)
                if n is not None:
                    for b in range(B):
                        if j is not None:
                            pl.wait_ge(S["y3"][b], j)
                        pl.wait_ge(S["gate"][b], n)
                        stand_alone(pl)
                        hold(gateh[b][:, :], gate[b][:, :]).then_inc(S["ghold"][b], 1)
                if j is not None:
                    for b in range(B):
                        rstd(b, j + NT, "rbn", "rrs")
                if n is not None:
                    for b in range(B):
                        if j is not None:
                            pl.wait_ge(x2_st[b], 16 * j)
                            pl.wait_ge(S["rxn"][b], j + NT)
                        stand_alone(pl)
                        hold(xh[b][:, :], xc[b][:, :]).then_inc(S["xhold"][b], 1)
                if m is not None:
                    for b in range(B):
                        rstd(b, m, "bn", "rs")
                    over_k(m)

            def over_k(m):
                for b in range(B):
                    pl.wait_ge(S["ssk"][b], m)
                    power(s(b, "rk"), s(b, "ssk"), H).then_inc(S["rk"][b], 1)

            for b in range(B):
                rstd(b, 1, "bn", "rs")
            over_k(1)
            step_pool(1, None, 2)
            PER = 1 + 2 * 4
            base = own.n
            with pl.Fori(1, NT - 1) as i:
                own.base, own.n = base + PER * (i - 1), 0
                step_pool(i + 1, i, i + 2)
                assert own.n == PER
            own.base, own.n = 0, base + PER * (NT - 2)
            step_pool(NT, NT - 1, None)
            step_pool(None, NT, None)

        @block.vector
        def _(ve):
            v = nc.vector
            tt, ts, stt = v.tensor_tensor, v.tensor_scalar, v.scalar_tensor_tensor
            own = Own(ve, dve_own)
            ve.wait_ge(ld, LD)
            own(ts(hs[:, :], hs[:, :], ssc, None, ALU.mult))
            own(v.memset(aT_in[:, :], 1.0 / NS))
            ve.nop().then_inc(set_dve, 1)
            v.memset(ones[:, :], 1.0)
            v.memset(half[:, :], -0.5)
            own(v.memset(slotacc[:, :], 0.0))
            own(stt(sm[0][:, 2:3], taut, -1.0, taut, ALU.mult, ALU.max))
            own(ts(sm[0][:, 3:4], sm[0][:, 2:3], 0.1, None, ALU.add))
            own(v.reciprocal(itau[:, :], sm[0][:, 3:4]))
            own(ts(b2s[:, :], b2s[:, :], itau[:, :], None, ALU.mult))
            for k in range(KC):
                own(ts(w_out[:, k * D:(k + 1) * D], w_out[:, k * D:(k + 1) * D], gcol[:, k:k + 1], 0.5, ALU.mult, ALU.mult))
            own(tt(gh[:, 0:2 * D], bih_t[0][:, :], bhh_t[0][:, :], ALU.add))
            own(v.tensor_copy(gh[:, 2 * D:3 * D], bhh_t[1][:, :]))
            own(v.tensor_copy(bih_n[:, :], bih_t[1][:, :]))
            for k in range(KC):
                own(ts(xin[0][:, k * P:(k + 1) * P], ones[:, :], bv_c[:, k:k + 1], None, ALU.mult))
            pi, fi = qa[0][:, 0:P].bitcast(i32), gateh[0][:, 0:P].bitcast(i32)
            u, w = (qa[0][:, P * m:P * (m + 1)].bitcast(i32) for m in (1, 2))
            ve.wait_ge(set_pool, 2)
            own(tt(u, pi, fi, ALU.bitwise_xor))
            own(ts(w, u, 5, None, ALU.logical_shift_right))
            own(ts(chunk[:, :], w, 0, None, ALU.is_equal))
            own(tt(before[:, :], pi, fi, ALU.is_lt))
            own(tt(before[:, :], before[:, :], chunk[:, :], ALU.mult))
            own(tt(upto[:, :], pi, fi, ALU.is_le))
            own(tt(upto[:, :], upto[:, :], chunk[:, :], ALU.mult))
            own(tt(after[:, :], chunk[:, :], upto[:, :], ALU.subtract))
            own(ts(w, pi, 31, None, ALU.bitwise_and))
            own(tt(tri[:, :], w[:, 0:CH], fi[:, 0:CH], ALU.is_le))
            own(tt(u[:, 0:CH], w[:, 0:CH], fi[:, 0:CH], ALU.bitwise_xor))
            own(ts(eye32[:, :], u[:, 0:CH], 0, None, ALU.is_equal))
            ve.nop().then_inc(set_dve, 1)
            for r in range(12):
                ve.wait_ge(gh_ps, r + 1)
                ins = tt(gh[:, r * P:(r + 1) * P], gh[:, r * P:(r + 1) * P], C[r % 2][:, 0:P], ALU.add)
                ins.then_inc(gh_ev, 1)
            ve.wait_ge(set_pe, 1)
            own(v.tensor_copy(mean_t[:, :], C[0][:, :]))
            for j in range(2):
                own(tt(prod_t[:, :], mean_t[:, :], w1b[j], ALU.mult))
                own(v.tensor_reduce(sm[0][:, 4 + j:5 + j], prod_t[:, :], AX.X, ALU.add))
            own(tt(h_bias[:, :], sm[0][:, 4:6], b1c[:, 0:2], ALU.add))
            for k in range(KC):
                ve.wait_ge(set_pe, 2 + k)
                ins = v.tensor_copy(voT[:, k * D:(k + 1) * D], ST[k % 2][:, :])
                ins.then_inc(set_dve, 1)
            ve.wait_ge(set_dve, 2 + KC)
            v.memset(ST[0][:, :], 0.0)
            own(v.memset(ST[1][:, :], 0.0))
            ve.nop().then_inc(set_dve, 1)
            ve.wait_ge(set_pe, 6)
            own(tt(bvo[:, :], C[0][:, :], bo_t[:, :], ALU.add))
            own(ts(bvo[:, :], bvo[:, :], 0.5, None, ALU.mult))
            ve.wait_ge(ld, LD + 16 * 6)
            ve.wait_ge(wt_ev, NJ)
            ve.nop().then_inc(ready, 1)

            def moments(b, src, bn):
                own(v.bn_stats(s(b, "stats"), src))
                stand_alone(ve)
                v.bn_aggr(s(b, "mv"), s(b, "stats")).then_inc(bn, 1)

            def route_moments(n, src, b):
                if src is xin:
                    ve.wait_ge(xin_in[b], 16 * n)
                else:
                    ve.wait_ge(S["x2"][b], n - NT)
                stand_alone(ve)
                moments(b, src[b][:, :], S["rbn"][b])

            def route_normalise(n, src, dst, b):
                ve.wait_ge(S["rrs"][b], n)
                ts(dst[b][:, :], src[b][:, :], s(b, "mv")[:, 0:1], s(b, "rstd"), ALU.subtract, ALU.mult)\
                    .then_inc(S["rxn"][b], 1)

            def route_top(n):
                for b in range(B):
                    lg, rep = lgt[b][:, 0:NS], lgt[b][:, NS:2 * NS]
                    ve.wait_ge(S["lg_ps"][b], n)
                    own(stt(lg, Bk[b][:, HID:HID + NS], itau[:, :], b2s[:, :], ALU.mult, ALU.add))
                    stand_alone(ve)
                    own(v.max(s(b, "top"), lg))
                    ts(s(b, "negm"), s(b, "top")[:, 0:1], -1.0, None, ALU.mult).then_inc(S["top"][b], 1)
                    stand_alone(ve)
                    own(v.match_replace(out=rep, in_to_replace=s(b, "top"), in_values=lg, imm_value=BIG))
                    own(tt(rep, lg, rep, ALU.not_equal))

            def route_weights(n):
                for b in range(B):
                    e, al = lgt[b][:, 2 * NS:3 * NS], alpha[:, b * NS:(b + 1) * NS]
                    ve.wait_ge(S["ex"][b], n)
                    own(tt(lgt[b][:, 0:NS], e, lgt[b][:, NS:2 * NS], ALU.mult))
                    own(v.tensor_reduce(s(b, "den"), lgt[b][:, 0:NS], AX.X, ALU.add))
                    own(v.reciprocal(s(b, "rden"), s(b, "den")))
                    ve.wait_ge(aT_ps, n - 1)
                    ts(al, lgt[b][:, 0:NS], s(b, "rden"), None, ALU.mult).then_inc(S["al"][b], 1)

            def route_sums(n):
                ve.wait_ge(sl_ps, n)
                tt(slotacc[:, 0:D], slotacc[:, 0:D], A[0][:, :], ALU.add)
                tt(slotacc[:, D:D + 1], slotacc[:, D:D + 1], A[1][:, 0:1], ALU.add).then_inc(sacc, 1)

            def pass1_dve(n, odd, more):
                route_top(n)
                if more:
                    for b in range(B):
                        route_moments(n + 2, xin, b)
                route_weights(n)
                route_sums(n)
                if more:
                    for b in range(B):
                        route_normalise(n + 2, xin, rx[odd], b)

            ROUTE = 2 * (1 + 1 + 1 + 1 + 1 + 3)
            for n in (1, 2):
                for b in range(B):
                    if n == 2:
                        ve.wait_ge(S["rxn"][b], 1)
                    route_moments(n, xin, b)
                    route_normalise(n, xin, rx[n % 2], b)
            base0 = own.n
            with ve.Fori(1, NT // 2) as i:
                own.base, own.n = base0 + 2 * ROUTE * (i - 1), 0
                pass1_dve(2 * i - 1, 1, True)
                pass1_dve(2 * i, 0, True)
                assert own.n == 2 * ROUTE
            own.base, own.n = 0, base0 + 2 * ROUTE * (NT // 2 - 1)
            pass1_dve(NT - 1, 1, False)
            pass1_dve(NT, 0, False)

            def mid_dve_part(m):
                o_pe, o_act = 4 * m, 5 * m
                ve.wait_ge(sacc, NT * (m + 1))
                own(ts(s(0, "den"), slotacc[:, D:D + 1], 1e-8, None, ALU.add))
                own(v.reciprocal(s(0, "rden"), s(0, "den")))
                own(ts(ht[:, :], slotacc[:, 0:D], s(0, "rden"), None, ALU.mult))
                own(v.memset(slotacc[:, :], 0.0))
                ve.nop().then_inc(mid_dve, 1)
                ve.wait_ge(mid_pe, o_pe + 2)
                tt(gr[:, :], A[0][:, :], gh[:, 0:D], ALU.add).then_inc(mid_dve, 1)
                tt(gz[:, :], A[1][:, :], gh[:, D:2 * D], ALU.add).then_inc(mid_dve, 1)
                own(tt(gn[:, :], C[0][:, :], bih_n[:, :], ALU.add))
                ve.wait_ge(mid_act, o_act + 2)
                own(tt(gr[:, :], gr[:, :], gh[:, 2 * D:3 * D], ALU.mult))
                tt(gn[:, :], gn[:, :], gr[:, :], ALU.add).then_inc(mid_dve, 1)
                ve.wait_ge(mid_act, o_act + 4)
                own(tt(gr[:, :], hs[:, :], gn[:, :], ALU.subtract))
                own(tt(gz[:, :], gz[:, :], gr[:, :], ALU.mult))
                own(tt(ht[:, :], gn[:, :], gz[:, :], ALU.add))
                ve.nop().then_inc(mid_dve, 2)
                ve.wait_ge(mid_pe, o_pe + 4)
                stt(sv[:, :], Bk[1][:, :], 0.5, bvo[:, :], ALU.mult, ALU.add).then_inc(mid_dve, 1)
            mid_dve_part(0)

            def first_x1(m, held):
                for b in range(B):
                    ve.wait_ge(S["ffn_ps"][b], m)
                    ve.wait_ge(xin_in[b], 16 * (m + NT))
                    if held:
                        ve.wait_ge(S["xhold"][b], both(m - 1, b))
                    tt(xc[b][:, :], xin[b][:, :], C[b][:, :], ALU.add).then_inc(S["x1"][b], 1)
                    ve.wait_ge(S["x1"][b], m)
                    moments(b, xc[b][:, :], S["bn"][b])
                for b in range(B):
                    ve.wait_ge(S["rs"][b], both(m, b))
                    ts(xn[b][:, :], xc[b][:, :], s(b, "mv")[:, 0:1], s(b, "rstd"), ALU.subtract, ALU.mult)\
                        .then_inc(S["xn"][b], 1)

            def invert(n, first, last):
                if n is None:
                    return
                if first == 0:
                    ve.wait_ge(eye_set, n)
                    ve.wait_ge(n_in, 16 * n)
                N = nblk[:, :].rearrange("p (s t) -> p s t", s=CH)
                Y = yblk[:, :].rearrange("p (r t) -> p r t", r=CH)
                for s_ in range(first, last):
                    rows, cols = s_ + 1, CH - 1 - s_
                    o = outer[:, 0:rows * cols].rearrange("p (r t) -> p r t", r=rows)
                    own(tt(o, Y[:, 0:rows, s_:s_ + 1].to_broadcast([P, rows, cols]),
                           N[:, s_:s_ + 1, s_ + 1:CH].to_broadcast([P, rows, cols]), ALU.mult))
                    ins = tt(Y[:, 0:rows, s_ + 1:CH], Y[:, 0:rows, s_ + 1:CH], o, ALU.subtract)
                    if s_ < CH - 2:
                        own(ins)
                    else:
                        ins.then_inc(inv, 1)

            def square_sums(m, b):
                ve.wait_ge(S["ksq"][b], both(m, b))
                own(v.tensor_reduce(s(b, "ssk"), heads(scr[b]), AX.X, ALU.add))
                ts(s(b, "ssk"), s(b, "ssk"), 1e-24, None, ALU.max).then_inc(S["ssk"][b], 1)

            def first_k(m):
                for b in range(B):
                    ve.wait_ge(S["rk"][b], both(m, b))
                    tt(heads(kn[b]), C[b][:, :].rearrange("p (h e) -> p h e", h=H), bc(s(b, "rk")), ALU.mult)\
                        .then_inc(S["kn"][b], 1)
                for b in range(B):
                    ve.wait_ge(S["kn"][b], m)
                    v.transpose(heads(kqT[b], 2)[:, :, 0:HD], heads(kn[b]))

            def step_dve(n, j, m):
                if n is not None:
                    for b in range(B):
                        ve.wait_ge(S["ab_ps"][b], n)
                    for b in range(B):
                        own(tt(s(b, "ab"), ab_place(b), ab_bias[:, :], ALU.add))
                        za, zb = s(b, "ab")[:, 0:H], s(b, "ab")[:, H:2 * H]
                        stt(s(b, "zi")[:, 0:H], za, -1.0, za, ALU.mult, ALU.min)
                        ts(s(b, "zi")[:, H:2 * H], zb, -1.0, 80.0, ALU.mult, ALU.min).then_inc(S["zi"][b], 1)
                    for b in range(B):
                        ve.wait_ge(S["ln"][b], both(n, b))
                        stt(s(b, "la"), s(b, "ab")[:, 0:H], 0.0, s(b, "ln"), ALU.min, ALU.subtract).then_inc(S["la"][b], 1)
                        own(ts(s(b, "opb"), s(b, "ez")[:, H:2 * H], 1.0, None, ALU.add))
                        v.reciprocal(s(b, "be"), s(b, "opb")).then_inc(S["be"][b], 1)
                if n is not None:
                    for b in range(B):
                        ve.wait_ge(S["q_ev"][b], n)
                        own(v.tensor_reduce(s(b, "ssq"), heads(scr[b]), AX.X, ALU.add))
                        ts(s(b, "ssq"), s(b, "ssq"), 1e-24, None, ALU.max).then_inc(S["ssq"][b], 1)
                        v.transpose(heads(kqT[b], 2)[:, :, HD:2 * HD], heads(qs[b])).then_inc(S["kqt"][b], 1)
                if j is not None:
                    for b in range(B):
                        ve.wait_ge(S["gq_ps"][b], both(j, b))
                        ve.wait_ge(S["qaT"][b], both(j, b))
                        tt(qg[b][:, :], qa[b][:, :], AB[b][:, :], ALU.subtract).then_inc(S["qg"][b], 1)
                if n is not None:
                    for b in range(B):
                        ve.wait_ge(S["e4"][b], n)
                        if j is not None:
                            ve.wait_ge(S["uw_ps"][b], both(j, b))
                        tt(heads(vk[b], 2)[:, :, HD:2 * HD], heads(kn[b]), bc(s(b, "e4")[:, 0:H]), ALU.mult)\
                            .then_inc(S["kp"][b], 1)
                    for b in range(B):
                        if j is not None:
                            ve.wait_ge(S["qg"][b], both(j, b))
                        own(tt(heads(scr[b]), heads(qs[b]), bc(s(b, "e4")[:, H:2 * H]), ALU.mult))
                        v.transpose(heads(qa[b], 2)[:, :, 0:HD], heads(scr[b])).then_inc(S["qe"][b], 1)
                    for b in range(B):
                        ve.wait_ge(S["gram_ps"][b], n)
                        ve.wait_ge(S["d33"][b], n)
                        tt(heads(nn[b]), AB[b][:, :].rearrange("p (h e) -> p h e", h=H)[:, :, 0:HD],
                           D33[b][:, :, 0:HD], ALU.mult).then_inc(S["nn"][b], 1)
                invert(n, 0, 8)
                if n is not None:
                    for b in range(B):
                        if j is not None:
                            ve.wait_ge(S["y1_ps"][b], both(j, b))
                        tt(heads(pk[b], 2)[:, :, 0:HD], AB[b][:, :].rearrange("p (h e) -> p h e", h=H)[:, :, HD:2 * HD],
                           D33[b][:, :, 1:HD + 1], ALU.mult).then_inc(S["pt"][b], 1)
                invert(n, 8, 15)
                for b in range(B):
                    if n is not None:
                        ve.wait_ge(S["tanh"][b], both(n, b))
                        if j is not None:
                            ve.wait_ge(S["ghold"][b], both(n - 1, b))
                        stt(gate[b][:, :], scr[b][:, :], 1.0, Bk[b][:, :], ALU.add, ALU.mult).then_inc(S["gate"][b], 1)
                    if b == 0:
                        invert(n, 15, 18)
                if j is not None:
                    for b in range(B):
                        ve.wait_ge(S["y_ps"][b], j)
                        ve.wait_ge(S["rqh"][b], both(j, b))
                        if n is not None:
                            ve.wait_ge(S["kd"][b], both(n, b))
                        tt(heads(kn[b]), C[b][:, :].rearrange("p (h e) -> p h e", h=H), bc(s(b, "rqh")), ALU.mult)\
                            .then_inc(S["yq"][b], 1)
                    for b in range(B):
                        ve.wait_ge(S["ysq"][b], both(j, b))
                        ts(s(b, "yv"), s(b, "ys"), 1.0 / D, 1e-5, ALU.mult, ALU.add).then_inc(S["yv"][b], 1)
                    for b in range(B):
                        ve.wait_ge(S["yrs"][b], both(j, b))
                        ve.wait_ge(S["ghold"][b], both(j, b))
                        stt(qs[b][:, :], kn[b][:, :], s(b, "yr"), gateh[b][:, :], ALU.mult, ALU.mult).then_inc(S["y3"][b], 1)
                invert(n, 18, 25)
                if j is not None:
                    for b in range(B):
                        ve.wait_ge(S["wo_ps"][b], both(j, b))
                        ve.wait_ge(S["xhold"][b], both(j, b))
                        tt(xh[b][:, :], xh[b][:, :], Bk[b][:, :], ALU.add).then_inc(S["x2"][b], 1)
                        route_moments(j + NT, xh, b)
                        route_normalise(j + NT, xh, qs, b)
                if m is not None:
                    first_x1(m, True)
                if j is not None:
                    route_top(j + NT)
                invert(n, 25, 27)
                if j is not None:
                    route_weights(j + NT)
                if m is not None:
                    square_sums(m, 0)
                invert(n, 27, CH - 1)
                if m is not None:
                    square_sums(m, 1)
                if j is not None:
                    route_sums(j + NT)
                if m is not None:
                    first_k(m)

            ve.wait_ge(wih_st, 16 * (len(wih_region) + 1))
            for b in range(B):
                v.memset(bd[b][:, :], 0.0)
                own(v.memset(ST[b][:, :], 0.0))
            first_x1(1, False)
            for b in range(B):
                square_sums(1, b)
            first_k(1)
            step_dve(1, None, 2)
            PER = ROUTE + 2 * 6 + 2 * (CH - 1) - 1
            base1 = own.n
            with ve.Fori(1, NT - 1) as i:
                own.base, own.n = base1 + PER * (i - 1), 0
                step_dve(i + 1, i, i + 2)
                assert own.n == PER, own.n
            own.base, own.n = 0, base1 + PER * (NT - 2)
            step_dve(NT, NT - 1, None)
            step_dve(None, NT, None)
            mid_dve_part(1)

            with ve.Fori(NT + 1, 2 * NT + 1) as i:
                for b in range(B):
                    ve.wait_ge(S["ffn_ps"][b], i)
                    ve.wait_ge(xin_in[b], 16 * (i + NT))
                    ve.wait_ge(x2_st[b], 16 * (i - 1))
                    tt(xc[b][:, :], xin[b][:, :], C[b][:, :], ALU.add).then_inc(S["x1"][b], 1)


_INS = ['L0_attn_x', 'L0_attn_Wq', 'L0_attn_Wk', 'L0_attn_Wv', 'L0_attn_Wa', 'L0_attn_ba', 'L0_attn_Wb', 'L0_attn_bb',
        'L0_attn_Wg', 'L0_attn_Wo', 'L0_attn_g_norm', 'L0_ffn_slot_init', 'L0_ffn_slot_scale', 'L0_ffn_w1', 'L0_ffn_b1',
        'L0_ffn_w2', 'L0_ffn_b2', 'L0_ffn_gru_wih', 'L0_ffn_gru_whh', 'L0_ffn_gru_bih', 'L0_ffn_gru_bhh', 'L0_ffn_wv',
        'L0_ffn_bv', 'L0_ffn_wo', 'L0_ffn_bo', 'L0_ffn_tau']
_OUTS = [((B, T, D), 'float32')]


def kernel(**inputs):
    import numpy as _np
    import concourse.bacc as _bacc
    from concourse import mybir as _mybir
    from concourse.bass_utils import run_bass_kernel_spmd as _run

    nc = _bacc.Bacc("TRN2", target_bir_lowering=False, num_devices=1)
    arrays, args = {}, []
    for name in _INS:
        a = _np.ascontiguousarray(inputs[name])
        arrays[f"in_{name}_dram"] = a
        args.append(nc.dram_tensor(f"in_{name}_dram", a.shape, _mybir.dt.from_np(a.dtype), kind="ExternalInput").ap())
    for i, (shape, dtype) in enumerate(_OUTS):
        dt = _mybir.dt.from_np(_np.dtype(dtype))
        args.append(nc.dram_tensor(f"out_{i}_dram", shape, dt, kind="ExternalOutput").ap())
    build(nc, *args)
    r = _run(nc, [arrays], core_ids=[0])
    got = tuple(r.results[0][f"out_{i}_dram"] for i in range(len(_OUTS)))
    return got[0]
```
